# Optimizing a Trainium2 kernel written in Bass

```python
import numpy as np
import jax
import jax.numpy as jnp

def _softmax(x, axis=-1):
    return jax.nn.softmax(x, axis=axis)

def _gelu(x):
    return jax.nn.gelu(x, approximate=True)

def _silu(x):
    return jax.nn.silu(x)

def _sigmoid(x):
    return jax.nn.sigmoid(x)

def _layernorm(x, axis=-1, eps=1e-05):
    m = jnp.mean(x, axis=axis, keepdims=True)
    v = jnp.var(x, axis=axis, keepdims=True)
    return (x - m) / jnp.sqrt(v + eps)

def _scatter_add(tgt, idx, src, axis=0):
    return tgt.at[idx].add(src)

def _segment_sum(src, seg, n):
    return jax.ops.segment_sum(src, seg, n)
kernel_name = 'mk_perceiver_d1_seqx_r4_b5b664'

def setup_inputs(seed: int=0):
    np.random.seed(seed)
    _w = jnp.asarray

    def _rec_inputs():
        import jax
        import jax.numpy as jnp
        _rk = jax.random.key(seed)
        x = 7.22e-05 + 1 * jax.random.normal(jax.random.fold_in(_rk, 1), (64, 64, 256), jnp.float32)
        _lenS = 64 - jax.random.randint(jax.random.fold_in(_rk, 7), (64,), 0, max(1, 64 // 4) + 1, jnp.int32)
        _lenS2 = 256 - jax.random.randint(jax.random.fold_in(_rk, 8), (64,), 0, max(1, 256 // 4) + 1, jnp.int32)
        _ctx_768P = jax.random.normal(jax.random.fold_in(_rk, 11), (64, 16, 192), jnp.float32)
        _ctx_768c = jax.random.dirichlet(jax.random.fold_in(_rk, 511), 0.3 * jnp.ones((16,), jnp.float32), (64, 256))
        _ctx_768t = jnp.einsum('bsk,bkd->bsd', _ctx_768c, _ctx_768P)
        _ctx_768t = _ctx_768t * jax.lax.rsqrt(jnp.mean(jnp.square(_ctx_768t)) + 1e-12) * 0.953939
        ctx_768 = -0.000191848 + 0.999787 * (_ctx_768t + 0.3 * jax.random.normal(jax.random.fold_in(_rk, 611), (64, 256, 192), jnp.float32))
        return (x, ctx_768)
    x, ctx_768 = _rec_inputs()

    def _L0_xattn_setup():
        import jax, jax.numpy as jnp
        import numpy as np
        HEADS = 8
        DIM_HEAD = 64
        SCALE = DIM_HEAD ** (-0.5)
        key = jax.random.key(seed)
        ks = jax.random.split(key, 7)
        B, Nq, Nc = (4, 512, 512)
        Dq, Dc = (256, 192)
        inner = HEADS * DIM_HEAD
        x = jax.random.normal(ks[0], (B, Nq, Dq), dtype=jnp.float32)
        context = jax.random.normal(ks[1], (B, Nc, Dc), dtype=jnp.float32)
        Wq = jax.random.normal(ks[2], (Dq, inner), dtype=jnp.float32) * Dq ** (-0.5)
        Wk = jax.random.normal(ks[3], (Dc, inner), dtype=jnp.float32) * Dc ** (-0.5)
        Wv = jax.random.normal(ks[4], (Dc, inner), dtype=jnp.float32) * Dc ** (-0.5)
        Wo = jax.random.normal(ks[5], (inner, Dq), dtype=jnp.float32) * inner ** (-0.5)
        bo = jax.random.normal(ks[6], (Dq,), dtype=jnp.float32) * 0.01
        return {'x': x, 'context': context, 'Wq': Wq, 'Wk': Wk, 'Wv': Wv, 'Wo': Wo, 'bo': bo}
    _L0_xattn_all = _L0_xattn_setup()
    _L0_xattn_in = {k: v for k, v in _L0_xattn_all.items() if k in ('Wq', 'Wk', 'Wv', 'Wo', 'bo')}
    del _L0_xattn_all

    def _L0_attn_setup():
        import jax, jax.numpy as jnp
        import numpy as np
        B, S, D, H, F = (4, 2048, 256, 16, 64)
        DK = D // H
        EPS = 1e-06

        def _heads(x, W, b):
            y = jnp.einsum('bsd,de->bse', x, W) + b
            return y.reshape(x.shape[0], x.shape[1], H, DK).transpose(0, 2, 1, 3)
        key = jax.random.key(seed)
        ks = jax.random.split(key, 6)
        scale = 1.0 / np.sqrt(D)
        x = jax.random.normal(ks[0], (B, S, D), dtype=jnp.float32)
        Wq = jax.random.normal(ks[1], (D, D), dtype=jnp.float32) * scale
        Wk = jax.random.normal(ks[2], (D, D), dtype=jnp.float32) * scale
        Wv = jax.random.normal(ks[3], (D, D), dtype=jnp.float32) * scale
        Wo = jax.random.normal(ks[4], (D, D), dtype=jnp.float32) * scale
        rw = jax.random.normal(ks[5], (H, DK, F), dtype=jnp.float32) / np.sqrt(DK)
        zb = jnp.zeros((D,), dtype=jnp.float32)
        return {'x': x, 'Wq': Wq, 'bq': zb, 'Wk': Wk, 'bk': zb, 'Wv': Wv, 'bv': zb, 'Wo': Wo, 'bo': zb, 'rw': rw}
    _L0_attn_all = _L0_attn_setup()
    _L0_attn_in = {k: v for k, v in _L0_attn_all.items() if k in ('Wq', 'bq', 'Wk', 'bk', 'Wv', 'bv', 'Wo', 'bo', 'rw')}
    del _L0_attn_all

    def _L0_ffn_setup():
        import jax, jax.numpy as jnp
        import numpy as np
        D, H, E, K = (256, 256, 8, 2)

        def _moe(x, router_w, w_in, b_in, w_out, b_out):
            B, S, Dm = x.shape
            T = B * S
            x2 = x.reshape(T, Dm)
            logits = x2 @ router_w
            probs = jax.nn.softmax(logits, axis=-1)
            top_p, top_e = jax.lax.top_k(probs, K)
            flat_e = top_e.reshape(-1)
            flat_p = top_p.reshape(-1)
            tok = jnp.repeat(jnp.arange(T), K)
            order = jnp.argsort(flat_e)
            se, sp, st = (flat_e[order], flat_p[order], tok[order])
            xd = x2[st]
            N = xd.shape[0]
            h = jnp.zeros((N, H), x.dtype)
            for e in range(E):
                m = (se == e)[:, None]
                h = h + jnp.where(m, jax.nn.gelu(xd @ w_in[e] + b_in[e]), 0.0)
            y = jnp.zeros((N, Dm), x.dtype)
            for e in range(E):
                m = (se == e)[:, None]
                y = y + jnp.where(m, h @ w_out[e] + b_out[e], 0.0)
            y = y * sp[:, None]
            out = jnp.zeros((T, Dm), x.dtype).at[st].add(y)
            return out.reshape(B, S, Dm)
        key = jax.random.key(seed)
        ks = jax.random.split(key, 5)
        s = lambda k, shape, scale: jax.random.normal(k, shape, dtype=jnp.float32) * scale
        return {'input_batch': s(ks[0], (2, 128, D), 1.0), 'router_w': s(ks[1], (D, E), D ** (-0.5)), 'w_in': s(ks[2], (E, D, H), D ** (-0.5)), 'b_in': jnp.zeros((E, H), jnp.float32), 'w_out': s(ks[3], (E, H, D), H ** (-0.5)), 'b_out': jnp.zeros((E, D), jnp.float32)}
    _L0_ffn_all = _L0_ffn_setup()
    _L0_ffn_in = {k: v for k, v in _L0_ffn_all.items() if k in ('router_w', 'w_in', 'b_in', 'w_out', 'b_out')}
    del _L0_ffn_all
    return {'x': x, 'ctx_768': ctx_768, 'L0_xattn_Wq': _L0_xattn_in['Wq'], 'L0_xattn_Wk': _L0_xattn_in['Wk'], 'L0_xattn_Wv': _L0_xattn_in['Wv'], 'L0_xattn_Wo': _L0_xattn_in['Wo'], 'L0_xattn_bo': _L0_xattn_in['bo'], 'L0_attn_Wq': _L0_attn_in['Wq'], 'L0_attn_bq': _L0_attn_in['bq'], 'L0_attn_Wk': _L0_attn_in['Wk'], 'L0_attn_bk': _L0_attn_in['bk'], 'L0_attn_Wv': _L0_attn_in['Wv'], 'L0_attn_bv': _L0_attn_in['bv'], 'L0_attn_Wo': _L0_attn_in['Wo'], 'L0_attn_bo': _L0_attn_in['bo'], 'L0_attn_rw': _L0_attn_in['rw'], 'L0_ffn_router_w': _L0_ffn_in['router_w'], 'L0_ffn_w_in': _L0_ffn_in['w_in'], 'L0_ffn_b_in': _L0_ffn_in['b_in'], 'L0_ffn_w_out': _L0_ffn_in['w_out'], 'L0_ffn_b_out': _L0_ffn_in['b_out']}

def reference(x, ctx_768, L0_xattn_Wq, L0_xattn_Wk, L0_xattn_Wv, L0_xattn_Wo, L0_xattn_bo, L0_attn_Wq, L0_attn_bq, L0_attn_Wk, L0_attn_bk, L0_attn_Wv, L0_attn_bv, L0_attn_Wo, L0_attn_bo, L0_attn_rw, L0_ffn_router_w, L0_ffn_w_in, L0_ffn_b_in, L0_ffn_w_out, L0_ffn_b_out):
    import jax
    import jax.numpy as jnp

    def _L0_xattn_ref(x, context, Wq, Wk, Wv, Wo, bo):
        import jax, jax.numpy as jnp
        import numpy as np
        HEADS = 8
        DIM_HEAD = 64
        SCALE = DIM_HEAD ** (-0.5)
        B, Nq, _ = x.shape
        q = (x @ Wq).reshape(B, Nq, HEADS, DIM_HEAD)
        k = (context @ Wk).reshape(B, context.shape[1], HEADS, DIM_HEAD)
        v = (context @ Wv).reshape(B, context.shape[1], HEADS, DIM_HEAD)
        sim = jnp.einsum('bihd,bjhd->bhij', q, k) * SCALE
        attn = jax.nn.softmax(sim, axis=-1)
        out = jnp.einsum('bhij,bjhd->bihd', attn, v)
        out = out.reshape(B, Nq, HEADS * DIM_HEAD)
        return out @ Wo + bo

    def _L0_attn_ref(x, Wq, bq, Wk, bk, Wv, bv, Wo, bo, rw):
        import jax, jax.numpy as jnp
        import numpy as np
        B, S, D, H, F = (4, 2048, 256, 16, 64)
        DK = D // H
        EPS = 1e-06

        def _heads(x, W, b):
            y = jnp.einsum('bsd,de->bse', x, W) + b
            return y.reshape(x.shape[0], x.shape[1], H, DK).transpose(0, 2, 1, 3)
        q = _heads(x, Wq, bq)
        k = _heads(x, Wk, bk)
        v = _heads(x, Wv, bv)
        qp = jax.nn.relu(jnp.einsum('bhsd,hdf->bhsf', q, rw)) + EPS
        kp = jax.nn.relu(jnp.einsum('bhsd,hdf->bhsf', k, rw)) + EPS
        kv = jnp.einsum('bhsf,bhsd->bhfd', kp, v)
        qkv = jnp.einsum('bhsf,bhfd->bhsd', qp, kv)
        norm = jnp.einsum('bhsf,bhf->bhs', qp, kp.sum(axis=2))
        out = qkv / (norm[..., None] + EPS)
        out = out.transpose(0, 2, 1, 3).reshape(x.shape[0], x.shape[1], D)
        return jnp.einsum('bsd,de->bse', out, Wo) + bo

    def _L0_ffn_ref(input_batch, router_w, w_in, b_in, w_out, b_out):
        import jax, jax.numpy as jnp
        import numpy as np
        D, H, E, K = (256, 256, 8, 2)

        def _moe(x, router_w, w_in, b_in, w_out, b_out):
            B, S, Dm = x.shape
            T = B * S
            x2 = x.reshape(T, Dm)
            logits = x2 @ router_w
            probs = jax.nn.softmax(logits, axis=-1)
            top_p, top_e = jax.lax.top_k(probs, K)
            flat_e = top_e.reshape(-1)
            flat_p = top_p.reshape(-1)
            tok = jnp.repeat(jnp.arange(T), K)
            order = jnp.argsort(flat_e)
            se, sp, st = (flat_e[order], flat_p[order], tok[order])
            xd = x2[st]
            N = xd.shape[0]
            h = jnp.zeros((N, H), x.dtype)
            for e in range(E):
                m = (se == e)[:, None]
                h = h + jnp.where(m, jax.nn.gelu(xd @ w_in[e] + b_in[e]), 0.0)
            y = jnp.zeros((N, Dm), x.dtype)
            for e in range(E):
                m = (se == e)[:, None]
                y = y + jnp.where(m, h @ w_out[e] + b_out[e], 0.0)
            y = y * sp[:, None]
            out = jnp.zeros((T, Dm), x.dtype).at[st].add(y)
            return out.reshape(B, S, Dm)
        return _moe(input_batch, router_w, w_in, b_in, w_out, b_out)
    x = x + _L0_xattn_ref(_layernorm(x, axis=-1), ctx_768, L0_xattn_Wq, L0_xattn_Wk, L0_xattn_Wv, L0_xattn_Wo, L0_xattn_bo)
    x = x + _L0_attn_ref(_layernorm(x, axis=-1), L0_attn_Wq, L0_attn_bq, L0_attn_Wk, L0_attn_bk, L0_attn_Wv, L0_attn_bv, L0_attn_Wo, L0_attn_bo, L0_attn_rw)
    x = x + _L0_ffn_ref(_layernorm(x, axis=-1), L0_ffn_router_w, L0_ffn_w_in, L0_ffn_b_in, L0_ffn_w_out, L0_ffn_b_out)
    return x

_drawn_inputs = setup_inputs


def setup_inputs(seed=0):
    import zlib

    import numpy as np

    out = dict(_drawn_inputs(seed))
    spreads = {'L0_attn_bq': (0.0, 0.8),
     'L0_attn_bk': (0.0, 0.8),
     'L0_attn_bv': (0.0, 0.1),
     'L0_attn_bo': (0.0, 0.1),
     'L0_ffn_b_in': (0.0, 0.334),
     'L0_ffn_b_out': (0.0, 0.1)}
    factors = {'L0_xattn_bo': 3.6}
    for name, (base, spread) in spreads.items():
        noise = np.random.default_rng([zlib.crc32(name.encode()), seed]).standard_normal(out[name].shape)
        drawn = base * np.exp(spread * noise) if base else spread * noise
        out[name] = jnp.asarray(drawn.astype(out[name].dtype))
    for name, factor in factors.items():
        out[name] = (out[name] * factor).astype(out[name].dtype)
    return out
```

```python
from contextlib import ExitStack

import concourse.bass as bass
from concourse import mybir

F32 = mybir.dt.float32
F32R = mybir.dt.float32r
U32 = mybir.dt.uint32
ALU = mybir.AluOpType
ACT = mybir.ActivationFunctionType
AX = mybir.AxisListType

P = 128
BANK = 512
LN_EPS = 1e-5
PHI_EPS = 1e-6


def after(engine, semaphore, value):
    if isinstance(value, int) and value <= 0:
        return
    engine.wait_ge(semaphore, value)


def settle(nc, semaphore, value, scratch):
    nc.vector.wait_ge(semaphore, value)
    nc.vector.memset(scratch, 0.0)


def slot(tiles, t):
    return tiles[:, bass.ds(t, 1), :]


def cross_attention(nc, x, ctx_in, Wq, Wk, Wv, Wo, bo, xres, ident):
    NB, NQ, D = x.shape
    _, NC, DC = ctx_in.shape
    INNER = Wq.shape[1]
    DH = 64
    SCALE = DH ** -0.5
    TB = P // NQ
    NT = NB // TB
    UT = 2
    NU = NT // UT
    UTOK = UT * P
    CB = TB * NC // P
    JT = NC // P
    HP = INNER // P
    KD = D // P
    DR = DC - P
    assert NQ == DH == DR == 64 and HP * P == BANK and CB * P == BANK

    x_tiles = x.rearrange("(t b) q d -> (b q) t d", b=TB)
    ctx_tiles = ctx_in.rearrange("(t b) (j p) d -> t p (b j) d", b=TB, p=P)

    with ExitStack() as stack:
        def sb(name, shape, dt=F32):
            return stack.enter_context(nc.sbuf_tensor(name, shape, dt))

        def sem(name):
            return stack.enter_context(nc.semaphore(name))

        raw = sb("xa_raw", [P, 8, BANK])
        wq_hi = sb("wq_hi", [P, KD, INNER], F32R)
        wq_lo = sb("wq_lo", [P, KD, INNER], F32R)
        wk_hi = sb("wk_hi", [P, 2, INNER], F32R)
        wk_lo = sb("wk_lo", [P, 2, INNER], F32R)
        wv_hi = sb("wv_hi", [P, 2, INNER], F32R)
        wv_lo = sb("wv_lo", [P, 2, INNER], F32R)
        wo_hi = sb("wo_hi", [P, HP, D], F32R)
        wo_lo = sb("wo_lo", [P, HP, D], F32R)
        bo_raw = sb("bo_raw", [P, D])
        bo_rows = sb("bo_rows", [P, D], F32R)
        ones_rows = sb("ones_rows", [P, P], F32R)

        ctx_nat = [sb(f"ctx_nat{i}", [P, CB, 2 * P]) for i in range(2)]
        ctxT_hi = sb("ctxT_hi", [P, BANK], F32R)
        ctxT_lo = sb("ctxT_lo", [P, BANK], F32R)
        ctxT_rest = sb("ctxT_rest", [P, BANK], F32R)
        kT_hi = sb("kT_hi", [P, HP, BANK], F32R)
        kT_lo = sb("kT_lo", [P, HP, BANK], F32R)
        v_nat = [sb(f"v_nat{i}", [P, CB, INNER]) for i in range(2)]
        scratch = sb("xa_scratch", [P, 1])
        stats = sb("xa_stats", [P, UT, 6])
        moments = sb("xa_moments", [P, UT, 2])
        var_eps = sb("xa_var_eps", [P, UT, 1])
        rstd = sb("xa_rstd", [P, UT, 1])
        minus_half = sb("xa_minus_half", [P, UT, 1])
        xn = sb("xa_xn", [P, UT, D])
        xnT_hi = sb("xa_xnT_hi", [P, KD, UTOK], F32R)
        xnT_lo = sb("xa_xnT_lo", [P, KD, UTOK], F32R)
        q_hi = sb("q_hi", [P, HP, UT * TB, P], F32R)
        q_lo = sb("q_lo", [P, HP, UT * TB, P], F32R)
        neg_max = sb("neg_max", [P, TB, HP])
        row_sum = sb("row_sum", [P, TB, HP])
        inv_sum = sb("inv_sum", [P, TB, HP])
        probs = sb("probs", [P, TB, HP, NC])
        probsT = sb("probsT", [P, TB * 2, BANK])
        oT_hi = sb("oT_hi", [P, HP, P], F32R)
        oT_lo = sb("oT_lo", [P, HP, P], F32R)

        score_ps = stack.enter_context(nc.psum_tensor("score_ps", [P, 4, BANK], F32))
        proj_ps = stack.enter_context(nc.psum_tensor("proj_ps", [P, 3, BANK], F32))
        turn_ps = stack.enter_context(nc.psum_tensor("turn_ps", [P, BANK], F32))

        x_here = sem("x_here")
        w_in = sem("w_in")
        ctx_here = [sem("ctx_here0"), sem("ctx_here1")]
        w_hi_done = sem("w_hi_done")
        w_lo_done = sem("w_lo_done")
        consts_done = sem("xa_consts_done")
        ident_zeroed = sem("ident_zeroed")
        ident_done = sem("ident_done")
        rows_zeroed = sem("xa_rows_zeroed")
        ctx_turned = sem("ctx_turned")
        ctxT_hi_done = sem("ctxT_hi_done")
        ctxT_done = sem("ctxT_done")
        k_full = sem("k_full")
        kT_hi_done = sem("kT_hi_done")
        kT_done = sem("kT_done")
        v_full = sem("v_full")
        v_even_done = sem("v_even_done")
        v_odd_done = sem("v_odd_done")
        stats_done = sem("xa_stats_done")
        moments_done = sem("xa_moments_done")
        var_done = sem("xa_var_done")
        rstd_done = sem("xa_rstd_done")
        xn_done = sem("xa_xn_done")
        xn_turned = sem("xa_xn_turned")
        xnT_hi_done = sem("xa_xnT_hi_done")
        xnT_done = sem("xa_xnT_done")
        q_full = sem("q_full")
        q_hi_done = sem("q_hi_done")
        q_done = sem("q_done")
        score_full = sem("score_full")
        max_done = sem("max_done")
        exp_done = sem("exp_done")
        inv_done = sem("inv_done")
        probs_done = sem("probs_done")
        pt_full = sem("pt_full")
        pt_even_done = sem("pt_even_done")
        pt_odd_done = sem("pt_odd_done")
        o_full = sem("o_full")
        oT_hi_done = sem("oT_hi_done")
        oT_done = sem("oT_done")
        out_full = sem("xa_out_full")
        x_done = sem("xa_x_done")

        CONSTS = 5
        CTX_BANK = [2, 0]
        KEY_BANK = [1, 2, 0, 1]
        VALUE_BANK = [2, 0, 1, 2]
        WEIGHTS = 6

        block = stack.enter_context(nc.Block())

        @block.sync
        def _(sp):
            def load_ctx(t, buf):
                src = ctx_tiles[bass.ds(t, 1), :, :, :].rearrange("a p m d -> p (a m) d")
                sp.dma_start(ctx_nat[buf][:, :, 0:DC], src).then_inc(ctx_here[buf], 16)
                sp.dma_start(ctx_nat[buf][:, :, DC:2 * P], src[:, :, P:DC]).then_inc(ctx_here[buf], 16)

            def load_x(u):
                sp.dma_start(xres[:, bass.ds(UT * u, UT), :], x_tiles[:, bass.ds(UT * u, UT), :]).then_inc(x_here, 16)

            load_x(0)
            load_ctx(0, 0)
            sp.dma_start(raw[:, 0:2, :], Wq.rearrange("(k p) n -> p k n", p=P)).then_inc(w_in, 16)
            for r, w in ((2, Wk), (4, Wv)):
                sp.dma_start(raw[:, r, :], w[0:P, :]).then_inc(w_in, 16)
                for half in range(2):
                    sp.dma_start(raw[half * DR:(half + 1) * DR, r + 1, :], w[P:DC, :]).then_inc(w_in, 16)
            sp.dma_start(raw[:, 6:8, :].rearrange("p a (b n) -> p (a b) n", b=2),
                         Wo.rearrange("(k p) n -> p k n", p=P)).then_inc(w_in, 16)
            for row in (0, 32):
                sp.dma_start(bo_raw[row:row + 1, :], bo.rearrange("(a n) -> a n", a=1)).then_inc(w_in, 16)
            load_ctx(1, 1)
            sp.wait_ge(x_here, 16)
            load_x(1)
            def loads(u):
                for a in range(2):
                    sp.wait_ge(ctxT_done, 4 * u + 2 * a - 2)
                    load_ctx(UT * u + a, a)

            with sp.Fori(1, NU - 1) as u:
                loads(u)
                sp.wait_ge(x_here, 16 * u + 16)
                load_x(u + 1)
            loads(NU - 1)

        @block.gpsimd
        def _(pool):
            nc.gpsimd.memset(ident[:, :], 0.0).then_inc(ident_zeroed, 1)
            pool.wait_ge(ident_zeroed, 1)
            nc.gpsimd.affine_select(out=ident[:, :], in_=ident[:, :], compare_op=ALU.not_equal, fill=1.0,
                                    base=0, pattern=[[-1, P]], channel_multiplier=1).then_inc(ident_done, 1)
            pool.wait_ge(ident_done, 1)

            def rstd_of(u):
                pool.wait_ge(var_done, u + 1)
                nc.gpsimd.tensor_tensor(rstd[:, :, :], var_eps[:, :, :], minus_half[:, :, :], ALU.pow
                                        ).then_inc(rstd_done, 1)

            def normalise(t):
                for b in range(TB):
                    pool.wait_ge(inv_done, TB * t + b + 1)
                    nc.gpsimd.tensor_tensor(probs[:, b, :, :], probs[:, b, :, :],
                                            inv_sum[:, b, :].unsqueeze(2).to_broadcast([P, HP, NC]), ALU.mult
                                            ).then_inc(probs_done, 1)

            pool.wait_ge(consts_done, CONSTS)
            rstd_of(0)
            with pool.Fori(0, NU - 1) as u:
                normalise(UT * u)
                rstd_of(u + 1)
                normalise(UT * u + 1)
            for a in range(UT):
                normalise(UT * (NU - 1) + a)

        W_IN = 16 * 10
        weights = [(wq_hi, wq_lo, 0), (wk_hi, wk_lo, 2), (wv_hi, wv_lo, 4)]

        def weight_views():
            for hi, lo, r in weights:
                yield hi[:, :, :], lo[:, :, :], raw[:, r:r + 2, :]
            yield wo_hi[:, :, :], wo_lo[:, :, :], raw[:, 6:8, :].rearrange("p a (b n) -> p (a b) n", b=2)

        @block.scalar
        def _(act):
            def ctxT_of(t):
                act.wait_ge(ctx_turned, 2 * t + 1)
                nc.scalar.activation(ctxT_hi[:, :], proj_ps[:, CTX_BANK[0], :], ACT.Copy).then_inc(ctxT_hi_done, 1)
                act.wait_ge(ctx_turned, 2 * t + 2)
                nc.scalar.activation(ctxT_rest[:, :], proj_ps[:, CTX_BANK[1], :], ACT.Copy).then_inc(ctxT_hi_done, 1)

            def kT_of(t, hp):
                act.wait_ge(k_full, HP * t + hp + 1)
                nc.scalar.activation(kT_hi[:, hp, :], proj_ps[:, KEY_BANK[hp], :], ACT.Copy).then_inc(kT_hi_done, 1)

            def v_of(t, buf, m):
                act.wait_ge(v_full, CB * t + m + 1)
                nc.scalar.activation(v_nat[buf][:, m, :], proj_ps[:, VALUE_BANK[m], :], ACT.Copy).then_inc(v_even_done, 1)

            def xnT_of(u):
                act.wait_ge(xn_turned, u + 1)
                nc.scalar.activation(xnT_hi[:, :, :].rearrange("p k n -> p (k n)"), turn_ps[:, :], ACT.Copy
                                     ).then_inc(xnT_hi_done, 1)

            def q_of(u, g):
                act.wait_ge(q_full, 2 * u + g + 1)
                src = turn_ps[:, :].rearrange("p (c i) -> p c i", i=NQ)
                for h in range(2):
                    rows = slice(h * DH, (h + 1) * DH)
                    dst = q_hi[rows, 2 * g:2 * g + 2, :, h * NQ:(h + 1) * NQ].rearrange("p a c i -> p (a c) i")
                    nc.scalar.activation(dst, src[rows], ACT.Copy, scale=SCALE).then_inc(q_hi_done, 1)

            def exp_of(t, b, hp):
                act.wait_ge(max_done, 4 * t + 2 * b + hp // 2 + 1)
                nc.scalar.activation(probs[:, b, hp, :], score_ps[:, 2 * b + hp // 2, (hp % 2) * NC:(hp % 2 + 1) * NC],
                                     ACT.Exp, bias=neg_max[:, b, hp:hp + 1], accum_out=row_sum[:, b, hp:hp + 1]
                                     ).then_inc(exp_done, 1)

            def probsT_of(t, g):
                act.wait_ge(pt_full, 4 * t + g + 1)
                nc.scalar.activation(probsT[:, g, :], turn_ps[:, :], ACT.Copy).then_inc(pt_even_done, 1)

            def oT_of(t):
                for b in range(TB):
                    act.wait_ge(o_full, TB * t + b + 1)
                    for h in range(2):
                        rows = slice(h * DH, (h + 1) * DH)
                        src = score_ps[rows, b, :].rearrange("p (a n) -> p a n", n=P)[:, :, h * NQ:(h + 1) * NQ]
                        nc.scalar.activation(oT_hi[rows, :, b * NQ:(b + 1) * NQ], src, ACT.Copy).then_inc(oT_hi_done, 1)

            act.wait_ge(w_in, W_IN)
            for hi, lo, src in weight_views():
                nc.scalar.activation(hi, src, ACT.Copy).then_inc(w_hi_done, 1)
            act.wait_ge(consts_done, CONSTS)
            act.wait_ge(rows_zeroed, 2)
            for row in (0, 32):
                nc.scalar.activation(bo_rows[row:row + 1, :], bo_raw[row:row + 1, :], ACT.Copy).then_inc(w_hi_done, 1)

            ctxT_of(0)
            xnT_of(0)
            kT_of(0, 0)
            kT_of(0, 1)
            q_of(0, 0)
            kT_of(0, 2)
            kT_of(0, 3)
            q_of(0, 1)
            v_of(0, 0, 0)
            v_of(0, 0, 2)

            def tile(u, a, last):
                t = UT * u + a
                nxt = (a + 1) % 2
                more = not (last and a == 1)
                if more:
                    ctxT_of(t + 1)
                for hp in range(HP):
                    exp_of(t, 0, hp)
                if not last and a == 1:
                    xnT_of(u + 1)
                if more:
                    kT_of(t + 1, 0)
                exp_of(t, 1, 0)
                if more:
                    kT_of(t + 1, 1)
                if not last and a == 1:
                    q_of(u + 1, 0)
                exp_of(t, 1, 1)
                if more:
                    kT_of(t + 1, 2)
                exp_of(t, 1, 2)
                exp_of(t, 1, 3)
                if more:
                    kT_of(t + 1, 3)
                if not last and a == 1:
                    q_of(u + 1, 1)
                if more:
                    v_of(t + 1, nxt, 0)
                probsT_of(t, 0)
                if more:
                    v_of(t + 1, nxt, 2)
                probsT_of(t, 2)
                oT_of(t)

            with act.Fori(0, NU - 1) as u:
                tile(u, 0, False)
                tile(u, 1, False)
            tile(NU - 1, 0, True)
            tile(NU - 1, 1, True)

        @block.vector
        def _(dve):
            def moments_of(u):
                for a in range(UT):
                    dve.wait_ge(x_here, 16 * u + 16)
                    nc.vector.bn_stats(stats[:, a, :], slot(xres, UT * u + a)).then_inc(stats_done, 1)
                settle(nc, stats_done, UT * u + UT, scratch[:, :])
                for a in range(UT):
                    nc.vector.bn_aggr(moments[:, a, :], stats[:, a, :]).then_inc(moments_done, 1)
                dve.wait_ge(moments_done, UT * u + UT)
                nc.vector.tensor_scalar(var_eps[:, :, :], moments[:, :, 1:2], LN_EPS, None, ALU.add).then_inc(var_done, 1)

            def xn_of(u):
                dve.wait_ge(rstd_done, u + 1)
                for a in range(UT):
                    nc.vector.tensor_scalar(xn[:, a:a + 1, :], slot(xres, UT * u + a), moments[:, a, 0:1], rstd[:, a, :],
                                            ALU.subtract, ALU.mult).then_inc(xn_done, 1)

            def ctxT_of(t):
                dve.wait_ge(ctxT_hi_done, 2 * t + 1)
                nc.vector.tensor_tensor(ctxT_lo[:, :], proj_ps[:, CTX_BANK[0], :], ctxT_hi[:, :].bitcast(F32), ALU.subtract
                                        ).then_inc(ctxT_done, 1)
                dve.wait_ge(ctxT_hi_done, 2 * t + 2)
                nc.vector.tensor_tensor(ctxT_rest[DR:P, :], proj_ps[DR:P, CTX_BANK[1], :], ctxT_rest[DR:P, :].bitcast(F32),
                                        ALU.subtract).then_inc(ctxT_done, 1)

            def kT_of(t, hp):
                dve.wait_ge(kT_hi_done, HP * t + hp + 1)
                nc.vector.tensor_tensor(kT_lo[:, hp, :], proj_ps[:, KEY_BANK[hp], :], kT_hi[:, hp, :].bitcast(F32),
                                        ALU.subtract).then_inc(kT_done, 1)

            def v_of(t, buf, m):
                dve.wait_ge(v_full, CB * t + m + 1)
                nc.vector.tensor_copy(v_nat[buf][:, m, :], proj_ps[:, VALUE_BANK[m], :]).then_inc(v_odd_done, 1)

            def xnT_of(u):
                dve.wait_ge(xnT_hi_done, u + 1)
                nc.vector.tensor_tensor(xnT_lo[:, :, :].rearrange("p k n -> p (k n)"), turn_ps[:, :],
                                        xnT_hi[:, :, :].rearrange("p k n -> p (k n)").bitcast(F32), ALU.subtract
                                        ).then_inc(xnT_done, 1)

            def q_of(u, g):
                src = turn_ps[:, :].rearrange("p (c i) -> p c i", i=NQ)
                for h in range(2):
                    rows = slice(h * DH, (h + 1) * DH)
                    part = [q[rows, 2 * g:2 * g + 2, :, h * NQ:(h + 1) * NQ].rearrange("p a c i -> p (a c) i")
                            for q in (q_hi, q_lo)]
                    dve.wait_ge(q_hi_done, 4 * u + 2 * g + h + 1)
                    nc.vector.scalar_tensor_tensor(out=part[1], in0=src[rows], scalar=SCALE, in1=part[0].bitcast(F32),
                                                   op0=ALU.mult, op1=ALU.subtract).then_inc(q_done, 1)

            def max_of(t, n):
                dve.wait_ge(score_full, 4 * t + n + 1)
                nc.vector.tensor_reduce(neg_max[:, n // 2, 2 * (n % 2):2 * (n % 2) + 2],
                                        score_ps[:, n, :].rearrange("p (h j) -> p h j", j=NC), AX.X, ALU.max,
                                        negate=True).then_inc(max_done, 1)

            def inverse_of(t, b):
                dve.wait_ge(exp_done, TB * HP * t + HP * (b + 1))
                nc.vector.reciprocal(inv_sum[:, b, :], row_sum[:, b, :]).then_inc(inv_done, 1)

            def probsT_of(t, g):
                dve.wait_ge(pt_full, 4 * t + g + 1)
                nc.vector.tensor_copy(probsT[:, g, :], turn_ps[:, :]).then_inc(pt_odd_done, 1)

            def oT_of(t):
                for b in range(TB):
                    for h in range(2):
                        rows = slice(h * DH, (h + 1) * DH)
                        cols = slice(b * NQ, (b + 1) * NQ)
                        src = score_ps[rows, b, :].rearrange("p (a n) -> p a n", n=P)[:, :, h * NQ:(h + 1) * NQ]
                        dve.wait_ge(oT_hi_done, 2 * TB * t + 2 * b + h + 1)
                        nc.vector.tensor_tensor(oT_lo[rows, :, cols], src, oT_hi[rows, :, cols].bitcast(F32),
                                                ALU.subtract).then_inc(oT_done, 1)

            def x_of(t):
                dve.wait_ge(out_full, t + 1)
                dst = slot(xres, t)
                nc.vector.tensor_tensor(dst, turn_ps[:, 0:D].unsqueeze(1), dst, ALU.add).then_inc(x_done, 1)

            nc.vector.memset(minus_half[:, :, :], -0.5).then_inc(consts_done, 1)
            for rows in (ones_rows, bo_rows):
                nc.vector.memset(rows[:, :].bitcast(F32), 0.0).then_inc(rows_zeroed, 1)
            for q in (q_hi, q_lo):
                nc.vector.memset(q[:, :, :, :].bitcast(F32), 0.0).then_inc(consts_done, 1)
            dve.wait_ge(rows_zeroed, 2)
            for row in (0, 32):
                nc.vector.memset(ones_rows[row:row + 1, :].bitcast(F32), 1.0).then_inc(consts_done, 1)
            moments_of(0)
            xn_of(0)
            dve.wait_ge(w_in, W_IN)
            for n, (hi, lo, src) in enumerate(weight_views()):
                dve.wait_ge(w_hi_done, n + 1)
                nc.vector.tensor_tensor(lo, src, hi.bitcast(F32), ALU.subtract).then_inc(w_lo_done, 1)
            dve.wait_ge(w_hi_done, WEIGHTS)
            nc.vector.tensor_tensor(bo_rows[32:33, :], bo_raw[32:33, :], bo_rows[32:33, :].bitcast(F32), ALU.subtract
                                    ).then_inc(w_lo_done, 1)
            ctxT_of(0)
            xnT_of(0)
            kT_of(0, 0)
            kT_of(0, 1)
            q_of(0, 0)
            kT_of(0, 2)
            kT_of(0, 3)
            q_of(0, 1)
            v_of(0, 0, 1)
            v_of(0, 0, 3)

            def tile(u, a, last):
                t = UT * u + a
                nxt = (a + 1) % 2
                more = not (last and a == 1)
                if more:
                    ctxT_of(t + 1)
                max_of(t, 0)
                if not (isinstance(t, int) and t == 0):
                    x_of(t - 1)
                for n in range(1, 4):
                    max_of(t, n)
                if not last and a == 1:
                    xnT_of(u + 1)
                if more:
                    kT_of(t + 1, 0)
                inverse_of(t, 0)
                if more:
                    kT_of(t + 1, 1)
                if not last and a == 1:
                    q_of(u + 1, 0)
                if more:
                    kT_of(t + 1, 2)
                inverse_of(t, 1)
                if more:
                    kT_of(t + 1, 3)
                if not last and a == 1:
                    q_of(u + 1, 1)
                if more:
                    v_of(t + 1, nxt, 1)
                probsT_of(t, 1)
                if not last and a == 0:
                    moments_of(u + 1)
                if more:
                    v_of(t + 1, nxt, 3)
                probsT_of(t, 3)
                if not last and a == 0:
                    xn_of(u + 1)
                oT_of(t)

            tile(0, 0, False)
            tile(0, 1, False)
            with dve.Fori(1, NU - 1) as u:
                tile(u, 0, False)
                tile(u, 1, False)
            tile(NU - 1, 0, True)
            tile(NU - 1, 1, True)
            x_of(NT - 1)

        @block.tensor
        def _(pe):
            def products(out, pairs):
                for n, (w, m) in enumerate(pairs):
                    ins = nc.tensor.matmul(out, w, m, start=n == 0, stop=n == len(pairs) - 1)
                return ins

            def turn_ctx(u, buf):
                t = UT * u + buf
                pe.wait_ge(ctx_here[buf], 32 * u + 32)
                after(pe, v_odd_done, 2 * t)
                for m in range(CB):
                    ins = nc.tensor.transpose(proj_ps[:, CTX_BANK[0], m * P:(m + 1) * P], ctx_nat[buf][:, m, 0:P], ident[:, :])
                ins.then_inc(ctx_turned, 1)
                for m in range(CB):
                    ins = nc.tensor.transpose(proj_ps[:, CTX_BANK[1], m * P:(m + 1) * P], ctx_nat[buf][:, m, P:2 * P], ident[:, :])
                ins.then_inc(ctx_turned, 1)

            def context_pairs(hi, lo, moving_context, cols):
                pairs = [(ctxT_hi, hi[:, 0, :]), (ctxT_lo, hi[:, 0, :]), (ctxT_hi, lo[:, 0, :]),
                         (ctxT_rest, hi[:, 1, :]), (ctxT_rest, lo[:, 1, :])]
                return [(w[:, cols], c[:, :]) if moving_context else (c[:, cols], w) for c, w in pairs]

            def keys(t, hp):
                if hp == 0:
                    pe.wait_ge(ctxT_done, 2 * t + 2)
                if hp == 0:
                    after(pe, v_even_done, 2 * t)
                elif hp == 3:
                    pe.wait_ge(kT_done, HP * t + 1)
                products(proj_ps[:, KEY_BANK[hp], :], context_pairs(wk_hi, wk_lo, True, slice(hp * P, (hp + 1) * P))
                         ).then_inc(k_full, 1)

            def values(t, m):
                if m < 3:
                    pe.wait_ge(kT_done, HP * t + m + 2)
                else:
                    pe.wait_ge(v_even_done, 2 * t + 1)
                products(proj_ps[:, VALUE_BANK[m], :], context_pairs(wv_hi, wv_lo, False, slice(m * P, (m + 1) * P))
                         ).then_inc(v_full, 1)

            def turn_xn(u):
                pe.wait_ge(xn_done, UT * u + UT)
                after(pe, x_done, UT * u - 1)
                for k in range(KD):
                    for a in range(UT):
                        c = k * UTOK + a * P
                        ins = nc.tensor.transpose(turn_ps[:, c:c + P], xn[:, a, k * P:(k + 1) * P], ident[:, :])
                ins.then_inc(xn_turned, 1)

            def queries(u, g):
                if g == 0:
                    pe.wait_ge(xnT_done, u + 1)
                else:
                    pe.wait_ge(q_done, 4 * u + 2)
                for i in range(2):
                    cols = slice((2 * g + i) * P, (2 * g + i + 1) * P)
                    ins = products(turn_ps[:, i * UTOK:(i + 1) * UTOK],
                                   [(w[:, k, cols], m[:, k, :]) for k in range(KD)
                                    for w, m in ((wq_hi, xnT_hi), (wq_hi, xnT_lo), (wq_lo, xnT_hi))])
                ins.then_inc(q_full, 1)

            def scores(u, a, n):
                t, b = UT * u + a, n // 2
                if n == 0:
                    pe.wait_ge(q_done, 4 * u + 4)
                    pe.wait_ge(kT_done, HP * t + HP)
                if n < TB:
                    after(pe, oT_done, 2 * TB * (t - 1) + 2 * n + 2)
                for i in range(2):
                    hp = 2 * (n % 2) + i
                    ins = products(score_ps[:, n, i * NC:(i + 1) * NC],
                                   [(q[:, hp, TB * a + b, :], k[:, hp, b * NC:(b + 1) * NC])
                                    for q, k in ((q_hi, kT_hi), (q_lo, kT_hi), (q_hi, kT_lo))])
                ins.then_inc(score_full, 1)

            def turn_probs(t, g):
                b = g // 2
                if g % 2 == 0:
                    pe.wait_ge(probs_done, TB * t + b + 1)
                if g == 0:
                    after(pe, x_done, t)
                else:
                    pe.wait_ge(pt_even_done if g % 2 else pt_odd_done, 2 * t + (g + 1) // 2)
                for i in range(2):
                    for j in range(JT):
                        c = (2 * i + j) * P
                        ins = nc.tensor.transpose(turn_ps[:, c:c + P],
                                                  probs[:, b, 2 * (g % 2) + i, j * P:(j + 1) * P], ident[:, :])
                ins.then_inc(pt_full, 1)

            def mix_values(t, buf):
                pe.wait_ge(v_even_done, 2 * t + 2)
                pe.wait_ge(v_odd_done, 2 * t + 2)
                for b in range(TB):
                    pe.wait_ge(pt_even_done, 2 * t + b + 1)
                    pe.wait_ge(pt_odd_done, 2 * t + b + 1)
                    for hp in range(HP):
                        ins = products(score_ps[:, b, hp * P:(hp + 1) * P],
                                       [(v_nat[buf][:, JT * b + j, hp * P:(hp + 1) * P],
                                         probsT[:, 2 * b + hp // 2, (2 * (hp % 2) + j) * P:(2 * (hp % 2) + j + 1) * P])
                                        for j in range(JT)])
                    ins.then_inc(o_full, 1)

            def project_out(t):
                pe.wait_ge(oT_done, 2 * TB * t + 2 * TB)
                products(turn_ps[:, 0:D],
                         [(ones_rows[:, :], bo_rows[:, :])] +
                         [(o[:, hp, :], w[:, hp, :]) for hp in range(HP)
                          for o, w in ((oT_hi, wo_hi), (oT_lo, wo_hi), (oT_hi, wo_lo))]).then_inc(out_full, 1)

            pe.wait_ge(ident_done, 1)
            pe.wait_ge(consts_done, CONSTS)
            turn_ctx(0, 0)
            turn_xn(0)
            pe.wait_ge(w_lo_done, WEIGHTS - 1)
            keys(0, 0)
            keys(0, 1)
            queries(0, 0)
            keys(0, 2)
            keys(0, 3)
            queries(0, 1)
            for m in range(CB):
                values(0, m)

            def tile(u, a, last):
                t = UT * u + a
                more = not (last and a == 1)
                if more:
                    turn_ctx(u + (a + 1) // 2, (a + 1) % 2)
                scores(u, a, 0)
                if not (isinstance(t, int) and t == 0):
                    project_out(t - 1)
                for n in range(1, 4):
                    scores(u, a, n)
                if not last and a == 1:
                    turn_xn(u + 1)
                if more:
                    keys(t + 1, 0)
                    keys(t + 1, 1)
                if not last and a == 1:
                    queries(u + 1, 0)
                if more:
                    keys(t + 1, 2)
                    keys(t + 1, 3)
                if not last and a == 1:
                    queries(u + 1, 1)
                for g in range(4):
                    if more:
                        values(t + 1, g)
                    if g == 0 and not last and a == 1:
                        pe.wait_ge(q_done, 4 * u + 8)
                    turn_probs(t, g)
                mix_values(t, a)

            tile(0, 0, False)
            tile(0, 1, False)
            with pe.Fori(1, NU - 1) as u:
                tile(u, 0, False)
                tile(u, 1, False)
            tile(NU - 1, 0, True)
            tile(NU - 1, 1, True)
            project_out(NT - 1)


def linear_attention(nc, Wq, bq, Wk, bk, Wv, bv, Wo, bo, rw, xres, ident):
    D = Wq.shape[0]
    H, DK, F = rw.shape
    NT = xres.shape[1]
    UT = 2
    NU = NT // UT
    UTOK = UT * P
    TB = 2
    ROWS = P // TB
    KD = D // P
    HP = H // 2
    GP = HP // KD
    DV = DK + 1
    PAIR = TB * 2 * DV
    assert GP * P == BANK and 2 * F == P and KD * UTOK == BANK

    with ExitStack() as stack:
        def sb(name, shape, dt=F32):
            return stack.enter_context(nc.sbuf_tensor("la_" + name, shape, dt))

        def sem(name):
            return stack.enter_context(nc.semaphore("la_" + name))

        raw = [sb(f"raw{i}", [P, KD, D]) for i in range(4)]
        raw_rw = sb("raw_rw", [P, KD, BANK])
        split = {n: (sb(n + "_hi", [P, KD, D], F32R), sb(n + "_lo", [P, KD, D], F32R)) for n in ("wq", "wk", "wv", "wo")}
        rw_hi = sb("rw_hi", [P, KD, BANK], F32R)
        rw_lo = sb("rw_lo", [P, KD, BANK], F32R)
        bias_cols = sb("bias_cols", [P, 2, KD])
        bias_raw = sb("bias_raw", [P, 2, D])
        bias_rows = sb("bias_rows", [P, 2, D], F32R)
        ones_rows = sb("ones_rows", [P, P], F32R)

        scratch = sb("scratch", [P, 1])
        stats = sb("stats", [P, UT, 6])
        moments = sb("moments", [P, UT, 2])
        var_eps = sb("var_eps", [P, UT, 1])
        rstd = sb("rstd", [P, UT, 1])
        minus_half = sb("minus_half", [P, UT, 1])
        xn = sb("xn", [P, UT, D])
        xnT_hi = sb("xnT_hi", [P, KD, UTOK], F32R)
        xnT_lo = sb("xnT_lo", [P, KD, UTOK], F32R)
        qk_hi = [sb(f"{n}_hi", [P, KD, UTOK], F32R) for n in "qk"]
        qk_lo = [sb(f"{n}_lo", [P, KD, UTOK], F32R) for n in "qk"]
        v_ones = sb("v_ones", [P, UT, HP, TB, 2, DV])
        k_feat = sb("k_feat", [P, UT, KD, BANK])
        q_feat = sb("q_feat", [P, HP, UTOK])
        kv = sb("kv", [P, UT, HP, TB, 2, DV])
        den = sb("den", [P, UT, H])
        inv_den = sb("inv_den", [P, UT, H])
        o_nat = sb("o_nat", [P, UT, D])
        oT_hi = sb("oT_hi", [P, UT, KD, P], F32R)
        oT_lo = sb("oT_lo", [P, UT, KD, P], F32R)

        turn_ps = stack.enter_context(nc.psum_tensor("la_turn_ps", [P, BANK], F32))
        q_ps = stack.enter_context(nc.psum_tensor("la_q_ps", [P, BANK], F32))
        k_ps = stack.enter_context(nc.psum_tensor("la_k_ps", [P, BANK], F32))
        feat_ps = stack.enter_context(nc.psum_tensor("la_feat_ps", [P, 2, BANK], F32))
        sum_ps = stack.enter_context(nc.psum_tensor("la_sum_ps", [P, 2, BANK], F32))
        ends_ps = stack.enter_context(nc.psum_tensor("la_ends_ps", [P, BANK], F32))

        w_here = sem("w_here")
        rw_zeroed = sem("rw_zeroed")
        rows_zeroed = sem("rows_zeroed")
        consts_done = sem("consts_done")
        w_hi_done = sem("w_hi_done")
        w_lo_done = sem("w_lo_done")
        stats_done = sem("stats_done")
        moments_done = sem("moments_done")
        var_done = sem("var_done")
        rstd_done = sem("rstd_done")
        xn_done = sem("xn_done")
        xn_turned = sem("xn_turned")
        xnT_hi_done = sem("xnT_hi_done")
        xnT_done = sem("xnT_done")
        qk_full = [sem("q_full"), sem("k_full")]
        qk_hi_done = [sem("q_hi_done"), sem("k_hi_done")]
        qk_done = [sem("q_done"), sem("k_done")]
        v_full = sem("v_full")
        v_done = sem("v_done")
        feat_full = sem("feat_full")
        feat_done = sem("feat_done")
        kv_full = sem("kv_full")
        kv_done = sem("kv_done")
        num_full = sem("num_full")
        den_done = sem("den_done")
        inv_done = sem("inv_done")
        o_done = sem("o_done")
        o_turned = sem("o_turned")
        oT_hi_done = sem("oT_hi_done")
        oT_done = sem("oT_done")
        out_full = sem("out_full")
        x_done = sem("x_done")

        W_HERE = 16 * (4 + 2 + 4 + H)
        CONSTS = 1 + 2 + 1 + 2 * TB
        FEATS = 2 * UT + HP // 2
        block = stack.enter_context(nc.Block())

        @block.sync
        def _(sp):
            for r, w in zip(raw, (Wq, Wk, Wv, Wo)):
                sp.dma_start(r[:, :, :], w.rearrange("(k p) n -> p k n", p=P)).then_inc(w_here, 16)
            for i, b in enumerate((bq, bk)):
                sp.dma_start(bias_cols[:, i, :], b.rearrange("(k p) -> p k", p=P), allow_slow_non_contiguous=True).then_inc(w_here, 16)
            for i, b in enumerate((bv, bo)):
                for row in (0, 32):
                    sp.dma_start(bias_raw[row:row + 1, i, :], b.rearrange("(a n) -> a n", a=1)).then_inc(w_here, 16)
            sp.wait_ge(rw_zeroed, 1)
            for h in range(H):
                k, i = h // (2 * GP), h % (2 * GP)
                sp.dma_start(raw_rw[i * DK:(i + 1) * DK, k, i * F:(i + 1) * F], rw[h, :, :]).then_inc(w_here, 16)

        @block.gpsimd
        def _(pool):
            pool.wait_ge(consts_done, CONSTS)
            with pool.Fori(0, NU) as u:
                pool.wait_ge(var_done, u + 1)
                nc.gpsimd.tensor_tensor(rstd[:, :, :], var_eps[:, :, :], minus_half[:, :, :], ALU.pow
                                        ).then_inc(rstd_done, 1)

        pieces = [(split[n][0][:, :, :], split[n][1][:, :, :], r[:, :, :]) for n, r in zip(("wq", "wk", "wv", "wo"), raw)]
        pieces.append((rw_hi[:, :, :], rw_lo[:, :, :], raw_rw[:, :, :]))
        WEIGHTS = len(pieces) + 2

        @block.scalar
        def _(act):
            def xnT_of(u):
                act.wait_ge(xn_turned, u + 1)
                nc.scalar.activation(xnT_hi[:, :, :].rearrange("p k n -> p (k n)"), turn_ps[:, :], ACT.Copy
                                     ).then_inc(xnT_hi_done, 1)

            def qk_of(u, i):
                act.wait_ge(qk_full[i], u + 1)
                for k in range(KD):
                    src = (q_ps, k_ps)[i][:, k * UTOK:(k + 1) * UTOK]
                    nc.scalar.activation(qk_hi[i][:, k, :], src, ACT.Identity, bias=bias_cols[:, i, k:k + 1]
                                         ).then_inc(qk_hi_done[i], 1)

            def v_of(u):
                act.wait_ge(v_full, u + 1)
                for a in range(UT):
                    for b in range(TB):
                        rows = slice(b * ROWS, (b + 1) * ROWS)
                        src = ends_ps[rows, a * D:(a + 1) * D].rearrange("p (c h d) -> p c h d", h=2, d=DK)
                        nc.scalar.activation(v_ones[rows, a, :, b, :, 0:DK], src, ACT.Copy).then_inc(v_done, 1)

            def kv_of(t, a):
                act.wait_ge(kv_full, t + 1)
                for h in range(2):
                    rows = slice(h * F, (h + 1) * F)
                    src = sum_ps[rows, :, 0:GP * PAIR].rearrange("p g (c n) -> p g c n", n=2 * DV)[:, :, :, h * DV:(h + 1) * DV]
                    dst = kv[rows, a, :, :, h, :].rearrange("p (g c) b d -> p g (c b) d", g=2)
                    nc.scalar.activation(dst, src, ACT.Copy).then_inc(kv_done, 1)

            def oT_of(t, a):
                act.wait_ge(o_turned, t + 1)
                nc.scalar.activation(oT_hi[:, a, :, :].rearrange("p k n -> p (k n)"), (turn_ps, q_ps)[a][:, 0:D],
                                     ACT.Copy).then_inc(oT_hi_done, 1)

            act.wait_ge(w_here, W_HERE)
            act.wait_ge(rw_zeroed, 1)
            for hi, lo, src in pieces:
                nc.scalar.activation(hi, src, ACT.Copy).then_inc(w_hi_done, 1)
            act.wait_ge(rows_zeroed, 2)
            for row in (0, 32):
                nc.scalar.activation(bias_rows[row:row + 1, :, :], bias_raw[row:row + 1, :, :], ACT.Copy
                                     ).then_inc(w_hi_done, 1)
            act.wait_ge(consts_done, CONSTS)
            xnT_of(0)
            qk_of(0, 0)
            qk_of(0, 1)
            v_of(0)

            def unit(u, first, last):
                if not first:
                    oT_of(UT * u - 1, 1)
                kv_of(UT * u, 0)
                if not last:
                    xnT_of(u + 1)
                kv_of(UT * u + 1, 1)
                if not last:
                    qk_of(u + 1, 0)
                    qk_of(u + 1, 1)
                oT_of(UT * u, 0)
                if not last:
                    v_of(u + 1)

            unit(0, True, False)
            with act.Fori(1, NU - 1) as u:
                unit(u, False, False)
            unit(NU - 1, False, True)
            oT_of(UT * NU - 1, 1)

        @block.vector
        def _(dve):
            def moments_of(u):
                for a in range(UT):
                    nc.vector.bn_stats(stats[:, a, :], slot(xres, UT * u + a)).then_inc(stats_done, 1)
                settle(nc, stats_done, UT * u + UT, scratch[:, :])
                for a in range(UT):
                    nc.vector.bn_aggr(moments[:, a, :], stats[:, a, :]).then_inc(moments_done, 1)
                dve.wait_ge(moments_done, UT * u + UT)
                nc.vector.tensor_scalar(var_eps[:, :, :], moments[:, :, 1:2], LN_EPS, None, ALU.add).then_inc(var_done, 1)

            def xn_of(u):
                dve.wait_ge(rstd_done, u + 1)
                for a in range(UT):
                    nc.vector.tensor_scalar(xn[:, a:a + 1, :], slot(xres, UT * u + a), moments[:, a, 0:1], rstd[:, a, :],
                                            ALU.subtract, ALU.mult).then_inc(xn_done, 1)

            def xnT_of(u):
                dve.wait_ge(xnT_hi_done, u + 1)
                nc.vector.tensor_tensor(xnT_lo[:, :, :].rearrange("p k n -> p (k n)"), turn_ps[:, :],
                                        xnT_hi[:, :, :].rearrange("p k n -> p (k n)").bitcast(F32), ALU.subtract
                                        ).then_inc(xnT_done, 1)

            def qk_of(u, i):
                dve.wait_ge(qk_hi_done[i], KD * u + KD)
                for k in range(KD):
                    nc.vector.scalar_tensor_tensor(out=qk_lo[i][:, k, :], in0=(q_ps, k_ps)[i][:, k * UTOK:(k + 1) * UTOK],
                                                   scalar=bias_cols[:, i, k:k + 1], in1=qk_hi[i][:, k, :].bitcast(F32),
                                                   op0=ALU.add, op1=ALU.subtract).then_inc(qk_done[i], 1)

            def feat_of(u, n, dst):
                dve.wait_ge(feat_full, FEATS * u + n + 1)
                nc.vector.tensor_scalar(dst, feat_ps[:, n % 2, :], 0.0, PHI_EPS, ALU.max, ALU.add).then_inc(feat_done, 1)

            def k_feat_of(u, a):
                for k in range(KD):
                    feat_of(u, KD * a + k, k_feat[:, a, k, :])

            def q_feat_of(u, c):
                feat_of(u, UT * KD + c, q_feat[:, 2 * c:2 * c + 2, :].rearrange("p c n -> p (c n)"))

            def divide(t, a):
                dve.wait_ge(num_full, t + 1)
                for b in range(TB):
                    rows = slice(b * ROWS, (b + 1) * ROWS)
                    src = sum_ps[rows, :, 0:GP * PAIR].rearrange("p g (c b h d) -> p g c b h d", b=TB, h=2, d=DV)
                    nc.vector.tensor_scalar(den[rows, a, :].rearrange("p (g c h) -> p g c h", g=2, h=2),
                                            src[:, :, :, b, :, DK], PHI_EPS, None, ALU.add).then_inc(den_done, 1)
                dve.wait_ge(den_done, TB * t + TB)
                nc.vector.reciprocal(inv_den[:, a, :], den[:, a, :]).then_inc(inv_done, 1)
                dve.wait_ge(inv_done, t + 1)
                for b in range(TB):
                    rows = slice(b * ROWS, (b + 1) * ROWS)
                    for g in range(2):
                        src = sum_ps[rows, g, 0:GP * PAIR].rearrange("p (c b h d) -> p c b h d", b=TB, h=2, d=DV)
                        inv = inv_den[rows, a, g * 2 * GP:(g + 1) * 2 * GP].rearrange("p (c h) -> p c h", h=2)
                        dst = o_nat[rows, a, g * P:(g + 1) * P].rearrange("p (c h d) -> p c h d", h=2, d=DK)
                        nc.vector.tensor_tensor(dst, src[:, :, b, :, 0:DK], inv.unsqueeze(3).to_broadcast([ROWS, GP, 2, DK]),
                                                ALU.mult).then_inc(o_done, 1)

            def oT_of(t, a):
                dve.wait_ge(oT_hi_done, t + 1)
                nc.vector.tensor_tensor(oT_lo[:, a, :, :].rearrange("p k n -> p (k n)"), (turn_ps, q_ps)[a][:, 0:D],
                                        oT_hi[:, a, :, :].rearrange("p k n -> p (k n)").bitcast(F32), ALU.subtract
                                        ).then_inc(oT_done, 1)

            def x_of(u):
                dve.wait_ge(out_full, u + 1)
                dst = xres[:, bass.ds(UT * u, UT), :]
                nc.vector.tensor_tensor(dst, ends_ps[:, :].rearrange("p (a n) -> p a n", a=UT), dst, ALU.add
                                        ).then_inc(x_done, 1)

            nc.vector.memset(minus_half[:, :, :], -0.5).then_inc(consts_done, 1)
            nc.vector.memset(raw_rw[:, :, :], 0.0).then_inc(rw_zeroed, 1)
            nc.vector.memset(ones_rows[:, :].bitcast(F32), 0.0).then_inc(rows_zeroed, 1)
            nc.vector.memset(bias_rows[:, :, :].bitcast(F32), 0.0).then_inc(rows_zeroed, 1)
            nc.vector.memset(v_ones[:, :, :, :, :, :].rearrange("p a c b h d -> p (a c b h d)"), 0.0).then_inc(rows_zeroed, 1)
            nc.vector.memset(kv[:, :, :, :, :, :].rearrange("p a c b h d -> p (a c b h d)"), 0.0).then_inc(consts_done, 1)
            dve.wait_ge(rows_zeroed, 3)
            for row in (0, 32):
                nc.vector.memset(ones_rows[row:row + 1, :].bitcast(F32), 1.0).then_inc(consts_done, 1)
            for a in range(UT):
                for b in range(TB):
                    rows = slice(b * ROWS, (b + 1) * ROWS)
                    nc.vector.memset(v_ones[rows, a, :, b, :, DK:DV], 1.0).then_inc(consts_done, 1)
            moments_of(0)
            xn_of(0)
            dve.wait_ge(w_here, W_HERE)
            for n, (hi, lo, src) in enumerate(pieces):
                dve.wait_ge(w_hi_done, n + 1)
                nc.vector.tensor_tensor(lo, src, hi.bitcast(F32), ALU.subtract).then_inc(w_lo_done, 1)
            dve.wait_ge(w_hi_done, WEIGHTS)
            nc.vector.tensor_tensor(bias_rows[32:33, :, :], bias_raw[32:33, :, :], bias_rows[32:33, :, :].bitcast(F32),
                                    ALU.subtract).then_inc(w_lo_done, 1)
            xnT_of(0)
            qk_of(0, 0)
            qk_of(0, 1)

            def unit(u, first, last):
                k_feat_of(u, 0)
                if not first:
                    oT_of(UT * u - 1, 1)
                k_feat_of(u, 1)
                if not last:
                    moments_of(u + 1)
                    xn_of(u + 1)
                q_feat_of(u, 0)
                q_feat_of(u, 1)
                if not first:
                    x_of(u - 1)
                if not last:
                    xnT_of(u + 1)
                q_feat_of(u, 2)
                q_feat_of(u, 3)
                if not last:
                    qk_of(u + 1, 0)
                divide(UT * u, 0)
                if not last:
                    qk_of(u + 1, 1)
                oT_of(UT * u, 0)
                divide(UT * u + 1, 1)

            unit(0, True, False)
            with dve.Fori(1, NU - 1) as u:
                unit(u, False, False)
            unit(NU - 1, False, True)
            oT_of(UT * NU - 1, 1)
            x_of(NU - 1)

        @block.tensor
        def _(pe):
            def products(out, pairs):
                for n, (w, m) in enumerate(pairs):
                    ins = nc.tensor.matmul(out, w, m, start=n == 0, stop=n == len(pairs) - 1)
                return ins

            def three(w_hi, w_lo, m_hi, m_lo):
                return [(w_hi, m_hi), (w_lo, m_hi), (w_hi, m_lo)]

            def turn_xn(u):
                pe.wait_ge(xn_done, UT * u + UT)
                after(pe, oT_done, UT * (u - 1))
                for k in range(KD):
                    for a in range(UT):
                        c = k * UTOK + a * P
                        ins = nc.tensor.transpose(turn_ps[:, c:c + P], xn[:, a, k * P:(k + 1) * P], ident[:, :])
                ins.then_inc(xn_turned, 1)

            def project_qk(u, i):
                pe.wait_ge(xnT_done, u + 1)
                if i == 0:
                    after(pe, oT_done, UT * (u - 1))
                w_hi, w_lo = split[("wq", "wk")[i]]
                for m in range(KD):
                    cols = slice(m * P, (m + 1) * P)
                    ins = products((q_ps, k_ps)[i][:, m * UTOK:(m + 1) * UTOK],
                                   [pair for k in range(KD) for pair in
                                    three(w_hi[:, k, cols], w_lo[:, k, cols], xnT_hi[:, k, :], xnT_lo[:, k, :])])
                ins.then_inc(qk_full[i], 1)

            def project_v(u):
                after(pe, x_done, u - 1)
                w_hi, w_lo = split["wv"]
                for a in range(UT):
                    tok = slice(a * P, (a + 1) * P)
                    ins = products(ends_ps[:, a * D:(a + 1) * D],
                                   [(ones_rows[:, :], bias_rows[:, 0, :])] +
                                   [pair for k in range(KD) for pair in
                                    three(xnT_hi[:, k, tok], xnT_lo[:, k, tok], w_hi[:, k, :], w_lo[:, k, :])])
                ins.then_inc(v_full, 1)

            def k_features(u, a):
                pe.wait_ge(qk_done[1], KD * u + KD)
                tok = slice(a * P, (a + 1) * P)
                for k in range(KD):
                    n = KD * a + k
                    after(pe, feat_done, FEATS * u + max(n - 1, 0))
                    products(feat_ps[:, n % 2, :], three(qk_hi[1][:, k, tok], qk_lo[1][:, k, tok],
                                                         rw_hi[:, k, :], rw_lo[:, k, :])).then_inc(feat_full, 1)

            def q_features(u, c):
                if c == 0:
                    pe.wait_ge(qk_done[0], KD * u + KD)
                n = UT * KD + c
                pe.wait_ge(feat_done, FEATS * u + n - 1)
                for i in range(2):
                    k, pair = (2 * c + i) // GP, (2 * c + i) % GP
                    cols = slice(pair * P, (pair + 1) * P)
                    ins = products(feat_ps[:, n % 2, i * UTOK:(i + 1) * UTOK],
                                   three(rw_hi[:, k, cols], rw_lo[:, k, cols], qk_hi[0][:, k, :], qk_lo[0][:, k, :]))
                ins.then_inc(feat_full, 1)

            def sum_kv(u, a):
                t = UT * u + a
                if a == 0:
                    pe.wait_ge(v_done, UT * TB * u + UT * TB)
                    after(pe, o_done, 2 * TB * t)
                else:
                    pe.wait_ge(kv_done, 2 * t)
                pe.wait_ge(feat_done, FEATS * u + KD * (a + 1))
                for c in range(HP):
                    out = sum_ps[:, c // GP, (c % GP) * PAIR:(c % GP + 1) * PAIR]
                    ins = nc.tensor.matmul(out, k_feat[:, a, c // GP, (c % GP) * P:(c % GP + 1) * P],
                                           v_ones[:, a, c, :, :, :].rearrange("p b h d -> p (b h d)"), start=True, stop=True)
                ins.then_inc(kv_full, 1)

            def numerators(u, a):
                t = UT * u + a
                if a == 0:
                    pe.wait_ge(feat_done, FEATS * u + FEATS)
                    pe.wait_ge(kv_done, 2 * t + 4)
                else:
                    pe.wait_ge(o_done, 2 * TB * t)
                tok = slice(a * P, (a + 1) * P)
                for c in range(HP):
                    out = sum_ps[:, c // GP, (c % GP) * PAIR:(c % GP + 1) * PAIR]
                    ins = nc.tensor.matmul(out, q_feat[:, c, tok],
                                           kv[:, a, c, :, :, :].rearrange("p b h d -> p (b h d)"), start=True, stop=True)
                ins.then_inc(num_full, 1)

            def turn_o(u, a, q_done_next=None):
                t = UT * u + a
                pe.wait_ge(o_done, 2 * TB * t + 2 * TB)
                if a == 1:
                    pe.wait_ge(qk_done[0], q_done_next)
                for k in range(KD):
                    ins = nc.tensor.transpose((turn_ps, q_ps)[a][:, k * P:(k + 1) * P], o_nat[:, a, k * P:(k + 1) * P], ident[:, :])
                ins.then_inc(o_turned, 1)

            def project_out(u, a, last_v):
                t = UT * u + a
                pe.wait_ge(oT_done, t + 1)
                if a == 0:
                    pe.wait_ge(v_done, last_v)
                w_hi, w_lo = split["wo"]
                ins = products(ends_ps[:, a * D:(a + 1) * D],
                         [(ones_rows[:, :], bias_rows[:, 1, :])] +
                         [pair for k in range(KD) for pair in
                          three(oT_hi[:, a, k, :], oT_lo[:, a, k, :], w_hi[:, k, :], w_lo[:, k, :])])
                if a == UT - 1:
                    ins.then_inc(out_full, 1)

            pe.wait_ge(consts_done, CONSTS)
            turn_xn(0)
            pe.wait_ge(w_lo_done, WEIGHTS - 1)
            project_qk(0, 0)
            project_qk(0, 1)
            project_v(0)

            def unit(u, first, last):
                V_DONE = UT * TB * (u + 1)
                k_features(u, 0)
                if not first:
                    project_out(u - 1, 0, V_DONE)
                    turn_o(u - 1, 1, KD * u + KD)
                k_features(u, 1)
                sum_kv(u, 0)
                if not first:
                    project_out(u - 1, 1, V_DONE)
                q_features(u, 0)
                q_features(u, 1)
                if not last:
                    turn_xn(u + 1)
                sum_kv(u, 1)
                q_features(u, 2)
                q_features(u, 3)
                if not last:
                    project_qk(u + 1, 0)
                numerators(u, 0)
                if not last:
                    project_qk(u + 1, 1)
                    project_v(u + 1)
                turn_o(u, 0)
                numerators(u, 1)

            unit(0, True, False)
            with pe.Fori(1, NU - 1) as u:
                unit(u, False, False)
            unit(NU - 1, False, True)
            project_out(NU - 1, 0, UT * TB * NU)
            turn_o(NU - 1, 1, KD * NU)
            project_out(NU - 1, 1, UT * TB * NU)


def mixture(nc, router_w, w_in, b_in, w_out, b_out, xres, ident, out):
    E, D, H = w_in.shape
    TOP = 2
    NT = xres.shape[1]
    UT = 4
    NU = NT // UT
    UTOK = UT * P
    KD = D // P
    KH = H // P
    LANE = 32
    USES = E + 1
    assert UTOK == BANK and 2 * D == BANK and TOP == 2

    out_tiles = out.rearrange("(t b) q d -> (b q) t d", b=P // out.shape[1])

    with ExitStack() as stack:
        def sb(name, shape, dt=F32):
            return stack.enter_context(nc.sbuf_tensor("moe_" + name, shape, dt))

        def sem(name):
            return stack.enter_context(nc.semaphore("moe_" + name))

        raw_in = sb("raw_in", [P, E, KD, H])
        raw_out = sb("raw_out", [P, E, KH, D])
        win_hi = sb("win_hi", [P, E, KD, H], F32R)
        win_lo = sb("win_lo", [P, E, KD, H], F32R)
        wout_hi = sb("wout_hi", [P, E, KH, D], F32R)
        wout_lo = sb("wout_lo", [P, E, KH, D], F32R)
        raw_router = sb("raw_router", [P, KD, E])
        router_hi = sb("router_hi", [P, KD, E], F32R)
        router_lo = sb("router_lo", [P, KD, E], F32R)
        b_in_cols = sb("b_in_cols", [P, E, KH])
        b_out_raw = sb("b_out_raw", [P, D])
        b_out_rows = sb("b_out_rows", [P, D], F32R)
        expert_ids = sb("expert_ids", [P, UT, E])

        scratch = sb("scratch", [P, 1])
        stats = sb("stats", [P, UT, 6])
        moments = sb("moments", [P, UT, 2])
        var_eps = sb("var_eps", [P, UT, 1])
        rstd = sb("rstd", [P, UT, 1])
        minus_half = sb("minus_half", [P, UT, 1])
        xn = sb("xn", [P, UT, D])
        xnT_hi = sb("xnT_hi", [P, KD, UTOK], F32R)
        xnT_lo = sb("xnT_lo", [P, KD, UTOK], F32R)
        neg_max = sb("neg_max", [P, UT, 1])
        shifted = sb("shifted", [P, UT, E])
        exps = sb("exps", [P, UT, E])
        exp_sum = sb("exp_sum", [P, UT, 1])
        inv_sum = sb("inv_sum", [P, UT, 1])
        probs = sb("probs", [P, UT, E])
        top_p = sb("top_p", [P, UT, 8])
        top_id = sb("top_id", [P, UT, 8], U32)
        top_idf = sb("top_idf", [P, UT, 8])
        is_first = sb("is_first", [P, UT, E])
        is_second = sb("is_second", [P, UT, E])
        chosen = sb("chosen", [P, UT, E])
        gates = sb("gates", [P, UT, E])
        gate_parts = sb("gate_parts", [P, UT, P])
        gatesT = sb("gatesT", [P, UTOK], F32R)
        h = [sb(f"h{i}", [P, KH, UTOK]) for i in range(2)]
        h_hi = [sb(f"h_hi{i}", [P, KH, UTOK], F32R) for i in range(2)]
        h_lo = [sb(f"h_lo{i}", [P, KH, UTOK], F32R) for i in range(2)]

        h_ps = stack.enter_context(nc.psum_tensor("moe_h_ps", [P, 4, BANK], F32))
        y_ps = stack.enter_context(nc.psum_tensor("moe_y_ps", [P, 2, BANK], F32))
        aux_ps = stack.enter_context(nc.psum_tensor("moe_aux_ps", [P, 2, BANK], F32))

        w_here = sem("w_here")
        zeroed = sem("zeroed")
        ids_done = sem("ids_done")
        consts_done = sem("consts_done")
        w_hi_done = sem("w_hi_done")
        w_lo_done = sem("w_lo_done")
        stats_done = sem("stats_done")
        moments_done = sem("moments_done")
        var_done = sem("var_done")
        rstd_done = sem("rstd_done")
        xn_done = sem("xn_done")
        xn_turned = sem("xn_turned")
        xnT_hi_done = sem("xnT_hi_done")
        xnT_done = sem("xnT_done")
        logits_full = sem("logits_full")
        shifted_done = sem("shifted_done")
        exps_done = sem("exps_done")
        route = sem("route")
        gates_turned = sem("gates_turned")
        gatesT_done = sem("gatesT_done")
        h_full = sem("h_full")
        gelu_done = sem("gelu_done")
        h_hi_done = sem("h_hi_done")
        h_done = sem("h_done")
        y_full = sem("y_full")
        y_done = sem("y_done")
        stored = sem("stored")

        W_HERE = 16 * (2 * E + KD + E + 3)
        CONSTS = 1
        ROUTE = 5 + 2 * UT + 7
        block = stack.enter_context(nc.Block())

        @block.sync
        def _(sp):
            for e in range(E):
                sp.dma_start(raw_in[:, e, :, :], w_in[e].rearrange("(k p) n -> p k n", p=P)).then_inc(w_here, 16)
                sp.dma_start(raw_out[:, e, :, :], w_out[e].rearrange("(k p) n -> p k n", p=P)).then_inc(w_here, 16)
                sp.dma_start(b_in_cols[:, e, :], b_in[e].rearrange("(k p) -> p k", p=P),
                             allow_slow_non_contiguous=True).then_inc(w_here, 16)
            for k in range(KD):
                sp.dma_start(raw_router[:, k, :], router_w[k * P:(k + 1) * P, :]).then_inc(w_here, 16)
            sp.wait_ge(zeroed, 3)
            for n in range(3):
                sp.dma_start(b_out_raw[n * LANE:n * LANE + E, :], b_out).then_inc(w_here, 16)

            with sp.Fori(0, NU) as u:
                sp.wait_ge(y_done, 2 * USES * u + 2 * USES)
                sp.dma_start(out_tiles[:, bass.ds(UT * u, UT), :], xres[:, bass.ds(UT * u, UT), :]).then_inc(stored, 16)
            sp.wait_ge(stored, 16 * NU)

        @block.gpsimd
        def _(pool):
            nc.gpsimd.iota(expert_ids[:, :, :], pattern=[[0, UT], [1, E]], base=0, channel_multiplier=0,
                           allow_small_or_imprecise_dtypes=True).then_inc(ids_done, 1)
            pool.wait_ge(ids_done, 1)
            pool.wait_ge(consts_done, CONSTS)
            with pool.Fori(0, NU) as u:
                pool.wait_ge(var_done, u + 1)
                nc.gpsimd.tensor_tensor(rstd[:, :, :], var_eps[:, :, :], minus_half[:, :, :], ALU.pow
                                        ).then_inc(rstd_done, 1)

        pieces = [(router_hi[:, :, :], router_lo[:, :, :], raw_router[:, :, :])]
        for e in range(E):
            pieces.append((win_hi[:, e, :, :], win_lo[:, e, :, :], raw_in[:, e, :, :]))
            pieces.append((wout_hi[:, e, :, :], wout_lo[:, e, :, :], raw_out[:, e, :, :]))
        WEIGHTS = len(pieces) + 1

        @block.scalar
        def _(act):
            def xnT_of(u):
                for k in range(KD):
                    act.wait_ge(xn_turned, KD * u + k + 1)
                    nc.scalar.activation(xnT_hi[:, k, :], aux_ps[:, k, :], ACT.Copy).then_inc(xnT_hi_done, 1)

            def exps_of(u):
                act.wait_ge(shifted_done, u + 1)
                nc.scalar.activation(exps[:, :, :], shifted[:, :, :], ACT.Exp).then_inc(exps_done, 1)

            def gatesT_of(u):
                act.wait_ge(gates_turned, u + 1)
                nc.scalar.activation(gatesT[:, :], aux_ps[:, 1, :], ACT.Copy).then_inc(gatesT_done, 1)

            def hidden_of(u, e):
                i = e % 2
                for m in range(KH):
                    act.wait_ge(h_full, KH * (E * u + e) + m + 1)
                    nc.scalar.activation(h[i][:, m, :], h_ps[:, 2 * i + m, :], ACT.Gelu_apprx_tanh,
                                         bias=b_in_cols[:, e, m:m + 1]).then_inc(gelu_done, 1)
                for m in range(KH):
                    act.wait_ge(gelu_done, KH * (E * u + e) + m + 1)
                    nc.scalar.activation(h_hi[i][:, m, :], h[i][:, m, :], ACT.Copy).then_inc(h_hi_done, 1)

            act.wait_ge(w_here, W_HERE)
            for hi, lo, src in pieces:
                nc.scalar.activation(hi, src, ACT.Copy).then_inc(w_hi_done, 1)
            act.wait_ge(zeroed, 3)
            nc.scalar.activation(b_out_rows[:, :], b_out_raw[:, :], ACT.Copy).then_inc(w_hi_done, 1)
            xnT_of(0)
            exps_of(0)

            def unit(u, last):
                hidden_of(u, 0)
                hidden_of(u, 1)
                gatesT_of(u)
                for e in range(2, E):
                    hidden_of(u, e)
                if not last:
                    xnT_of(u + 1)
                    exps_of(u + 1)

            with act.Fori(0, NU - 1) as u:
                unit(u, False)
            unit(NU - 1, True)

        @block.vector
        def _(dve):
            def moments_of(u):
                for a in range(UT):
                    nc.vector.bn_stats(stats[:, a, :], slot(xres, UT * u + a)).then_inc(stats_done, 1)
                settle(nc, stats_done, UT * u + UT, scratch[:, :])
                for a in range(UT):
                    nc.vector.bn_aggr(moments[:, a, :], stats[:, a, :]).then_inc(moments_done, 1)
                dve.wait_ge(moments_done, UT * u + UT)
                nc.vector.tensor_scalar(var_eps[:, :, :], moments[:, :, 1:2], LN_EPS, None, ALU.add).then_inc(var_done, 1)

            def xn_of(u):
                dve.wait_ge(rstd_done, u + 1)
                for a in range(UT):
                    nc.vector.tensor_scalar(xn[:, a:a + 1, :], slot(xres, UT * u + a), moments[:, a, 0:1], rstd[:, a, :],
                                            ALU.subtract, ALU.mult).then_inc(xn_done, 1)

            def xnT_of(u):
                for k in range(KD):
                    dve.wait_ge(xnT_hi_done, KD * u + k + 1)
                    nc.vector.tensor_tensor(xnT_lo[:, k, :], aux_ps[:, k, :], xnT_hi[:, k, :].bitcast(F32), ALU.subtract
                                            ).then_inc(xnT_done, 1)

            def shift_of(u):
                dve.wait_ge(logits_full, u + 1)
                lg = aux_ps[:, 0, 0:UT * E].rearrange("p (a e) -> p a e", e=E)
                nc.vector.tensor_reduce(neg_max[:, :, :].rearrange("p a o -> p (a o)"), lg, AX.X, ALU.max, negate=True
                                        ).then_inc(route, 1)
                dve.wait_ge(route, ROUTE * u + 1)
                nc.vector.tensor_tensor(shifted[:, :, :], lg, neg_max[:, :, :].to_broadcast([P, UT, E]), ALU.add
                                        ).then_inc(shifted_done, 1)

            def gates_of(u):
                step = ROUTE * u + 1
                dve.wait_ge(exps_done, u + 1)
                nc.vector.tensor_reduce(exp_sum[:, :, :].rearrange("p a o -> p (a o)"), exps[:, :, :], AX.X, ALU.add
                                        ).then_inc(route, 1)
                dve.wait_ge(route, step + 1)
                nc.vector.reciprocal(inv_sum[:, :, :], exp_sum[:, :, :]).then_inc(route, 1)
                dve.wait_ge(route, step + 2)
                nc.vector.tensor_tensor(probs[:, :, :], exps[:, :, :], inv_sum[:, :, :].to_broadcast([P, UT, E]), ALU.mult
                                        ).then_inc(route, 1)
                settle(nc, route, step + 3, scratch[:, :])
                for a in range(UT):
                    nc.vector.max(top_p[:, a, :], probs[:, a, :]).then_inc(route, 1)
                settle(nc, route, step + 3 + UT, scratch[:, :])
                for a in range(UT):
                    nc.vector.max_index(top_id[:, a, :], top_p[:, a, :], probs[:, a, :]).then_inc(route, 1)
                dve.wait_ge(route, step + 3 + 2 * UT)
                nc.vector.tensor_copy(top_idf[:, :, :], top_id[:, :, :]).then_inc(route, 1)
                dve.wait_ge(route, step + 4 + 2 * UT)
                for n, same in enumerate((is_first, is_second)):
                    nc.vector.tensor_tensor(same[:, :, :], expert_ids[:, :, :],
                                            top_idf[:, :, n:n + 1].to_broadcast([P, UT, E]), ALU.is_equal).then_inc(route, 1)
                dve.wait_ge(route, step + 6 + 2 * UT)
                nc.vector.tensor_tensor(chosen[:, :, :], is_first[:, :, :], is_second[:, :, :], ALU.add).then_inc(route, 1)
                dve.wait_ge(route, step + 7 + 2 * UT)
                nc.vector.tensor_tensor(gates[:, :, :], probs[:, :, :], chosen[:, :, :], ALU.mult).then_inc(route, 1)
                dve.wait_ge(route, step + 8 + 2 * UT)
                for lane in (0, 2):
                    nc.vector.tensor_copy(gate_parts[:, :, lane * LANE:lane * LANE + E].bitcast(F32R), gates[:, :, :]
                                          ).then_inc(route, 1)
                dve.wait_ge(route, step + 10 + 2 * UT)
                nc.vector.tensor_tensor(gate_parts[:, :, LANE:LANE + E], gates[:, :, :], gate_parts[:, :, 0:E], ALU.subtract
                                        ).then_inc(route, 1)

            def hidden_of(u, e):
                i = e % 2
                for m in range(KH):
                    dve.wait_ge(h_hi_done, KH * (E * u + e) + m + 1)
                    nc.vector.tensor_tensor(h_lo[i][:, m, :], h[i][:, m, :], h_hi[i][:, m, :].bitcast(F32), ALU.subtract
                                            ).then_inc(h_done, 1)

            def add_expert(u, use, e):
                for j in range(2):
                    dve.wait_ge(y_full, 2 * (USES * u + use) + j + 1)
                    after(dve, y_done, 2 * USES * u + max(2 * use + j - 1, 0))
                    for i in range(2):
                        a = 2 * j + i
                        dst = slot(xres, UT * u + a)
                        ins = nc.vector.scalar_tensor_tensor(out=dst, in0=y_ps[:, j, i * D:(i + 1) * D].unsqueeze(1),
                                                             scalar=gates[:, a, e:e + 1], in1=dst,
                                                             op0=ALU.mult, op1=ALU.add)
                    ins.then_inc(y_done, 1)

            def add_biases(u, use):
                for j in range(2):
                    dve.wait_ge(y_full, 2 * (USES * u + use) + j + 1)
                    dve.wait_ge(y_done, 2 * USES * u + max(2 * use + j - 1, 0))
                    dst = xres[:, bass.ds(UT * u + 2 * j, 2), :]
                    nc.vector.tensor_tensor(dst, y_ps[:, j, :].rearrange("p (i n) -> p i n", i=2), dst, ALU.add
                                            ).then_inc(y_done, 1)

            nc.vector.memset(minus_half[:, :, :], -0.5).then_inc(consts_done, 1)
            nc.vector.memset(b_out_raw[:, :], 0.0).then_inc(zeroed, 1)
            nc.vector.memset(b_out_rows[:, :].bitcast(F32), 0.0).then_inc(zeroed, 1)
            nc.vector.memset(gate_parts[:, :, :], 0.0).then_inc(zeroed, 1)
            moments_of(0)
            xn_of(0)
            dve.wait_ge(w_here, W_HERE)
            for n, (hi, lo, src) in enumerate(pieces):
                dve.wait_ge(w_hi_done, n + 1)
                nc.vector.tensor_tensor(lo, src, hi.bitcast(F32), ALU.subtract).then_inc(w_lo_done, 1)
            dve.wait_ge(w_hi_done, WEIGHTS)
            rows = slice(2 * LANE, 3 * LANE)
            nc.vector.tensor_tensor(b_out_rows[rows, :], b_out_raw[rows, :], b_out_rows[rows, :].bitcast(F32), ALU.subtract
                                    ).then_inc(w_lo_done, 1)
            xnT_of(0)
            shift_of(0)
            dve.wait_ge(ids_done, 1)
            dve.wait_ge(zeroed, 3)
            gates_of(0)

            def unit(u, last):
                hidden_of(u, 0)
                hidden_of(u, 1)
                add_expert(u, 0, 0)
                add_biases(u, 1)
                for e in range(2, E):
                    hidden_of(u, e)
                    add_expert(u, e, e - 1)
                    if not last and e == 3:
                        moments_of(u + 1)
                    if not last and e == 4:
                        xn_of(u + 1)
                if not last:
                    xnT_of(u + 1)
                add_expert(u, E, E - 1)
                if not last:
                    shift_of(u + 1)
                    gates_of(u + 1)

            unit(0, False)
            with dve.Fori(1, NU - 1) as u:
                unit(u, False)
            unit(NU - 1, True)

        @block.tensor
        def _(pe):
            def products(out, pairs):
                for n, (w, m) in enumerate(pairs):
                    ins = nc.tensor.matmul(out, w, m, start=n == 0, stop=n == len(pairs) - 1)
                return ins

            def three(w_hi, w_lo, m_hi, m_lo):
                return [(w_hi, m_hi), (w_lo, m_hi), (w_hi, m_lo)]

            def turn_xn(u, k):
                if k == 0:
                    pe.wait_ge(xn_done, UT * u + UT)
                    after(pe, shifted_done, u)
                    after(pe, gatesT_done, u)
                for a in range(UT):
                    ins = nc.tensor.transpose(aux_ps[:, k, a * P:(a + 1) * P], xn[:, a, k * P:(k + 1) * P], ident[:, :])
                ins.then_inc(xn_turned, 1)

            def logits(u):
                pe.wait_ge(xnT_done, KD * u + KD)
                for a in range(UT):
                    tok = slice(a * P, (a + 1) * P)
                    ins = products(aux_ps[:, 0, a * E:(a + 1) * E],
                                   [pair for k in range(KD) for pair in
                                    three(xnT_hi[:, k, tok], xnT_lo[:, k, tok], router_hi[:, k, :], router_lo[:, k, :])])
                ins.then_inc(logits_full, 1)

            def turn_gates(u):
                pe.wait_ge(route, ROUTE * u + ROUTE)
                for a in range(UT):
                    ins = nc.tensor.transpose(aux_ps[:, 1, a * P:(a + 1) * P], gate_parts[:, a, :], ident[:, :])
                ins.then_inc(gates_turned, 1)

            def hidden(u, e):
                i = e % 2
                if e == 0:
                    pe.wait_ge(xnT_done, KD * u + KD)
                for m in range(KH):
                    after(pe, gelu_done, KH * E * u + max(KH * (e - 2) + m + 1, 0))
                    cols = slice(m * P, (m + 1) * P)
                    products(h_ps[:, 2 * i + m, :],
                             [pair for k in range(KD) for pair in
                              three(win_hi[:, e, k, cols], win_lo[:, e, k, cols], xnT_hi[:, k, :], xnT_lo[:, k, :])]
                             ).then_inc(h_full, 1)

            def outputs(u, use, e):
                i = e % 2
                pe.wait_ge(h_done, KH * (E * u + e) + KH)
                for j in range(2):
                    after(pe, y_done, 2 * USES * u + max(2 * use + j - 1, 0))
                    for n in range(2):
                        tok = slice((2 * j + n) * P, (2 * j + n + 1) * P)
                        ins = products(y_ps[:, j, n * D:(n + 1) * D],
                                       [pair for k in range(KH) for pair in
                                        three(h_hi[i][:, k, tok], h_lo[i][:, k, tok], wout_hi[:, e, k, :], wout_lo[:, e, k, :])])
                    ins.then_inc(y_full, 1)

            def biases(u, use):
                pe.wait_ge(gatesT_done, u + 1)
                for j in range(2):
                    pe.wait_ge(y_done, 2 * USES * u + max(2 * use + j - 1, 0))
                    for n in range(2):
                        tok = slice((2 * j + n) * P, (2 * j + n + 1) * P)
                        ins = nc.tensor.matmul(y_ps[:, j, n * D:(n + 1) * D], gatesT[:, tok], b_out_rows[:, :],
                                               start=True, stop=True)
                    ins.then_inc(y_full, 1)

            turn_xn(0, 0)
            turn_xn(0, 1)
            pe.wait_ge(w_lo_done, WEIGHTS)
            logits(0)

            def unit(u, last):
                hidden(u, 0)
                hidden(u, 1)
                outputs(u, 0, 0)
                turn_gates(u)
                hidden(u, 2)
                biases(u, 1)
                outputs(u, 2, 1)
                for e in range(3, E):
                    hidden(u, e)
                    outputs(u, e, e - 1)
                if not last:
                    turn_xn(u + 1, 0)
                    turn_xn(u + 1, 1)
                outputs(u, E, E - 1)
                if not last:
                    logits(u + 1)

            unit(0, False)
            with pe.Fori(1, NU - 1) as u:
                unit(u, False)
            unit(NU - 1, True)


def perceiver_block(nc, x, ctx, xattn, attn, ffn, out):
    NT = x.shape[0] * x.shape[1] // P
    with ExitStack() as stack:
        xres = stack.enter_context(nc.sbuf_tensor("xres", [P, NT, x.shape[2]], F32))
        ident = stack.enter_context(nc.sbuf_tensor("ident", [P, P], F32))
        cross_attention(nc, x, ctx, *xattn, xres, ident)
        linear_attention(nc, *attn, xres, ident)
        mixture(nc, *ffn, xres, ident, out)


_XATTN = ["L0_xattn_Wq", "L0_xattn_Wk", "L0_xattn_Wv", "L0_xattn_Wo", "L0_xattn_bo"]
_ATTN = ["L0_attn_Wq", "L0_attn_bq", "L0_attn_Wk", "L0_attn_bk", "L0_attn_Wv", "L0_attn_bv", "L0_attn_Wo", "L0_attn_bo",
         "L0_attn_rw"]
_FFN = ["L0_ffn_router_w", "L0_ffn_w_in", "L0_ffn_b_in", "L0_ffn_w_out", "L0_ffn_b_out"]


def kernel(**inputs):
    import numpy as _np
    import concourse.bacc as _bacc
    from concourse.bass_utils import run_bass_kernel_spmd as _run

    nc = _bacc.Bacc("TRN2", target_bir_lowering=False, num_devices=1)
    arrays, aps = {}, {}
    for name in ["x", "ctx_768"] + _XATTN + _ATTN + _FFN:
        a = _np.ascontiguousarray(inputs[name])
        arrays[f"in_{name}"] = a
        aps[name] = nc.dram_tensor(f"in_{name}", a.shape, mybir.dt.from_np(a.dtype), kind="ExternalInput").ap()
    out = nc.dram_tensor("out", inputs["x"].shape, F32, kind="ExternalOutput").ap()
    perceiver_block(nc, aps["x"], aps["ctx_768"], [aps[n] for n in _XATTN], [aps[n] for n in _ATTN],
                    [aps[n] for n in _FFN], out)
    return _run(nc, [arrays], core_ids=[0]).results[0]["out"]
```

```python
from contextlib import ExitStack

import concourse.bass as bass
from concourse import mybir

F32 = mybir.dt.float32
F32R = mybir.dt.float32r
U32 = mybir.dt.uint32
ALU = mybir.AluOpType
ACT = mybir.ActivationFunctionType
AX = mybir.AxisListType

P = 128
BANK = 512
LN_EPS = 1e-5
PHI_EPS = 1e-6


def after(engine, semaphore, value):
    if isinstance(value, int) and value <= 0:
        return
    engine.wait_ge(semaphore, value)


def settle(nc, semaphore, value, scratch):
    nc.vector.wait_ge(semaphore, value)
    nc.vector.memset(scratch, 0.0)


def slot(tiles, t):
    return tiles[:, bass.ds(t, 1), :]


def linear_attention_weights(nc, stack, D, H, F):
    KD = D // P
    w = {}
    for name, cols in (("wq", D), ("wk", D), ("wv", D), ("wo", D), ("rw", H // KD * F)):
        for part in ("hi", "lo"):
            w[f"{name}_{part}"] = stack.enter_context(nc.sbuf_tensor(f"la_{name}_{part}", [P, KD, cols], F32R))
    w["bias_cols"] = stack.enter_context(nc.sbuf_tensor("la_bias_cols", [P, 2, KD], F32))
    w["bias_raw"] = stack.enter_context(nc.sbuf_tensor("la_bias_raw", [P, 2, D], F32))
    w["bias_rows"] = stack.enter_context(nc.sbuf_tensor("la_bias_rows", [P, 2, D], F32R))
    for name in ("rw_zeroed", "rows_zeroed", "here", "hi_done", "lo_done"):
        w[name] = stack.enter_context(nc.semaphore("la_w_" + name))
    return w


LA_PIECES = ("wq", "wk", "wv", "wo", "rw")


def la_raw(raw, n, w):
    start = sum(w[name + "_hi"].shape[1] * w[name + "_hi"].shape[2] for name in LA_PIECES[:n])
    _, kd, cols = w[LA_PIECES[n] + "_hi"].shape
    return raw[:, start:start + kd * cols].rearrange("p (k n) -> p k n", k=kd)


def linear_attention_loads(sp, raw, w, Wq, bq, Wk, bk, Wv, bv, Wo, bo, rw):
    H, DK, F = rw.shape
    KD = Wq.shape[0] // P

    def matrices():
        for n, src in enumerate((Wq, Wk, Wv, Wo)):
            sp.dma_start(la_raw(raw, n, w), src.rearrange("(k p) n -> p k n", p=P)).then_inc(w["here"], 16)

    def biases():
        for i, b in enumerate((bq, bk)):
            sp.dma_start(w["bias_cols"][:, i, :], b.rearrange("(k p) -> p k", p=P), allow_slow_non_contiguous=True
                         ).then_inc(w["here"], 16)
        for i, b in enumerate((bv, bo)):
            for row in (0, 32):
                sp.dma_start(w["bias_raw"][row:row + 1, i, :], b.rearrange("(a n) -> a n", a=1)).then_inc(w["here"], 16)

    def features(k):
        sp.wait_ge(w["rw_zeroed"], 1)
        for i in range(H // KD):
            sp.dma_start(la_raw(raw, 4, w)[i * DK:(i + 1) * DK, k, i * F:(i + 1) * F], rw[k * (H // KD) + i, :, :]
                         ).then_inc(w["here"], 16)

    return [matrices, biases] + [lambda k=k: features(k) for k in range(KD)]


def zero_linear_attention(nc, raw, w):
    nc.vector.memset(la_raw(raw, 4, w), 0.0).then_inc(w["rw_zeroed"], 1)
    nc.vector.memset(w["bias_rows"][:, :, :].bitcast(F32), 0.0).then_inc(w["rows_zeroed"], 1)


def split_linear_attention_hi(nc, act, raw, w, here):
    act.wait_ge(w["here"], here)
    act.wait_ge(w["rw_zeroed"], 1)
    for n, name in enumerate(LA_PIECES):
        nc.scalar.activation(w[name + "_hi"][:, :, :], la_raw(raw, n, w), ACT.Copy
                             ).then_inc(w["hi_done"], 1)
    act.wait_ge(w["rows_zeroed"], 1)
    for row in (0, 32):
        nc.scalar.activation(w["bias_rows"][row:row + 1, :, :], w["bias_raw"][row:row + 1, :, :], ACT.Copy
                             ).then_inc(w["hi_done"], 1)


def split_linear_attention_lo(nc, dve, raw, w, here):
    dve.wait_ge(w["here"], here)
    for n, name in enumerate(LA_PIECES):
        dve.wait_ge(w["hi_done"], n + 1)
        nc.vector.tensor_tensor(w[name + "_lo"][:, :, :], la_raw(raw, n, w), w[name + "_hi"][:, :, :].bitcast(F32), ALU.subtract
                                ).then_inc(w["lo_done"], 1)
    dve.wait_ge(w["hi_done"], len(LA_PIECES) + 2)
    nc.vector.tensor_tensor(w["bias_rows"][32:33, :, :], w["bias_raw"][32:33, :, :], w["bias_rows"][32:33, :, :].bitcast(F32),
                            ALU.subtract).then_inc(w["lo_done"], 1)


def cross_attention(nc, x, ctx_in, Wq, Wk, Wv, Wo, bo, xres, ident, next_weights, next_inputs):
    NB, NQ, D = x.shape
    _, NC, DC = ctx_in.shape
    INNER = Wq.shape[1]
    DH = 64
    SCALE = DH ** -0.5
    TB = P // NQ
    NT = NB // TB
    UT = 2
    NU = NT // UT
    UTOK = UT * P
    CB = TB * NC // P
    JT = NC // P
    HP = INNER // P
    KD = D // P
    DR = DC - P
    assert NQ == DH == DR == 64 and HP * P == BANK and CB * P == BANK

    x_tiles = x.rearrange("(t b) q d -> (b q) t d", b=TB)
    ctx_tiles = ctx_in.rearrange("(t b) (j p) d -> t p (b j) d", b=TB, p=P)

    with ExitStack() as stack:
        def sb(name, shape, dt=F32):
            return stack.enter_context(nc.sbuf_tensor(name, shape, dt))

        def sem(name):
            return stack.enter_context(nc.semaphore(name))

        raw = sb("xa_raw", [P, 8, BANK])
        wq_hi = sb("wq_hi", [P, KD, INNER], F32R)
        wq_lo = sb("wq_lo", [P, KD, INNER], F32R)
        wk_hi = sb("wk_hi", [P, 2, INNER], F32R)
        wk_lo = sb("wk_lo", [P, 2, INNER], F32R)
        wv_hi = sb("wv_hi", [P, 2, INNER], F32R)
        wv_lo = sb("wv_lo", [P, 2, INNER], F32R)
        wo_hi = sb("wo_hi", [P, HP, D], F32R)
        wo_lo = sb("wo_lo", [P, HP, D], F32R)
        bo_raw = sb("bo_raw", [P, D])
        bo_rows = sb("bo_rows", [P, D], F32R)
        ones_rows = sb("ones_rows", [P, P], F32R)

        ctx_nat = [sb(f"ctx_nat{i}", [P, CB, 2 * P]) for i in range(2)]
        ctxT_hi = sb("ctxT_hi", [P, BANK], F32R)
        ctxT_lo = sb("ctxT_lo", [P, BANK], F32R)
        ctxT_rest = sb("ctxT_rest", [P, BANK], F32R)
        kT_hi = sb("kT_hi", [P, HP, BANK], F32R)
        kT_lo = sb("kT_lo", [P, HP, BANK], F32R)
        v_nat = [sb(f"v_nat{i}", [P, CB, INNER]) for i in range(2)]
        scratch = sb("xa_scratch", [P, 1])
        stats = sb("xa_stats", [P, UT, 6])
        moments = sb("xa_moments", [P, UT, 2])
        var_eps = sb("xa_var_eps", [P, UT, 1])
        rstd = sb("xa_rstd", [P, UT, 1])
        minus_half = sb("xa_minus_half", [P, UT, 1])
        xn = sb("xa_xn", [P, UT, D])
        xnT_hi = sb("xa_xnT_hi", [P, KD, UTOK], F32R)
        xnT_lo = sb("xa_xnT_lo", [P, KD, UTOK], F32R)
        q_hi = sb("q_hi", [P, HP, UT * TB, P], F32R)
        q_lo = sb("q_lo", [P, HP, UT * TB, P], F32R)
        neg_max = sb("neg_max", [P, TB, HP])
        row_sum = sb("row_sum", [P, TB, HP])
        inv_sum = sb("inv_sum", [P, TB, HP])
        probs = sb("probs", [P, TB, HP, NC])
        probsT = sb("probsT", [P, TB * 2, BANK])
        oT_hi = sb("oT_hi", [P, HP, P], F32R)
        oT_lo = sb("oT_lo", [P, HP, P], F32R)

        score_ps = stack.enter_context(nc.psum_tensor("score_ps", [P, 4, BANK], F32))
        proj_ps = stack.enter_context(nc.psum_tensor("proj_ps", [P, 3, BANK], F32))
        turn_ps = stack.enter_context(nc.psum_tensor("turn_ps", [P, BANK], F32))

        x_here = sem("x_here")
        w_in = [sem(f"w_in_{n}") for n in ("wk", "wq", "wv", "wo")]
        ctx_here = [sem("ctx_here0"), sem("ctx_here1")]
        w_hi_done = sem("w_hi_done")
        w_lo_done = sem("w_lo_done")
        consts_done = sem("xa_consts_done")
        ident_zeroed = sem("ident_zeroed")
        ident_done = sem("ident_done")
        rows_zeroed = sem("xa_rows_zeroed")
        ctx_turned = sem("ctx_turned")
        ctxT_hi_done = sem("ctxT_hi_done")
        ctxT_done = sem("ctxT_done")
        k_full = sem("k_full")
        kT_hi_done = sem("kT_hi_done")
        kT_done = sem("kT_done")
        v_full = sem("v_full")
        v_even_done = sem("v_even_done")
        v_odd_done = sem("v_odd_done")
        stats_done = sem("xa_stats_done")
        moments_done = sem("xa_moments_done")
        var_done = sem("xa_var_done")
        rstd_done = sem("xa_rstd_done")
        xn_done = sem("xa_xn_done")
        xn_turned = sem("xa_xn_turned")
        xnT_hi_done = sem("xa_xnT_hi_done")
        xnT_done = sem("xa_xnT_done")
        q_full = sem("q_full")
        q_hi_done = sem("q_hi_done")
        q_done = sem("q_done")
        score_full = sem("score_full")
        max_done = sem("max_done")
        exp_done = sem("exp_done")
        inv_done = sem("inv_done")
        probs_done = sem("probs_done")
        pt_full = sem("pt_full")
        pt_even_done = sem("pt_even_done")
        pt_odd_done = sem("pt_odd_done")
        o_full = sem("o_full")
        oT_hi_done = sem("oT_hi_done")
        oT_done = sem("oT_done")
        out_full = sem("xa_out_full")
        x_done = sem("xa_x_done")

        NEXT_HERE = 16 * (4 + 2 + 4 + next_inputs[-1].shape[0])
        raw_flat = raw[:, :, :].rearrange("p a n -> p (a n)")
        CONSTS = 5
        CTX_BANK = [2, 0]
        KEY_BANK = [1, 2, 0, 1]
        VALUE_BANK = [2, 0, 1, 2]
        WEIGHTS = 6

        block = stack.enter_context(nc.Block())

        def load_split_rows(queue, n, w):
            queue.dma_start(raw[:, 2 * n, :], w[0:P, :]).then_inc(w_in[n], 16)
            for half in range(2):
                queue.dma_start(raw[half * DR:(half + 1) * DR, 2 * n + 1, :], w[P:DC, :]).then_inc(w_in[n], 16)

        @block.sync
        def _(sp):
            def load_ctx(t, buf):
                src = ctx_tiles[bass.ds(t, 1), :, :, :].rearrange("a p m d -> p (a m) d")
                sp.dma_start(ctx_nat[buf][:, :, 0:DC], src).then_inc(ctx_here[buf], 16)
                sp.dma_start(ctx_nat[buf][:, :, DC:2 * P], src[:, :, P:DC]).then_inc(ctx_here[buf], 16)

            def load_x(u):
                sp.dma_start(xres[:, bass.ds(UT * u, UT), :], x_tiles[:, bass.ds(UT * u, UT), :]).then_inc(x_here, 16)

            load_x(0)
            load_ctx(0, 0)
            load_split_rows(sp, 0, Wk)
            sp.dma_start(raw[:, 2:4, :], Wq.rearrange("(k p) n -> p k n", p=P)).then_inc(w_in[1], 16)
            load_ctx(1, 1)
            sp.wait_ge(x_here, 16)
            load_x(1)
            def loads(u):
                for a in range(2):
                    sp.wait_ge(ctxT_done, 4 * u + 2 * a - 2)
                    load_ctx(UT * u + a, a)

            def unit(u):
                loads(u)
                sp.wait_ge(x_here, 16 * u + 16)
                load_x(u + 1)

            parts = linear_attention_loads(sp, raw_flat, next_weights, *next_inputs)
            for n, part in enumerate(parts):
                unit(n + 1)
                sp.wait_ge(w_hi_done, WEIGHTS)
                sp.wait_ge(w_lo_done, WEIGHTS - 1)
                part()
            with sp.Fori(len(parts) + 1, NU - 1) as u:
                unit(u)
            loads(NU - 1)

        @block.gpsimd
        def _(pool):
            nc.gpsimd.memset(ident[:, :], 0.0).then_inc(ident_zeroed, 1)
            pool.wait_ge(ident_zeroed, 1)
            nc.gpsimd.affine_select(out=ident[:, :], in_=ident[:, :], compare_op=ALU.not_equal, fill=1.0,
                                    base=0, pattern=[[-1, P]], channel_multiplier=1).then_inc(ident_done, 1)
            pool.wait_ge(ident_done, 1)

            def rstd_of(u):
                pool.wait_ge(var_done, u + 1)
                nc.gpsimd.tensor_tensor(rstd[:, :, :], var_eps[:, :, :], minus_half[:, :, :], ALU.pow
                                        ).then_inc(rstd_done, 1)

            def normalise(t):
                for b in range(TB):
                    pool.wait_ge(inv_done, TB * t + b + 1)
                    nc.gpsimd.tensor_tensor(probs[:, b, :, :], probs[:, b, :, :],
                                            inv_sum[:, b, :].unsqueeze(2).to_broadcast([P, HP, NC]), ALU.mult
                                            ).then_inc(probs_done, 1)

            pool.wait_ge(consts_done, CONSTS)
            rstd_of(0)
            with pool.Fori(0, NU - 1) as u:
                normalise(UT * u)
                rstd_of(u + 1)
                normalise(UT * u + 1)
            for a in range(UT):
                normalise(UT * (NU - 1) + a)

        weight_views = [(hi[:, :, :], lo[:, :, :], raw[:, 2 * n:2 * n + 2, :], loads) for n, (hi, lo, loads) in
                        enumerate(((wk_hi, wk_lo, 3), (wq_hi, wq_lo, 1), (wv_hi, wv_lo, 3)))]
        weight_views.append((wo_hi[:, :, :], wo_lo[:, :, :], raw[:, 6:8, :].rearrange("p a (b n) -> p (a b) n", b=2), 3))

        @block.scalar
        def _(act):
            def ctxT_of(t):
                act.wait_ge(ctx_turned, 2 * t + 1)
                nc.scalar.activation(ctxT_hi[:, :], proj_ps[:, CTX_BANK[0], :], ACT.Copy).then_inc(ctxT_hi_done, 1)
                act.wait_ge(ctx_turned, 2 * t + 2)
                nc.scalar.activation(ctxT_rest[:, :], proj_ps[:, CTX_BANK[1], :], ACT.Copy).then_inc(ctxT_hi_done, 1)

            def kT_of(t, hp):
                act.wait_ge(k_full, HP * t + hp + 1)
                nc.scalar.activation(kT_hi[:, hp, :], proj_ps[:, KEY_BANK[hp], :], ACT.Copy).then_inc(kT_hi_done, 1)

            def v_of(t, buf, m):
                act.wait_ge(v_full, CB * t + m + 1)
                nc.scalar.activation(v_nat[buf][:, m, :], proj_ps[:, VALUE_BANK[m], :], ACT.Copy).then_inc(v_even_done, 1)

            def xnT_of(u):
                act.wait_ge(xn_turned, u + 1)
                nc.scalar.activation(xnT_hi[:, :, :].rearrange("p k n -> p (k n)"), turn_ps[:, :], ACT.Copy
                                     ).then_inc(xnT_hi_done, 1)

            def q_of(u, g):
                act.wait_ge(q_full, 2 * u + g + 1)
                src = turn_ps[:, :].rearrange("p (c i) -> p c i", i=NQ)
                for h in range(2):
                    rows = slice(h * DH, (h + 1) * DH)
                    dst = q_hi[rows, 2 * g:2 * g + 2, :, h * NQ:(h + 1) * NQ].rearrange("p a c i -> p (a c) i")
                    nc.scalar.activation(dst, src[rows], ACT.Copy, scale=SCALE).then_inc(q_hi_done, 1)

            def exp_of(t, b, hp):
                act.wait_ge(max_done, 4 * t + 2 * b + hp // 2 + 1)
                nc.scalar.activation(probs[:, b, hp, :], score_ps[:, 2 * b + hp // 2, (hp % 2) * NC:(hp % 2 + 1) * NC],
                                     ACT.Exp, bias=neg_max[:, b, hp:hp + 1], accum_out=row_sum[:, b, hp:hp + 1]
                                     ).then_inc(exp_done, 1)

            def probsT_of(t, g):
                act.wait_ge(pt_full, 4 * t + g + 1)
                nc.scalar.activation(probsT[:, g, :], turn_ps[:, :], ACT.Copy).then_inc(pt_even_done, 1)

            def oT_of(t):
                for b in range(TB):
                    act.wait_ge(o_full, TB * t + b + 1)
                    for h in range(2):
                        rows = slice(h * DH, (h + 1) * DH)
                        src = score_ps[rows, b, :].rearrange("p (a n) -> p a n", n=P)[:, :, h * NQ:(h + 1) * NQ]
                        nc.scalar.activation(oT_hi[rows, :, b * NQ:(b + 1) * NQ], src, ACT.Copy).then_inc(oT_hi_done, 1)

            def weight_hi(n):
                hi, _, src, loads = weight_views[n]
                act.wait_ge(w_in[n], 16 * loads)
                nc.scalar.activation(hi, src, ACT.Copy).then_inc(w_hi_done, 1)

            load_split_rows(act, 2, Wv)
            act.dma_start(weight_views[3][2], Wo.rearrange("(k p) n -> p k n", p=P)).then_inc(w_in[3], 16)
            for row in (0, 32):
                act.dma_start(bo_raw[row:row + 1, :], bo.rearrange("(a n) -> a n", a=1)).then_inc(w_in[3], 16)
            ctxT_of(0)
            xnT_of(0)
            weight_hi(0)
            weight_hi(1)
            kT_of(0, 0)
            kT_of(0, 1)
            weight_hi(2)
            q_of(0, 0)
            kT_of(0, 2)
            weight_hi(3)
            kT_of(0, 3)
            q_of(0, 1)
            act.wait_ge(consts_done, CONSTS)
            act.wait_ge(rows_zeroed, 2)
            for row in (0, 32):
                nc.scalar.activation(bo_rows[row:row + 1, :], bo_raw[row:row + 1, :], ACT.Copy).then_inc(w_hi_done, 1)
            v_of(0, 0, 0)
            v_of(0, 0, 2)

            def tile(u, a, last):
                t = UT * u + a
                nxt = (a + 1) % 2
                more = not (last and a == 1)
                if more:
                    ctxT_of(t + 1)
                for hp in range(HP):
                    if not last and a == 1 and hp == 2:
                        xnT_of(u + 1)
                    exp_of(t, 0, hp)
                if more:
                    kT_of(t + 1, 0)
                if not last and a == 1:
                    q_of(u + 1, 0)
                exp_of(t, 1, 0)
                if more:
                    kT_of(t + 1, 1)
                exp_of(t, 1, 1)
                if more:
                    kT_of(t + 1, 2)
                if not last and a == 1:
                    q_of(u + 1, 1)
                exp_of(t, 1, 2)
                exp_of(t, 1, 3)
                if more:
                    kT_of(t + 1, 3)
                    v_of(t + 1, nxt, 0)
                probsT_of(t, 0)
                if more:
                    v_of(t + 1, nxt, 2)
                probsT_of(t, 2)
                oT_of(t)

            tile(0, 0, False)
            tile(0, 1, False)
            with act.Fori(1, NU - 1) as u:
                tile(u, 0, False)
                tile(u, 1, False)
            split_linear_attention_hi(nc, act, raw_flat, next_weights, NEXT_HERE)
            tile(NU - 1, 0, True)
            tile(NU - 1, 1, True)

        @block.vector
        def _(dve):
            def moments_of(u):
                for a in range(UT):
                    dve.wait_ge(x_here, 16 * u + 16)
                    nc.vector.bn_stats(stats[:, a, :], slot(xres, UT * u + a)).then_inc(stats_done, 1)
                settle(nc, stats_done, UT * u + UT, scratch[:, :])
                for a in range(UT):
                    nc.vector.bn_aggr(moments[:, a, :], stats[:, a, :]).then_inc(moments_done, 1)
                dve.wait_ge(moments_done, UT * u + UT)
                nc.vector.tensor_scalar(var_eps[:, :, :], moments[:, :, 1:2], LN_EPS, None, ALU.add).then_inc(var_done, 1)

            def xn_of(u):
                dve.wait_ge(rstd_done, u + 1)
                for a in range(UT):
                    nc.vector.tensor_scalar(xn[:, a:a + 1, :], slot(xres, UT * u + a), moments[:, a, 0:1], rstd[:, a, :],
                                            ALU.subtract, ALU.mult).then_inc(xn_done, 1)

            def ctxT_of(t):
                dve.wait_ge(ctxT_hi_done, 2 * t + 1)
                nc.vector.tensor_tensor(ctxT_lo[:, :], proj_ps[:, CTX_BANK[0], :], ctxT_hi[:, :].bitcast(F32), ALU.subtract
                                        ).then_inc(ctxT_done, 1)
                dve.wait_ge(ctxT_hi_done, 2 * t + 2)
                nc.vector.tensor_tensor(ctxT_rest[DR:P, :], proj_ps[DR:P, CTX_BANK[1], :], ctxT_rest[DR:P, :].bitcast(F32),
                                        ALU.subtract).then_inc(ctxT_done, 1)

            def kT_of(t, hp):
                dve.wait_ge(kT_hi_done, HP * t + hp + 1)
                nc.vector.tensor_tensor(kT_lo[:, hp, :], proj_ps[:, KEY_BANK[hp], :], kT_hi[:, hp, :].bitcast(F32),
                                        ALU.subtract).then_inc(kT_done, 1)

            def v_of(t, buf, m):
                dve.wait_ge(v_full, CB * t + m + 1)
                nc.vector.tensor_copy(v_nat[buf][:, m, :], proj_ps[:, VALUE_BANK[m], :]).then_inc(v_odd_done, 1)

            def xnT_of(u):
                dve.wait_ge(xnT_hi_done, u + 1)
                nc.vector.tensor_tensor(xnT_lo[:, :, :].rearrange("p k n -> p (k n)"), turn_ps[:, :],
                                        xnT_hi[:, :, :].rearrange("p k n -> p (k n)").bitcast(F32), ALU.subtract
                                        ).then_inc(xnT_done, 1)

            def q_of(u, g):
                src = turn_ps[:, :].rearrange("p (c i) -> p c i", i=NQ)
                for h in range(2):
                    rows = slice(h * DH, (h + 1) * DH)
                    part = [q[rows, 2 * g:2 * g + 2, :, h * NQ:(h + 1) * NQ].rearrange("p a c i -> p (a c) i")
                            for q in (q_hi, q_lo)]
                    dve.wait_ge(q_hi_done, 4 * u + 2 * g + h + 1)
                    nc.vector.scalar_tensor_tensor(out=part[1], in0=src[rows], scalar=SCALE, in1=part[0].bitcast(F32),
                                                   op0=ALU.mult, op1=ALU.subtract).then_inc(q_done, 1)

            def max_of(t, n):
                dve.wait_ge(score_full, 4 * t + n + 1)
                nc.vector.tensor_reduce(neg_max[:, n // 2, 2 * (n % 2):2 * (n % 2) + 2],
                                        score_ps[:, n, :].rearrange("p (h j) -> p h j", j=NC), AX.X, ALU.max,
                                        negate=True).then_inc(max_done, 1)

            def inverse_of(t, b):
                dve.wait_ge(exp_done, TB * HP * t + HP * (b + 1))
                nc.vector.reciprocal(inv_sum[:, b, :], row_sum[:, b, :]).then_inc(inv_done, 1)

            def probsT_of(t, g):
                dve.wait_ge(pt_full, 4 * t + g + 1)
                nc.vector.tensor_copy(probsT[:, g, :], turn_ps[:, :]).then_inc(pt_odd_done, 1)

            def oT_of(t):
                for b in range(TB):
                    for h in range(2):
                        rows = slice(h * DH, (h + 1) * DH)
                        cols = slice(b * NQ, (b + 1) * NQ)
                        src = score_ps[rows, b, :].rearrange("p (a n) -> p a n", n=P)[:, :, h * NQ:(h + 1) * NQ]
                        dve.wait_ge(oT_hi_done, 2 * TB * t + 2 * b + h + 1)
                        nc.vector.tensor_tensor(oT_lo[rows, :, cols], src, oT_hi[rows, :, cols].bitcast(F32),
                                                ALU.subtract).then_inc(oT_done, 1)

            def x_of(t):
                dve.wait_ge(out_full, t + 1)
                dst = slot(xres, t)
                nc.vector.tensor_tensor(dst, turn_ps[:, 0:D].unsqueeze(1), dst, ALU.add).then_inc(x_done, 1)

            nc.vector.memset(minus_half[:, :, :], -0.5).then_inc(consts_done, 1)
            for rows in (ones_rows, bo_rows):
                nc.vector.memset(rows[:, :].bitcast(F32), 0.0).then_inc(rows_zeroed, 1)
            for q in (q_hi, q_lo):
                nc.vector.memset(q[:, :, :, :].bitcast(F32), 0.0).then_inc(consts_done, 1)
            dve.wait_ge(rows_zeroed, 2)
            for row in (0, 32):
                nc.vector.memset(ones_rows[row:row + 1, :].bitcast(F32), 1.0).then_inc(consts_done, 1)
            moments_of(0)
            xn_of(0)
            def weight_lo(n):
                hi, lo, src, loads = weight_views[n]
                dve.wait_ge(w_in[n], 16 * loads)
                dve.wait_ge(w_hi_done, n + 1)
                nc.vector.tensor_tensor(lo, src, hi.bitcast(F32), ALU.subtract).then_inc(w_lo_done, 1)

            ctxT_of(0)
            xnT_of(0)
            weight_lo(0)
            weight_lo(1)
            kT_of(0, 0)
            kT_of(0, 1)
            weight_lo(2)
            q_of(0, 0)
            kT_of(0, 2)
            weight_lo(3)
            kT_of(0, 3)
            q_of(0, 1)
            dve.wait_ge(w_hi_done, WEIGHTS)
            nc.vector.tensor_tensor(bo_rows[32:33, :], bo_raw[32:33, :], bo_rows[32:33, :].bitcast(F32), ALU.subtract
                                    ).then_inc(w_lo_done, 1)
            v_of(0, 0, 1)
            v_of(0, 0, 3)

            def tile(u, a, last):
                t = UT * u + a
                nxt = (a + 1) % 2
                more = not (last and a == 1)
                if more:
                    ctxT_of(t + 1)
                max_of(t, 0)
                if not (isinstance(t, int) and t == 0):
                    x_of(t - 1)
                max_of(t, 1)
                max_of(t, 2)
                if not last and a == 1:
                    xnT_of(u + 1)
                max_of(t, 3)
                if more:
                    kT_of(t + 1, 0)
                if not last and a == 1:
                    q_of(u + 1, 0)
                inverse_of(t, 0)
                if more:
                    kT_of(t + 1, 1)
                    kT_of(t + 1, 2)
                if not last and a == 1:
                    q_of(u + 1, 1)
                inverse_of(t, 1)
                if more:
                    kT_of(t + 1, 3)
                if more:
                    v_of(t + 1, nxt, 1)
                probsT_of(t, 1)
                if not last and a == 0:
                    moments_of(u + 1)
                if more:
                    v_of(t + 1, nxt, 3)
                probsT_of(t, 3)
                if not last and a == 0:
                    xn_of(u + 1)
                oT_of(t)

            tile(0, 0, False)
            zero_linear_attention(nc, raw_flat, next_weights)
            tile(0, 1, False)
            with dve.Fori(1, NU - 1) as u:
                tile(u, 0, False)
                tile(u, 1, False)
            split_linear_attention_lo(nc, dve, raw_flat, next_weights, NEXT_HERE)
            tile(NU - 1, 0, True)
            tile(NU - 1, 1, True)
            x_of(NT - 1)

        @block.tensor
        def _(pe):
            def products(out, pairs):
                for n, (w, m) in enumerate(pairs):
                    ins = nc.tensor.matmul(out, w, m, start=n == 0, stop=n == len(pairs) - 1)
                return ins

            def turn_ctx(u, buf):
                t = UT * u + buf
                pe.wait_ge(ctx_here[buf], 32 * u + 32)
                after(pe, v_odd_done, 2 * t)
                for m in range(CB):
                    ins = nc.tensor.transpose(proj_ps[:, CTX_BANK[0], m * P:(m + 1) * P], ctx_nat[buf][:, m, 0:P], ident[:, :])
                ins.then_inc(ctx_turned, 1)
                for m in range(CB):
                    ins = nc.tensor.transpose(proj_ps[:, CTX_BANK[1], m * P:(m + 1) * P], ctx_nat[buf][:, m, P:2 * P], ident[:, :])
                ins.then_inc(ctx_turned, 1)

            def context_pairs(hi, lo, moving_context, cols):
                pairs = [(ctxT_hi, hi[:, 0, :]), (ctxT_lo, hi[:, 0, :]), (ctxT_hi, lo[:, 0, :]),
                         (ctxT_rest, hi[:, 1, :]), (ctxT_rest, lo[:, 1, :])]
                return [(w[:, cols], c[:, :]) if moving_context else (c[:, cols], w) for c, w in pairs]

            def keys(t, hp):
                if hp == 0:
                    pe.wait_ge(ctxT_done, 2 * t + 2)
                if hp == 0:
                    after(pe, v_even_done, 2 * t)
                elif hp == 3:
                    pe.wait_ge(kT_done, HP * t + 1)
                products(proj_ps[:, KEY_BANK[hp], :], context_pairs(wk_hi, wk_lo, True, slice(hp * P, (hp + 1) * P))
                         ).then_inc(k_full, 1)

            def values(t, m):
                if m < 3:
                    pe.wait_ge(kT_done, HP * t + m + 2)
                else:
                    pe.wait_ge(v_even_done, 2 * t + 1)
                products(proj_ps[:, VALUE_BANK[m], :], context_pairs(wv_hi, wv_lo, False, slice(m * P, (m + 1) * P))
                         ).then_inc(v_full, 1)

            def turn_xn(u):
                pe.wait_ge(xn_done, UT * u + UT)
                after(pe, x_done, UT * u - 1)
                for k in range(KD):
                    for a in range(UT):
                        c = k * UTOK + a * P
                        ins = nc.tensor.transpose(turn_ps[:, c:c + P], xn[:, a, k * P:(k + 1) * P], ident[:, :])
                ins.then_inc(xn_turned, 1)

            def queries(u, g):
                if g == 0:
                    pe.wait_ge(xnT_done, u + 1)
                else:
                    pe.wait_ge(q_done, 4 * u + 2)
                for i in range(2):
                    cols = slice((2 * g + i) * P, (2 * g + i + 1) * P)
                    ins = products(turn_ps[:, i * UTOK:(i + 1) * UTOK],
                                   [(w[:, k, cols], m[:, k, :]) for k in range(KD)
                                    for w, m in ((wq_hi, xnT_hi), (wq_hi, xnT_lo), (wq_lo, xnT_hi))])
                ins.then_inc(q_full, 1)

            def scores(u, a, n):
                t, b = UT * u + a, n // 2
                if n == 0:
                    pe.wait_ge(q_done, 4 * u + 4)
                    pe.wait_ge(kT_done, HP * t + HP)
                if n < TB:
                    after(pe, oT_done, 2 * TB * (t - 1) + 2 * n + 2)
                for i in range(2):
                    hp = 2 * (n % 2) + i
                    ins = products(score_ps[:, n, i * NC:(i + 1) * NC],
                                   [(q[:, hp, TB * a + b, :], k[:, hp, b * NC:(b + 1) * NC])
                                    for q, k in ((q_hi, kT_hi), (q_lo, kT_hi), (q_hi, kT_lo))])
                ins.then_inc(score_full, 1)

            def turn_probs(t, g):
                b = g // 2
                if g % 2 == 0:
                    pe.wait_ge(probs_done, TB * t + b + 1)
                if g == 0:
                    after(pe, x_done, t)
                else:
                    pe.wait_ge(pt_even_done if g % 2 else pt_odd_done, 2 * t + (g + 1) // 2)
                for i in range(2):
                    for j in range(JT):
                        c = (2 * i + j) * P
                        ins = nc.tensor.transpose(turn_ps[:, c:c + P],
                                                  probs[:, b, 2 * (g % 2) + i, j * P:(j + 1) * P], ident[:, :])
                ins.then_inc(pt_full, 1)

            def mix_values(t, buf):
                pe.wait_ge(v_even_done, 2 * t + 2)
                pe.wait_ge(v_odd_done, 2 * t + 2)
                for b in range(TB):
                    pe.wait_ge(pt_even_done, 2 * t + b + 1)
                    pe.wait_ge(pt_odd_done, 2 * t + b + 1)
                    for hp in range(HP):
                        ins = products(score_ps[:, b, hp * P:(hp + 1) * P],
                                       [(v_nat[buf][:, JT * b + j, hp * P:(hp + 1) * P],
                                         probsT[:, 2 * b + hp // 2, (2 * (hp % 2) + j) * P:(2 * (hp % 2) + j + 1) * P])
                                        for j in range(JT)])
                    ins.then_inc(o_full, 1)

            def project_out(t):
                pe.wait_ge(oT_done, 2 * TB * t + 2 * TB)
                products(turn_ps[:, 0:D],
                         [(ones_rows[:, :], bo_rows[:, :])] +
                         [(o[:, hp, :], w[:, hp, :]) for hp in range(HP)
                          for o, w in ((oT_hi, wo_hi), (oT_lo, wo_hi), (oT_hi, wo_lo))]).then_inc(out_full, 1)

            pe.wait_ge(ident_done, 1)
            pe.wait_ge(consts_done, CONSTS)
            turn_ctx(0, 0)
            turn_xn(0)
            pe.wait_ge(w_lo_done, 1)
            keys(0, 0)
            keys(0, 1)
            pe.wait_ge(w_lo_done, 2)
            queries(0, 0)
            keys(0, 2)
            keys(0, 3)
            queries(0, 1)
            pe.wait_ge(w_lo_done, 3)
            for m in range(CB):
                values(0, m)

            pe.wait_ge(w_lo_done, WEIGHTS - 1)

            def tile(u, a, last):
                t = UT * u + a
                more = not (last and a == 1)
                if more:
                    turn_ctx(u + (a + 1) // 2, (a + 1) % 2)
                scores(u, a, 0)
                if not (isinstance(t, int) and t == 0):
                    project_out(t - 1)
                scores(u, a, 1)
                scores(u, a, 2)
                if not last and a == 1:
                    turn_xn(u + 1)
                scores(u, a, 3)
                if more:
                    keys(t + 1, 0)
                if not last and a == 1:
                    queries(u + 1, 0)
                if more:
                    keys(t + 1, 1)
                    keys(t + 1, 2)
                if not last and a == 1:
                    queries(u + 1, 1)
                if more:
                    keys(t + 1, 3)
                for g in range(4):
                    if more:
                        values(t + 1, g)
                    if g == 0 and not last and a == 1:
                        pe.wait_ge(q_done, 4 * u + 8)
                    turn_probs(t, g)
                mix_values(t, a)

            tile(0, 0, False)
            tile(0, 1, False)
            with pe.Fori(1, NU - 1) as u:
                tile(u, 0, False)
                tile(u, 1, False)
            tile(NU - 1, 0, True)
            tile(NU - 1, 1, True)
            project_out(NT - 1)


MOE_LANE = 32


def mixture_weights(nc, stack, raw_stack, E, D, H):
    KD, KH = D // P, H // P
    w = {}

    def sb(name, shape, dt=F32, until=stack):
        w[name] = until.enter_context(nc.sbuf_tensor("moe_" + name, shape, dt))

    for part in ("hi", "lo"):
        sb("win_" + part, [P, E, KD, H], F32R)
        sb("wout_" + part, [P, E, KH, D], F32R)
    sb("raw_router", [P, KD, E])
    sb("router", [P, KD, 2 * E], F32R)
    sb("b_in_cols", [P, E, KH])
    sb("b_out_raw", [P, D])
    sb("b_out_rows", [P, D], F32R)
    sb("raw_in", [P, E, KD, H], until=raw_stack)
    sb("raw_out", [P, E, KH, D], until=raw_stack)
    for name in ("here", "zeroed", "hi_done", "lo_done", "small_hi_done", "small_lo_done"):
        w[name] = stack.enter_context(nc.semaphore("moe_w_" + name))
    w["HERE"] = 16 * (3 * E + KD + 3)
    return w


def load_mixture(sp, w, router_w, w_in, b_in, w_out, b_out):
    E, KD = w_in.shape[0], w_in.shape[1] // P
    for e in range(E):
        sp.dma_start(w["raw_in"][:, e, :, :], w_in[e].rearrange("(k p) n -> p k n", p=P)).then_inc(w["here"], 16)
        sp.dma_start(w["raw_out"][:, e, :, :], w_out[e].rearrange("(k p) n -> p k n", p=P)).then_inc(w["here"], 16)
        sp.dma_start(w["b_in_cols"][:, e, :], b_in[e].rearrange("(k p) -> p k", p=P),
                     allow_slow_non_contiguous=True).then_inc(w["here"], 16)
    for k in range(KD):
        sp.dma_start(w["raw_router"][:, k, :], router_w[k * P:(k + 1) * P, :]).then_inc(w["here"], 16)
    sp.wait_ge(w["zeroed"], 1)
    for n in range(3):
        sp.dma_start(w["b_out_raw"][n * MOE_LANE:n * MOE_LANE + E, :], b_out).then_inc(w["here"], 16)


def split_expert_hi(nc, act, w, e):
    act.wait_ge(w["here"], w["HERE"])
    for part, raw in (("win_hi", "raw_in"), ("wout_hi", "raw_out")):
        nc.scalar.activation(w[part][:, bass.ds(e, 1), :, :].rearrange("p e k n -> p (e k n)"),
                             w[raw][:, bass.ds(e, 1), :, :].rearrange("p e k n -> p (e k n)"), ACT.Copy
                             ).then_inc(w["hi_done"], 1)


def split_expert_lo(nc, pool, w, e):
    for n, (hi, lo, raw) in enumerate((("win_hi", "win_lo", "raw_in"), ("wout_hi", "wout_lo", "raw_out"))):
        pool.wait_ge(w["hi_done"], 2 * e + n + 1)
        views = [w[name][:, bass.ds(e, 1), :, :].rearrange("p e k n -> p (e k n)") for name in (lo, raw, hi)]
        nc.gpsimd.tensor_tensor(views[0], views[1], views[2].bitcast(F32), ALU.subtract).then_inc(w["lo_done"], 1)


def split_small_hi(nc, act, w):
    E = w["raw_router"].shape[2]
    act.wait_ge(w["here"], w["HERE"])
    nc.scalar.activation(w["router"][:, :, 0:E], w["raw_router"][:, :, :], ACT.Copy).then_inc(w["small_hi_done"], 1)
    act.wait_ge(w["zeroed"], 1)
    nc.scalar.activation(w["b_out_rows"][:, :], w["b_out_raw"][:, :], ACT.Copy).then_inc(w["small_hi_done"], 1)


def split_small_lo(nc, dve, w):
    E = w["raw_router"].shape[2]
    dve.wait_ge(w["small_hi_done"], 2)
    nc.vector.tensor_tensor(w["router"][:, :, E:2 * E], w["raw_router"][:, :, :], w["router"][:, :, 0:E].bitcast(F32),
                            ALU.subtract).then_inc(w["small_lo_done"], 1)
    rows = slice(2 * MOE_LANE, 3 * MOE_LANE)
    nc.vector.tensor_tensor(w["b_out_rows"][rows, :], w["b_out_raw"][rows, :], w["b_out_rows"][rows, :].bitcast(F32),
                            ALU.subtract).then_inc(w["small_lo_done"], 1)


def linear_attention(nc, weights, D, H, DK, F, xres, ident, next_weights, next_inputs):
    NT = xres.shape[1]
    UT = 2
    NU = NT // UT
    UTOK = UT * P
    TB = 2
    ROWS = P // TB
    KD = D // P
    HP = H // 2
    GP = HP // KD
    DV = DK + 1
    PAIR = TB * 2 * DV
    assert GP * P == BANK and 2 * F == P and KD * UTOK == BANK

    with ExitStack() as stack:
        def sb(name, shape, dt=F32):
            return stack.enter_context(nc.sbuf_tensor("la_" + name, shape, dt))

        def sem(name):
            return stack.enter_context(nc.semaphore("la_" + name))

        split = {n: (weights[n + "_hi"], weights[n + "_lo"]) for n in ("wq", "wk", "wv", "wo")}
        rw_hi, rw_lo = weights["rw_hi"], weights["rw_lo"]
        bias_cols, bias_rows = weights["bias_cols"], weights["bias_rows"]
        ones_rows = sb("ones_rows", [P, P], F32R)

        scratch = sb("scratch", [P, 1])
        stats = sb("stats", [P, UT, 6])
        moments = sb("moments", [P, UT, 2])
        var_eps = sb("var_eps", [P, UT, 1])
        rstd = sb("rstd", [P, UT, 1])
        minus_half = sb("minus_half", [P, UT, 1])
        xn = sb("xn", [P, UT, D])
        xnT_hi = sb("xnT_hi", [P, KD, UTOK], F32R)
        xnT_lo = sb("xnT_lo", [P, KD, UTOK], F32R)
        qk_hi = [sb(f"{n}_hi", [P, KD, UTOK], F32R) for n in "qk"]
        qk_lo = [sb(f"{n}_lo", [P, KD, UTOK], F32R) for n in "qk"]
        v_ones = sb("v_ones", [P, UT, HP, TB, 2, DV])
        k_feat = sb("k_feat", [P, UT, KD, BANK])
        q_feat = sb("q_feat", [P, HP, UTOK])
        kv = sb("kv", [P, UT, HP, TB, 2, DV])
        den = sb("den", [P, UT, H])
        inv_den = sb("inv_den", [P, UT, H])
        o_nat = sb("o_nat", [P, UT, D])
        oT_hi = sb("oT_hi", [P, UT, KD, P], F32R)
        oT_lo = sb("oT_lo", [P, UT, KD, P], F32R)

        turn_ps = stack.enter_context(nc.psum_tensor("la_turn_ps", [P, BANK], F32))
        q_ps = stack.enter_context(nc.psum_tensor("la_q_ps", [P, BANK], F32))
        k_ps = stack.enter_context(nc.psum_tensor("la_k_ps", [P, BANK], F32))
        feat_ps = stack.enter_context(nc.psum_tensor("la_feat_ps", [P, 2, BANK], F32))
        sum_ps = stack.enter_context(nc.psum_tensor("la_sum_ps", [P, 2, BANK], F32))
        ends_ps = stack.enter_context(nc.psum_tensor("la_ends_ps", [P, BANK], F32))

        consts_done = sem("consts_done")
        exponent_done = sem("exponent_done")
        stats_done = sem("stats_done")
        moments_done = sem("moments_done")
        var_done = sem("var_done")
        rstd_done = sem("rstd_done")
        xn_done = sem("xn_done")
        xn_turned = sem("xn_turned")
        xnT_hi_done = sem("xnT_hi_done")
        xnT_done = sem("xnT_done")
        qk_full = [sem("q_full"), sem("k_full")]
        qk_hi_done = [sem("q_hi_done"), sem("k_hi_done")]
        qk_done = [sem("q_done"), sem("k_done")]
        v_full = sem("v_full")
        v_done = sem("v_done")
        feat_full = sem("feat_full")
        feat_done = sem("feat_done")
        kv_full = sem("kv_full")
        kv_done = sem("kv_done")
        num_full = sem("num_full")
        den_done = sem("den_done")
        inv_done = sem("inv_done")
        o_done = sem("o_done")
        o_turned = sem("o_turned")
        oT_hi_done = sem("oT_hi_done")
        oT_done = sem("oT_done")
        out_full = sem("out_full")
        x_done = sem("x_done")

        CONSTS = 3 + 2 + UT * TB
        FEATS = 2 * UT + HP // 2
        block = stack.enter_context(nc.Block())

        E = next_inputs[1].shape[0]
        assert E + 1 < NU - 1

        @block.sync
        def _(sp):
            load_mixture(sp, next_weights, *next_inputs)

        @block.gpsimd
        def _(pool):
            def rstd_of(u):
                pool.wait_ge(var_done, u + 1)
                nc.gpsimd.tensor_tensor(rstd[:, :, :], var_eps[:, :, :], minus_half[:, :, :], ALU.pow
                                        ).then_inc(rstd_done, 1)

            pool.wait_ge(exponent_done, 1)
            rstd_of(0)
            pool.wait_ge(rstd_done, 1)
            fills = [(ones_rows[:, :].bitcast(F32), 0.0),
                     (v_ones[:, :, :, :, :, :].rearrange("p a c b h d -> p (a c b h d)"), 0.0),
                     (kv[:, :, :, :, :, :].rearrange("p a c b h d -> p (a c b h d)"), 0.0)]
            fills += [(ones_rows[row:row + 1, :].bitcast(F32), 1.0) for row in (0, 32)]
            fills += [(v_ones[b * ROWS:(b + 1) * ROWS, a, :, b, :, DK:DV], 1.0) for a in range(UT) for b in range(TB)]
            for n, (dst, value) in enumerate(fills):
                after(pool, consts_done, n)
                nc.gpsimd.memset(dst, value).then_inc(consts_done, 1)
            pool.wait_ge(consts_done, CONSTS)
            rstd_of(1)
            with pool.Fori(2, E + 2) as u:
                rstd_of(u)
                split_expert_lo(nc, pool, next_weights, u - 2)
            pool.wait_ge(next_weights["lo_done"], 2 * E)
            with pool.Fori(E + 2, NU) as u:
                rstd_of(u)

        @block.scalar
        def _(act):
            def xnT_of(u):
                act.wait_ge(xn_turned, u + 1)
                nc.scalar.activation(xnT_hi[:, :, :].rearrange("p k n -> p (k n)"), turn_ps[:, :], ACT.Copy
                                     ).then_inc(xnT_hi_done, 1)

            def qk_of(u, i):
                act.wait_ge(qk_full[i], u + 1)
                for k in range(KD):
                    src = (q_ps, k_ps)[i][:, k * UTOK:(k + 1) * UTOK]
                    nc.scalar.activation(qk_hi[i][:, k, :], src, ACT.Identity, bias=bias_cols[:, i, k:k + 1]
                                         ).then_inc(qk_hi_done[i], 1)

            def v_of(u):
                act.wait_ge(v_full, u + 1)
                for a in range(UT):
                    for b in range(TB):
                        rows = slice(b * ROWS, (b + 1) * ROWS)
                        src = ends_ps[rows, a * D:(a + 1) * D].rearrange("p (c h d) -> p c h d", h=2, d=DK)
                        nc.scalar.activation(v_ones[rows, a, :, b, :, 0:DK], src, ACT.Copy).then_inc(v_done, 1)

            def kv_of(t, a):
                act.wait_ge(kv_full, t + 1)
                for h in range(2):
                    rows = slice(h * F, (h + 1) * F)
                    src = sum_ps[rows, :, 0:GP * PAIR].rearrange("p g (c n) -> p g c n", n=2 * DV)[:, :, :, h * DV:(h + 1) * DV]
                    dst = kv[rows, a, :, :, h, :].rearrange("p (g c) b d -> p g (c b) d", g=2)
                    nc.scalar.activation(dst, src, ACT.Copy).then_inc(kv_done, 1)

            def oT_of(t, a):
                act.wait_ge(o_turned, t + 1)
                nc.scalar.activation(oT_hi[:, a, :, :].rearrange("p k n -> p (k n)"), (turn_ps, q_ps)[a][:, 0:D],
                                     ACT.Copy).then_inc(oT_hi_done, 1)

            xnT_of(0)
            qk_of(0, 0)
            qk_of(0, 1)
            act.wait_ge(consts_done, CONSTS)
            v_of(0)

            def unit(u, first, last):
                if not first:
                    oT_of(UT * u - 1, 1)
                kv_of(UT * u, 0)
                if not last:
                    xnT_of(u + 1)
                kv_of(UT * u + 1, 1)
                if not last:
                    qk_of(u + 1, 0)
                    qk_of(u + 1, 1)
                oT_of(UT * u, 0)
                if not last:
                    v_of(u + 1)

            unit(0, True, False)
            with act.Fori(1, E + 1) as u:
                unit(u, False, False)
                split_expert_hi(nc, act, next_weights, u - 1)
            split_small_hi(nc, act, next_weights)
            with act.Fori(E + 1, NU - 1) as u:
                unit(u, False, False)
            unit(NU - 1, False, True)
            oT_of(UT * NU - 1, 1)

        @block.vector
        def _(dve):
            def moments_of(u):
                for a in range(UT):
                    nc.vector.bn_stats(stats[:, a, :], slot(xres, UT * u + a)).then_inc(stats_done, 1)
                settle(nc, stats_done, UT * u + UT, scratch[:, :])
                for a in range(UT):
                    nc.vector.bn_aggr(moments[:, a, :], stats[:, a, :]).then_inc(moments_done, 1)
                dve.wait_ge(moments_done, UT * u + UT)
                nc.vector.tensor_scalar(var_eps[:, :, :], moments[:, :, 1:2], LN_EPS, None, ALU.add).then_inc(var_done, 1)

            def xn_of(u):
                dve.wait_ge(rstd_done, u + 1)
                for a in range(UT):
                    nc.vector.tensor_scalar(xn[:, a:a + 1, :], slot(xres, UT * u + a), moments[:, a, 0:1], rstd[:, a, :],
                                            ALU.subtract, ALU.mult).then_inc(xn_done, 1)

            def xnT_of(u):
                dve.wait_ge(xnT_hi_done, u + 1)
                nc.vector.tensor_tensor(xnT_lo[:, :, :].rearrange("p k n -> p (k n)"), turn_ps[:, :],
                                        xnT_hi[:, :, :].rearrange("p k n -> p (k n)").bitcast(F32), ALU.subtract
                                        ).then_inc(xnT_done, 1)

            def qk_of(u, i):
                dve.wait_ge(qk_hi_done[i], KD * u + KD)
                for k in range(KD):
                    nc.vector.scalar_tensor_tensor(out=qk_lo[i][:, k, :], in0=(q_ps, k_ps)[i][:, k * UTOK:(k + 1) * UTOK],
                                                   scalar=bias_cols[:, i, k:k + 1], in1=qk_hi[i][:, k, :].bitcast(F32),
                                                   op0=ALU.add, op1=ALU.subtract).then_inc(qk_done[i], 1)

            def feat_of(u, n, dst):
                dve.wait_ge(feat_full, FEATS * u + n + 1)
                nc.vector.tensor_scalar(dst, feat_ps[:, n % 2, :], 0.0, PHI_EPS, ALU.max, ALU.add).then_inc(feat_done, 1)

            def k_feat_of(u, a):
                for k in range(KD):
                    feat_of(u, KD * a + k, k_feat[:, a, k, :])

            def q_feat_of(u, c):
                feat_of(u, UT * KD + c, q_feat[:, 2 * c:2 * c + 2, :].rearrange("p c n -> p (c n)"))

            def divide(t, a):
                dve.wait_ge(num_full, t + 1)
                for b in range(TB):
                    rows = slice(b * ROWS, (b + 1) * ROWS)
                    src = sum_ps[rows, :, 0:GP * PAIR].rearrange("p g (c b h d) -> p g c b h d", b=TB, h=2, d=DV)
                    nc.vector.tensor_scalar(den[rows, a, :].rearrange("p (g c h) -> p g c h", g=2, h=2),
                                            src[:, :, :, b, :, DK], PHI_EPS, None, ALU.add).then_inc(den_done, 1)
                dve.wait_ge(den_done, TB * t + TB)
                nc.vector.reciprocal(inv_den[:, a, :], den[:, a, :]).then_inc(inv_done, 1)
                dve.wait_ge(inv_done, t + 1)
                for b in range(TB):
                    rows = slice(b * ROWS, (b + 1) * ROWS)
                    for g in range(2):
                        src = sum_ps[rows, g, 0:GP * PAIR].rearrange("p (c b h d) -> p c b h d", b=TB, h=2, d=DV)
                        inv = inv_den[rows, a, g * 2 * GP:(g + 1) * 2 * GP].rearrange("p (c h) -> p c h", h=2)
                        dst = o_nat[rows, a, g * P:(g + 1) * P].rearrange("p (c h d) -> p c h d", h=2, d=DK)
                        nc.vector.tensor_tensor(dst, src[:, :, b, :, 0:DK], inv.unsqueeze(3).to_broadcast([ROWS, GP, 2, DK]),
                                                ALU.mult).then_inc(o_done, 1)

            def oT_of(t, a):
                dve.wait_ge(oT_hi_done, t + 1)
                nc.vector.tensor_tensor(oT_lo[:, a, :, :].rearrange("p k n -> p (k n)"), (turn_ps, q_ps)[a][:, 0:D],
                                        oT_hi[:, a, :, :].rearrange("p k n -> p (k n)").bitcast(F32), ALU.subtract
                                        ).then_inc(oT_done, 1)

            def x_of(u):
                dve.wait_ge(out_full, u + 1)
                dst = xres[:, bass.ds(UT * u, UT), :]
                nc.vector.tensor_tensor(dst, ends_ps[:, :].rearrange("p (a n) -> p a n", a=UT), dst, ALU.add
                                        ).then_inc(x_done, 1)

            nc.vector.memset(minus_half[:, :, :], -0.5).then_inc(exponent_done, 1)
            moments_of(0)
            xn_of(0)
            xnT_of(0)
            qk_of(0, 0)
            qk_of(0, 1)

            def unit(u, first, last):
                k_feat_of(u, 0)
                if not first:
                    oT_of(UT * u - 1, 1)
                k_feat_of(u, 1)
                if not last:
                    moments_of(u + 1)
                    xn_of(u + 1)
                q_feat_of(u, 0)
                q_feat_of(u, 1)
                if not first:
                    x_of(u - 1)
                if not last:
                    xnT_of(u + 1)
                q_feat_of(u, 2)
                q_feat_of(u, 3)
                if not last:
                    qk_of(u + 1, 0)
                divide(UT * u, 0)
                if not last:
                    qk_of(u + 1, 1)
                oT_of(UT * u, 0)
                divide(UT * u + 1, 1)

            unit(0, True, False)
            nc.vector.memset(next_weights["b_out_raw"][:, :], 0.0).then_inc(next_weights["zeroed"], 1)
            with dve.Fori(1, E + 1) as u:
                unit(u, False, False)
            split_small_lo(nc, dve, next_weights)
            with dve.Fori(E + 1, NU - 1) as u:
                unit(u, False, False)
            unit(NU - 1, False, True)
            oT_of(UT * NU - 1, 1)
            x_of(NU - 1)

        @block.tensor
        def _(pe):
            def products(out, pairs):
                for n, (w, m) in enumerate(pairs):
                    ins = nc.tensor.matmul(out, w, m, start=n == 0, stop=n == len(pairs) - 1)
                return ins

            def three(w_hi, w_lo, m_hi, m_lo):
                return [(w_hi, m_hi), (w_lo, m_hi), (w_hi, m_lo)]

            def turn_xn(u):
                pe.wait_ge(xn_done, UT * u + UT)
                after(pe, oT_done, UT * (u - 1))
                for k in range(KD):
                    for a in range(UT):
                        c = k * UTOK + a * P
                        ins = nc.tensor.transpose(turn_ps[:, c:c + P], xn[:, a, k * P:(k + 1) * P], ident[:, :])
                ins.then_inc(xn_turned, 1)

            def project_qk(u, i):
                pe.wait_ge(xnT_done, u + 1)
                if i == 0:
                    after(pe, oT_done, UT * (u - 1))
                w_hi, w_lo = split[("wq", "wk")[i]]
                for m in range(KD):
                    cols = slice(m * P, (m + 1) * P)
                    ins = products((q_ps, k_ps)[i][:, m * UTOK:(m + 1) * UTOK],
                                   [pair for k in range(KD) for pair in
                                    three(w_hi[:, k, cols], w_lo[:, k, cols], xnT_hi[:, k, :], xnT_lo[:, k, :])])
                ins.then_inc(qk_full[i], 1)

            def project_v(u):
                after(pe, x_done, u - 1)
                w_hi, w_lo = split["wv"]
                for a in range(UT):
                    tok = slice(a * P, (a + 1) * P)
                    ins = products(ends_ps[:, a * D:(a + 1) * D],
                                   [(ones_rows[:, :], bias_rows[:, 0, :])] +
                                   [pair for k in range(KD) for pair in
                                    three(xnT_hi[:, k, tok], xnT_lo[:, k, tok], w_hi[:, k, :], w_lo[:, k, :])])
                ins.then_inc(v_full, 1)

            def k_features(u, a):
                pe.wait_ge(qk_done[1], KD * u + KD)
                tok = slice(a * P, (a + 1) * P)
                for k in range(KD):
                    n = KD * a + k
                    after(pe, feat_done, FEATS * u + max(n - 1, 0))
                    products(feat_ps[:, n % 2, :], three(qk_hi[1][:, k, tok], qk_lo[1][:, k, tok],
                                                         rw_hi[:, k, :], rw_lo[:, k, :])).then_inc(feat_full, 1)

            def q_features(u, c):
                if c == 0:
                    pe.wait_ge(qk_done[0], KD * u + KD)
                n = UT * KD + c
                pe.wait_ge(feat_done, FEATS * u + n - 1)
                for i in range(2):
                    k, pair = (2 * c + i) // GP, (2 * c + i) % GP
                    cols = slice(pair * P, (pair + 1) * P)
                    ins = products(feat_ps[:, n % 2, i * UTOK:(i + 1) * UTOK],
                                   three(rw_hi[:, k, cols], rw_lo[:, k, cols], qk_hi[0][:, k, :], qk_lo[0][:, k, :]))
                ins.then_inc(feat_full, 1)

            def sum_kv(u, a):
                t = UT * u + a
                if a == 0:
                    pe.wait_ge(v_done, UT * TB * u + UT * TB)
                    after(pe, o_done, 2 * TB * t)
                else:
                    pe.wait_ge(kv_done, 2 * t)
                pe.wait_ge(feat_done, FEATS * u + KD * (a + 1))
                for c in range(HP):
                    out = sum_ps[:, c // GP, (c % GP) * PAIR:(c % GP + 1) * PAIR]
                    ins = nc.tensor.matmul(out, k_feat[:, a, c // GP, (c % GP) * P:(c % GP + 1) * P],
                                           v_ones[:, a, c, :, :, :].rearrange("p b h d -> p (b h d)"), start=True, stop=True)
                ins.then_inc(kv_full, 1)

            def numerators(u, a):
                t = UT * u + a
                if a == 0:
                    pe.wait_ge(feat_done, FEATS * u + FEATS)
                    pe.wait_ge(kv_done, 2 * t + 4)
                else:
                    pe.wait_ge(o_done, 2 * TB * t)
                tok = slice(a * P, (a + 1) * P)
                for c in range(HP):
                    out = sum_ps[:, c // GP, (c % GP) * PAIR:(c % GP + 1) * PAIR]
                    ins = nc.tensor.matmul(out, q_feat[:, c, tok],
                                           kv[:, a, c, :, :, :].rearrange("p b h d -> p (b h d)"), start=True, stop=True)
                ins.then_inc(num_full, 1)

            def turn_o(u, a, q_done_next=None):
                t = UT * u + a
                pe.wait_ge(o_done, 2 * TB * t + 2 * TB)
                if a == 1:
                    pe.wait_ge(qk_done[0], q_done_next)
                for k in range(KD):
                    ins = nc.tensor.transpose((turn_ps, q_ps)[a][:, k * P:(k + 1) * P], o_nat[:, a, k * P:(k + 1) * P], ident[:, :])
                ins.then_inc(o_turned, 1)

            def project_out(u, a, last_v):
                t = UT * u + a
                pe.wait_ge(oT_done, t + 1)
                if a == 0:
                    pe.wait_ge(v_done, last_v)
                w_hi, w_lo = split["wo"]
                ins = products(ends_ps[:, a * D:(a + 1) * D],
                         [(ones_rows[:, :], bias_rows[:, 1, :])] +
                         [pair for k in range(KD) for pair in
                          three(oT_hi[:, a, k, :], oT_lo[:, a, k, :], w_hi[:, k, :], w_lo[:, k, :])])
                if a == UT - 1:
                    ins.then_inc(out_full, 1)

            turn_xn(0)
            pe.wait_ge(weights["lo_done"], len(LA_PIECES) + 1)
            project_qk(0, 0)
            project_qk(0, 1)
            pe.wait_ge(consts_done, CONSTS)
            project_v(0)

            def unit(u, first, last):
                V_DONE = UT * TB * (u + 1)
                k_features(u, 0)
                if not first:
                    project_out(u - 1, 0, V_DONE)
                    turn_o(u - 1, 1, KD * u + KD)
                k_features(u, 1)
                sum_kv(u, 0)
                if not first:
                    project_out(u - 1, 1, V_DONE)
                q_features(u, 0)
                q_features(u, 1)
                if not last:
                    turn_xn(u + 1)
                sum_kv(u, 1)
                q_features(u, 2)
                q_features(u, 3)
                if not last:
                    project_qk(u + 1, 0)
                numerators(u, 0)
                if not last:
                    project_qk(u + 1, 1)
                    project_v(u + 1)
                turn_o(u, 0)
                numerators(u, 1)

            unit(0, True, False)
            with pe.Fori(1, NU - 1) as u:
                unit(u, False, False)
            unit(NU - 1, False, True)
            project_out(NU - 1, 0, UT * TB * NU)
            turn_o(NU - 1, 1, KD * NU)
            project_out(NU - 1, 1, UT * TB * NU)


def mixture(nc, weights, xres, ident, out):
    _, E, KD, H = weights["win_hi"].shape
    D = KD * P
    TOP = 2
    NT = xres.shape[1]
    UT = 4
    NU = NT // UT
    UTOK = UT * P
    KH = H // P
    LANE = MOE_LANE
    assert UTOK == BANK and 2 * D == BANK and TOP == 2

    out_tiles = out.rearrange("(t b) q d -> (b q) t d", b=P // out.shape[1])

    with ExitStack() as stack:
        def sb(name, shape, dt=F32):
            return stack.enter_context(nc.sbuf_tensor("moe_" + name, shape, dt))

        def sem(name):
            return stack.enter_context(nc.semaphore("moe_" + name))

        win_hi, win_lo, wout_hi, wout_lo = (weights[n] for n in ("win_hi", "win_lo", "wout_hi", "wout_lo"))
        router = weights["router"]
        b_in_cols, b_out_rows = weights["b_in_cols"], weights["b_out_rows"]
        expert_ids = sb("expert_ids", [P, UT, E])

        scratch = sb("scratch", [P, 1])
        stats = sb("stats", [P, UT, 6])
        moments = sb("moments", [P, UT, 2])
        var_eps = sb("var_eps", [P, UT, 1])
        rstd = sb("rstd", [P, UT, 1])
        minus_half = sb("minus_half", [P, UT, 1])
        xn = sb("xn", [P, UT, D])
        xnT_hi = [sb(f"xnT_hi{i}", [P, KD, UTOK], F32R) for i in range(2)]
        xnT_lo = [sb(f"xnT_lo{i}", [P, KD, UTOK], F32R) for i in range(2)]
        logitsT = sb("logitsT", [P, UTOK])
        part_sums = sb("part_sums", [P, UT, 2 * E])
        logit_sums = sb("logit_sums", [P, UT, E])
        neg_max = sb("neg_max", [P, UT, 1])
        shifted = sb("shifted", [P, UT, E])
        exps = sb("exps", [P, UT, E])
        exp_sum = sb("exp_sum", [P, UT, 1])
        inv_sum = sb("inv_sum", [P, UT, 1])
        probs = sb("probs", [P, UT, E])
        top_p = sb("top_p", [P, UT, 8])
        top_id = sb("top_id", [P, UT, 8], U32)
        top_idf = sb("top_idf", [P, UT, 8])
        is_first = sb("is_first", [P, UT, E])
        is_second = sb("is_second", [P, UT, E])
        chosen = sb("chosen", [P, UT, E])
        gates = [sb(f"gates{i}", [P, UT, E]) for i in range(2)]
        gate_parts = sb("gate_parts", [P, UT, P])
        gatesT = [sb(f"gatesT{i}", [P, UTOK], F32R) for i in range(2)]
        h = [sb(f"h{i}", [P, KH, UTOK]) for i in range(2)]
        h_hi = [sb(f"h_hi{i}", [P, KH, UTOK], F32R) for i in range(2)]
        h_lo = [sb(f"h_lo{i}", [P, KH, UTOK], F32R) for i in range(2)]

        h_ps = stack.enter_context(nc.psum_tensor("moe_h_ps", [P, 4, BANK], F32))
        y_ps = stack.enter_context(nc.psum_tensor("moe_y_ps", [P, 2, BANK], F32))
        aux_ps = stack.enter_context(nc.psum_tensor("moe_aux_ps", [P, 2, BANK], F32))

        zeroed = sem("zeroed")
        ids_done = sem("ids_done")
        consts_done = sem("consts_done")
        stats_done = sem("stats_done")
        moments_done = sem("moments_done")
        var_done = sem("var_done")
        rstd_done = sem("rstd_done")
        xn_done = sem("xn_done")
        xn_turned = sem("xn_turned")
        xnT_hi_done = sem("xnT_hi_done")
        xnT_done = sem("xnT_done")
        logits_full = sem("logits_full")
        logitsT_done = sem("logitsT_done")
        logits_turned = sem("logits_turned")
        shifted_done = sem("shifted_done")
        exps_done = sem("exps_done")
        route = sem("route")
        gates_turned = sem("gates_turned")
        gatesT_done = sem("gatesT_done")
        h_full = sem("h_full")
        gelu_done = sem("gelu_done")
        h_hi_done = sem("h_hi_done")
        h_done = sem("h_done")
        y_full = sem("y_full")
        y_done = sem("y_done")
        biases_full = sem("biases_full")
        biases_done = sem("biases_done")
        stored = sem("stored")

        CONSTS = 1
        ROUTE = 7 + 2 * UT + 7
        block = stack.enter_context(nc.Block())

        @block.sync
        def _(sp):
            with sp.Fori(0, NU) as u:
                sp.wait_ge(y_done, 2 * E * u + 2 * E)
                sp.dma_start(out_tiles[:, bass.ds(UT * u, UT), :], xres[:, bass.ds(UT * u, UT), :]).then_inc(stored, 16)
            sp.wait_ge(stored, 16 * NU)

        @block.gpsimd
        def _(pool):
            nc.gpsimd.iota(expert_ids[:, :, :], pattern=[[0, UT], [1, E]], base=0, channel_multiplier=0,
                           allow_small_or_imprecise_dtypes=True).then_inc(ids_done, 1)
            pool.wait_ge(ids_done, 1)
            pool.wait_ge(consts_done, CONSTS)
            with pool.Fori(0, NU) as u:
                pool.wait_ge(var_done, u + 1)
                nc.gpsimd.tensor_tensor(rstd[:, :, :], var_eps[:, :, :], minus_half[:, :, :], ALU.pow
                                        ).then_inc(rstd_done, 1)

        @block.scalar
        def _(act):
            def xnT_of(u, u_parity):
                for k in range(KD):
                    act.wait_ge(xn_turned, KD * u + k + 1)
                    nc.scalar.activation(xnT_hi[u_parity][:, k, :], aux_ps[:, k, :], ACT.Copy).then_inc(xnT_hi_done, 1)

            def exps_of(u):
                act.wait_ge(shifted_done, u + 1)
                nc.scalar.activation(exps[:, :, :], shifted[:, :, :], ACT.Exp).then_inc(exps_done, 1)

            def logitsT_of(u):
                act.wait_ge(logits_full, u + 1)
                nc.scalar.activation(logitsT[0:2 * E, :], aux_ps[0:2 * E, 0, :], ACT.Copy).then_inc(logitsT_done, 1)

            def gatesT_of(u, u_parity):
                act.wait_ge(gates_turned, u + 1)
                nc.scalar.activation(gatesT[u_parity][:, :], aux_ps[:, 0, :], ACT.Copy).then_inc(gatesT_done, 1)

            def hidden_of(u, e):
                i = e % 2
                for m in range(KH):
                    act.wait_ge(h_full, KH * (E * u + e) + m + 1)
                    nc.scalar.activation(h[i][:, m, :], h_ps[:, 2 * i + m, :], ACT.Gelu_apprx_tanh,
                                         bias=b_in_cols[:, e, m:m + 1]).then_inc(gelu_done, 1)
                for m in range(KH):
                    act.wait_ge(gelu_done, KH * (E * u + e) + m + 1)
                    nc.scalar.activation(h_hi[i][:, m, :], h[i][:, m, :], ACT.Copy).then_inc(h_hi_done, 1)

            xnT_of(0, 0)
            act.wait_ge(zeroed, 2)
            logitsT_of(0)
            exps_of(0)
            hidden_of(0, 0)
            gatesT_of(0, 0)

            def unit(u, i, last):
                for e in range(1, E):
                    hidden_of(u, e)
                    if not last:
                        if e == 4:
                            xnT_of(u + 1, 1 - i)
                        if e == 5:
                            logitsT_of(u + 1)
                        if e == 6:
                            exps_of(u + 1)
                if not last:
                    hidden_of(u + 1, 0)
                    gatesT_of(u + 1, 1 - i)

            unit(0, 0, False)
            unit(1, 1, False)
            with act.Fori(1, NU // 2 - 1) as v:
                unit(2 * v, 0, False)
                unit(2 * v + 1, 1, False)
            unit(NU - 2, 0, False)
            unit(NU - 1, 1, True)

        @block.vector
        def _(dve):
            def moments_of(u):
                for a in range(UT):
                    nc.vector.bn_stats(stats[:, a, :], slot(xres, UT * u + a)).then_inc(stats_done, 1)
                settle(nc, stats_done, UT * u + UT, scratch[:, :])
                for a in range(UT):
                    nc.vector.bn_aggr(moments[:, a, :], stats[:, a, :]).then_inc(moments_done, 1)
                dve.wait_ge(moments_done, UT * u + UT)
                nc.vector.tensor_scalar(var_eps[:, :, :], moments[:, :, 1:2], LN_EPS, None, ALU.add).then_inc(var_done, 1)

            def xn_of(u):
                dve.wait_ge(rstd_done, u + 1)
                for a in range(UT):
                    nc.vector.tensor_scalar(xn[:, a:a + 1, :], slot(xres, UT * u + a), moments[:, a, 0:1], rstd[:, a, :],
                                            ALU.subtract, ALU.mult).then_inc(xn_done, 1)

            def xnT_of(u, u_parity):
                for k in range(KD):
                    dve.wait_ge(xnT_hi_done, KD * u + k + 1)
                    nc.vector.tensor_tensor(xnT_lo[u_parity][:, k, :], aux_ps[:, k, :], xnT_hi[u_parity][:, k, :].bitcast(F32), ALU.subtract
                                            ).then_inc(xnT_done, 1)

            def shift_of(u):
                dve.wait_ge(logits_turned, u + 1)
                nc.vector.tensor_copy(part_sums[:, :, :], aux_ps[:, 1, :].rearrange("p (a n) -> p a n", a=UT)[:, :, 0:2 * E]
                                      ).then_inc(route, 1)
                dve.wait_ge(route, ROUTE * u + 1)
                lg = logit_sums[:, :, :]
                nc.vector.tensor_tensor(lg, part_sums[:, :, 0:E], part_sums[:, :, E:2 * E], ALU.add).then_inc(route, 1)
                dve.wait_ge(route, ROUTE * u + 2)
                nc.vector.tensor_reduce(neg_max[:, :, :].rearrange("p a o -> p (a o)"), lg, AX.X, ALU.max, negate=True
                                        ).then_inc(route, 1)
                dve.wait_ge(route, ROUTE * u + 3)
                nc.vector.tensor_tensor(shifted[:, :, :], lg, neg_max[:, :, :].to_broadcast([P, UT, E]), ALU.add
                                        ).then_inc(shifted_done, 1)

            def gates_of(u, u_parity):
                step = ROUTE * u + 3
                dve.wait_ge(exps_done, u + 1)
                nc.vector.tensor_reduce(exp_sum[:, :, :].rearrange("p a o -> p (a o)"), exps[:, :, :], AX.X, ALU.add
                                        ).then_inc(route, 1)
                dve.wait_ge(route, step + 1)
                nc.vector.reciprocal(inv_sum[:, :, :], exp_sum[:, :, :]).then_inc(route, 1)
                dve.wait_ge(route, step + 2)
                nc.vector.tensor_tensor(probs[:, :, :], exps[:, :, :], inv_sum[:, :, :].to_broadcast([P, UT, E]), ALU.mult
                                        ).then_inc(route, 1)
                settle(nc, route, step + 3, scratch[:, :])
                for a in range(UT):
                    nc.vector.max(top_p[:, a, :], probs[:, a, :]).then_inc(route, 1)
                settle(nc, route, step + 3 + UT, scratch[:, :])
                for a in range(UT):
                    nc.vector.max_index(top_id[:, a, :], top_p[:, a, :], probs[:, a, :]).then_inc(route, 1)
                dve.wait_ge(route, step + 3 + 2 * UT)
                nc.vector.tensor_copy(top_idf[:, :, :], top_id[:, :, :]).then_inc(route, 1)
                dve.wait_ge(route, step + 4 + 2 * UT)
                for n, same in enumerate((is_first, is_second)):
                    nc.vector.tensor_tensor(same[:, :, :], expert_ids[:, :, :],
                                            top_idf[:, :, n:n + 1].to_broadcast([P, UT, E]), ALU.is_equal).then_inc(route, 1)
                dve.wait_ge(route, step + 6 + 2 * UT)
                nc.vector.tensor_tensor(chosen[:, :, :], is_first[:, :, :], is_second[:, :, :], ALU.add).then_inc(route, 1)
                dve.wait_ge(route, step + 7 + 2 * UT)
                nc.vector.tensor_tensor(gates[u_parity][:, :, :], probs[:, :, :], chosen[:, :, :], ALU.mult).then_inc(route, 1)
                dve.wait_ge(route, step + 8 + 2 * UT)
                for lane in (0, 2):
                    nc.vector.tensor_copy(gate_parts[:, :, lane * LANE:lane * LANE + E].bitcast(F32R), gates[u_parity][:, :, :]
                                          ).then_inc(route, 1)
                dve.wait_ge(route, step + 10 + 2 * UT)
                nc.vector.tensor_tensor(gate_parts[:, :, LANE:LANE + E], gates[u_parity][:, :, :], gate_parts[:, :, 0:E], ALU.subtract
                                        ).then_inc(route, 1)

            def hidden_of(u, e):
                i = e % 2
                for m in range(KH):
                    dve.wait_ge(h_hi_done, KH * (E * u + e) + m + 1)
                    nc.vector.tensor_tensor(h_lo[i][:, m, :], h[i][:, m, :], h_hi[i][:, m, :].bitcast(F32), ALU.subtract
                                            ).then_inc(h_done, 1)

            def add_expert(u, u_parity, e):
                if e == 2:
                    dve.wait_ge(biases_done, u + 1)
                for j in range(2):
                    dve.wait_ge(y_full, 2 * (E * u + e) + j + 1)
                    after(dve, y_done, 2 * E * u + 2 * e + j - 1)
                    for i in range(2):
                        a = 2 * j + i
                        dst = slot(xres, UT * u + a)
                        ins = nc.vector.scalar_tensor_tensor(out=dst, in0=y_ps[:, j, i * D:(i + 1) * D].unsqueeze(1),
                                                             scalar=gates[u_parity][:, a, e:e + 1], in1=dst,
                                                             op0=ALU.mult, op1=ALU.add)
                    ins.then_inc(y_done, 1)

            def add_biases(u):
                dve.wait_ge(biases_full, u + 1)
                dve.wait_ge(y_done, 2 * E * u + 4)
                dst = xres[:, bass.ds(UT * u, UT), :]
                nc.vector.tensor_tensor(dst, aux_ps[:, :, :].rearrange("p j (i n) -> p (j i) n", i=2), dst, ALU.add
                                        ).then_inc(biases_done, 1)

            nc.vector.memset(minus_half[:, :, :], -0.5).then_inc(consts_done, 1)
            nc.vector.memset(gate_parts[:, :, :], 0.0).then_inc(zeroed, 1)
            nc.vector.memset(logitsT[:, :], 0.0).then_inc(zeroed, 1)
            moments_of(0)
            xn_of(0)
            xnT_of(0, 0)
            shift_of(0)
            dve.wait_ge(ids_done, 1)
            dve.wait_ge(zeroed, 2)
            gates_of(0, 0)

            def unit(u, i, last):
                hidden_of(u, 0)
                hidden_of(u, 1)
                add_expert(u, i, 0)
                hidden_of(u, 2)
                add_expert(u, i, 1)
                add_biases(u)
                for e in range(3, E):
                    hidden_of(u, e)
                    add_expert(u, i, e - 1)
                    if not last:
                        if e == 3:
                            moments_of(u + 1)
                            xn_of(u + 1)
                        if e == 4:
                            xnT_of(u + 1, 1 - i)
                        if e == 5:
                            shift_of(u + 1)
                        if e == 6:
                            gates_of(u + 1, 1 - i)
                add_expert(u, i, E - 1)

            unit(0, 0, False)
            unit(1, 1, False)
            with dve.Fori(1, NU // 2 - 1) as v:
                unit(2 * v, 0, False)
                unit(2 * v + 1, 1, False)
            unit(NU - 2, 0, False)
            unit(NU - 1, 1, True)

        @block.tensor
        def _(pe):
            def products(out, pairs):
                for n, (w, m) in enumerate(pairs):
                    ins = nc.tensor.matmul(out, w, m, start=n == 0, stop=n == len(pairs) - 1)
                return ins

            def three(w_hi, w_lo, m_hi, m_lo):
                return [(w_hi, m_hi), (w_lo, m_hi), (w_hi, m_lo)]

            def turn_xn(u, k):
                if k == 0:
                    pe.wait_ge(xn_done, UT * u + UT)
                    after(pe, biases_done, u)
                for a in range(UT):
                    ins = nc.tensor.transpose(aux_ps[:, k, a * P:(a + 1) * P], xn[:, a, k * P:(k + 1) * P], ident[:, :])
                ins.then_inc(xn_turned, 1)

            def logits(u, i):
                pe.wait_ge(xnT_done, KD * u + KD)
                products(aux_ps[0:2 * E, 0, :],
                         [(router[:, k, :], part[i][:, k, :]) for k in range(KD) for part in (xnT_hi, xnT_lo)]
                         ).then_inc(logits_full, 1)

            def turn_logits(u):
                pe.wait_ge(logitsT_done, u + 1)
                for a in range(UT):
                    ins = nc.tensor.transpose(aux_ps[:, 1, a * P:(a + 1) * P], logitsT[:, a * P:(a + 1) * P], ident[:, :])
                ins.then_inc(logits_turned, 1)

            def turn_gates(u):
                pe.wait_ge(route, ROUTE * u + ROUTE)
                for a in range(UT):
                    ins = nc.tensor.transpose(aux_ps[:, 0, a * P:(a + 1) * P], gate_parts[:, a, :], ident[:, :])
                ins.then_inc(gates_turned, 1)

            def hidden(u, u_parity, e):
                i = e % 2
                if e == 0:
                    pe.wait_ge(xnT_done, KD * u + KD)
                for m in range(KH):
                    after(pe, gelu_done, KH * E * u + max(KH * (e - 2) + m + 1, 0))
                    cols = slice(m * P, (m + 1) * P)
                    products(h_ps[:, 2 * i + m, :],
                             [pair for k in range(KD) for pair in
                              three(win_hi[:, e, k, cols], win_lo[:, e, k, cols], xnT_hi[u_parity][:, k, :],
                                    xnT_lo[u_parity][:, k, :])]
                             ).then_inc(h_full, 1)

            def outputs(u, e):
                i = e % 2
                pe.wait_ge(h_done, KH * (E * u + e) + KH)
                for j in range(2):
                    after(pe, y_done, 2 * E * u + 2 * e + j - 1)
                    for n in range(2):
                        tok = slice((2 * j + n) * P, (2 * j + n + 1) * P)
                        ins = products(y_ps[:, j, n * D:(n + 1) * D],
                                       [pair for k in range(KH) for pair in
                                        three(h_hi[i][:, k, tok], h_lo[i][:, k, tok], wout_hi[:, e, k, :], wout_lo[:, e, k, :])])
                    ins.then_inc(y_full, 1)

            def biases(u, u_parity):
                pe.wait_ge(gatesT_done, u + 1)
                for a in range(UT):
                    ins = nc.tensor.matmul(aux_ps[:, a // 2, (a % 2) * D:(a % 2 + 1) * D],
                                           gatesT[u_parity][:, a * P:(a + 1) * P], b_out_rows[:, :], start=True, stop=True)
                ins.then_inc(biases_full, 1)

            turn_xn(0, 0)
            turn_xn(0, 1)
            pe.wait_ge(weights["small_lo_done"], 2)
            pe.wait_ge(weights["lo_done"], 2 * E)
            logits(0, 0)
            turn_logits(0)
            hidden(0, 0, 0)
            hidden(0, 0, 1)
            turn_gates(0)

            def unit(u, i, last):
                outputs(u, 0)
                hidden(u, i, 2)
                biases(u, i)
                outputs(u, 1)
                for e in range(3, E):
                    hidden(u, i, e)
                    if e == 5 and not last:
                        turn_xn(u + 1, 0)
                        turn_xn(u + 1, 1)
                    if e == 6 and not last:
                        turn_logits(u + 1)
                    outputs(u, e - 1)
                    if e == 5 and not last:
                        logits(u + 1, 1 - i)
                if not last:
                    hidden(u + 1, 1 - i, 0)
                    turn_gates(u + 1)
                outputs(u, E - 1)
                if not last:
                    hidden(u + 1, 1 - i, 1)

            unit(0, 0, False)
            unit(1, 1, False)
            with pe.Fori(1, NU // 2 - 1) as v:
                unit(2 * v, 0, False)
                unit(2 * v + 1, 1, False)
            unit(NU - 2, 0, False)
            unit(NU - 1, 1, True)


def perceiver_block(nc, x, ctx, xattn, attn, ffn, out):
    NT = x.shape[0] * x.shape[1] // P
    with ExitStack() as stack:
        xres = stack.enter_context(nc.sbuf_tensor("xres", [P, NT, x.shape[2]], F32))
        ident = stack.enter_context(nc.sbuf_tensor("ident", [P, P], F32))
        H, DK, F = attn[-1].shape
        weights = linear_attention_weights(nc, stack, x.shape[2], H, F)
        cross_attention(nc, x, ctx, *xattn, xres, ident, weights, attn)
        with ExitStack() as raw_stack:
            expert_weights = mixture_weights(nc, stack, raw_stack, *ffn[1].shape)
            linear_attention(nc, weights, x.shape[2], H, DK, F, xres, ident, expert_weights, ffn)
        mixture(nc, expert_weights, xres, ident, out)


_XATTN = ["L0_xattn_Wq", "L0_xattn_Wk", "L0_xattn_Wv", "L0_xattn_Wo", "L0_xattn_bo"]
_ATTN = ["L0_attn_Wq", "L0_attn_bq", "L0_attn_Wk", "L0_attn_bk", "L0_attn_Wv", "L0_attn_bv", "L0_attn_Wo", "L0_attn_bo",
         "L0_attn_rw"]
_FFN = ["L0_ffn_router_w", "L0_ffn_w_in", "L0_ffn_b_in", "L0_ffn_w_out", "L0_ffn_b_out"]


def kernel(**inputs):
    import numpy as _np
    import concourse.bacc as _bacc
    from concourse.bass_utils import run_bass_kernel_spmd as _run

    nc = _bacc.Bacc("TRN2", target_bir_lowering=False, num_devices=1)
    arrays, aps = {}, {}
    for name in ["x", "ctx_768"] + _XATTN + _ATTN + _FFN:
        a = _np.ascontiguousarray(inputs[name])
        arrays[f"in_{name}"] = a
        aps[name] = nc.dram_tensor(f"in_{name}", a.shape, mybir.dt.from_np(a.dtype), kind="ExternalInput").ap()
    out = nc.dram_tensor("out", inputs["x"].shape, F32, kind="ExternalOutput").ap()
    perceiver_block(nc, aps["x"], aps["ctx_768"], [aps[n] for n in _XATTN], [aps[n] for n in _ATTN],
                    [aps[n] for n in _FFN], out)
    return _run(nc, [arrays], core_ids=[0]).results[0]["out"]
```

```python
from contextlib import ExitStack

import concourse.bass as bass
from concourse import mybir

F32 = mybir.dt.float32
F32R = mybir.dt.float32r
U32 = mybir.dt.uint32
ALU = mybir.AluOpType
ACT = mybir.ActivationFunctionType
AX = mybir.AxisListType

P = 128
BANK = 512
LN_EPS = 1e-5
PHI_EPS = 1e-6


def after(engine, semaphore, value):
    if isinstance(value, int) and value <= 0:
        return
    engine.wait_ge(semaphore, value)


def settle(nc, semaphore, value, scratch):
    nc.vector.wait_ge(semaphore, value)
    nc.vector.memset(scratch, 0.0)


def slot(tiles, t):
    return tiles[:, bass.ds(t, 1), :]


class Norm:

    def __init__(self, nc, stack, name, UT, D):
        def sb(part, shape):
            return stack.enter_context(nc.sbuf_tensor(f"{name}_{part}", shape, F32))

        def sem(part):
            return stack.enter_context(nc.semaphore(f"{name}_{part}"))

        self.UT = UT
        self.scratch = sb("scratch", [P, 1])
        self.stats = sb("stats", [P, UT, 6])
        self.moments = sb("moments", [P, UT, 2])
        self.var_eps = sb("var_eps", [P, UT, 1])
        self.rstd = sb("rstd", [P, UT, 1])
        self.minus_half = sb("minus_half", [P, UT, 1])
        self.xn = sb("xn", [P, UT, D])
        self.exponent_done = sem("exponent_done")
        self.stats_done = sem("stats_done")
        self.moments_done = sem("moments_done")
        self.var_done = sem("var_done")
        self.rstd_done = sem("rstd_done")
        self.xn_done = sem("xn_done")

    def set_exponent(self, nc):
        nc.vector.memset(self.minus_half[:, :, :], -0.5).then_inc(self.exponent_done, 1)

    def moments_of(self, nc, dve, xres, u):
        UT = self.UT
        for a in range(UT):
            nc.vector.bn_stats(self.stats[:, a, :], slot(xres, UT * u + a)).then_inc(self.stats_done, 1)
        settle(nc, self.stats_done, UT * u + UT, self.scratch[:, :])
        for a in range(UT):
            nc.vector.bn_aggr(self.moments[:, a, :], self.stats[:, a, :]).then_inc(self.moments_done, 1)
        dve.wait_ge(self.moments_done, UT * u + UT)
        nc.vector.tensor_scalar(self.var_eps[:, :, :], self.moments[:, :, 1:2], LN_EPS, None, ALU.add
                                ).then_inc(self.var_done, 1)

    def rstd_of(self, nc, pool, u):
        pool.wait_ge(self.var_done, u + 1)
        nc.gpsimd.tensor_tensor(self.rstd[:, :, :], self.var_eps[:, :, :], self.minus_half[:, :, :], ALU.pow
                                ).then_inc(self.rstd_done, 1)

    def xn_of(self, nc, dve, xres, u):
        dve.wait_ge(self.rstd_done, u + 1)
        for a in range(self.UT):
            nc.vector.tensor_scalar(self.xn[:, a:a + 1, :], slot(xres, self.UT * u + a), self.moments[:, a, 0:1],
                                    self.rstd[:, a, :], ALU.subtract, ALU.mult).then_inc(self.xn_done, 1)


class TurnedTokens:

    def __init__(self, nc, stack, KD, UTOK, E):
        def sem(part):
            return stack.enter_context(nc.semaphore("moe_" + part))

        self.KD, self.E = KD, E
        self.hi, self.lo = ([stack.enter_context(nc.sbuf_tensor(f"moe_xnT_{part}{i}", [P, KD, UTOK], F32R))
                             for i in range(2)] for part in ("hi", "lo"))
        self.logitsT = stack.enter_context(nc.sbuf_tensor("moe_logitsT", [P, UTOK], F32))
        self.zeroed = sem("logitsT_zeroed")
        self.turned = sem("xn_turned")
        self.hi_done = sem("xnT_hi_done")
        self.done = sem("xnT_done")
        self.logits_full = sem("logits_full")
        self.logitsT_done = sem("logitsT_done")

    def zero(self, nc):
        nc.vector.memset(self.logitsT[:, :], 0.0).then_inc(self.zeroed, 1)

    def turn(self, nc, pe, norm, ident, u, k, bank):
        pe.wait_ge(norm.xn_done, norm.UT * u + norm.UT)
        for a in range(norm.UT):
            ins = nc.tensor.transpose(bank[:, a * P:(a + 1) * P], norm.xn[:, a, k * P:(k + 1) * P], ident[:, :])
        ins.then_inc(self.turned, 1)

    def hi_of(self, nc, act, u, parity, banks):
        for k in range(self.KD):
            act.wait_ge(self.turned, self.KD * u + k + 1)
            nc.scalar.activation(self.hi[parity][:, k, :], banks[k], ACT.Copy).then_inc(self.hi_done, 1)

    def lo_of(self, nc, dve, u, parity, banks):
        for k in range(self.KD):
            dve.wait_ge(self.hi_done, self.KD * u + k + 1)
            nc.vector.tensor_tensor(self.lo[parity][:, k, :], banks[k], self.hi[parity][:, k, :].bitcast(F32),
                                    ALU.subtract).then_inc(self.done, 1)

    def logits(self, nc, pe, router, u, parity, bank):
        pe.wait_ge(self.done, self.KD * u + self.KD)
        pairs = [(router[:, k, :], part[parity][:, k, :]) for k in range(self.KD) for part in (self.hi, self.lo)]
        for n, (w, m) in enumerate(pairs):
            ins = nc.tensor.matmul(bank[0:2 * self.E, :], w, m, start=n == 0, stop=n == len(pairs) - 1)
        ins.then_inc(self.logits_full, 1)

    def logitsT_of(self, nc, act, u, bank):
        act.wait_ge(self.logits_full, u + 1)
        nc.scalar.activation(self.logitsT[0:2 * self.E, :], bank[0:2 * self.E, :], ACT.Copy).then_inc(self.logitsT_done, 1)


class QueryTokens:

    def __init__(self, nc, stack, KD, UTOK):
        def sb(part):
            return stack.enter_context(nc.sbuf_tensor("la_" + part, [P, KD, UTOK], F32R))

        def sem(part):
            return stack.enter_context(nc.semaphore("la_" + part))

        self.KD, self.UTOK = KD, UTOK
        self.hi, self.lo, self.q_hi, self.q_lo = (sb(part) for part in ("xnT_hi", "xnT_lo", "q_hi", "q_lo"))
        self.turned = sem("xn_turned")
        self.hi_done = sem("xnT_hi_done")
        self.done = sem("xnT_done")
        self.q_full = sem("q_full")
        self.q_hi_done = sem("q_hi_done")
        self.q_done = sem("q_done")

    def turn(self, nc, pe, norm, ident, u, bank):
        pe.wait_ge(norm.xn_done, norm.UT * u + norm.UT)
        for k in range(self.KD):
            for a in range(norm.UT):
                c = k * self.UTOK + a * P
                ins = nc.tensor.transpose(bank[:, c:c + P], norm.xn[:, a, k * P:(k + 1) * P], ident[:, :])
        ins.then_inc(self.turned, 1)

    def hi_of(self, nc, act, u, bank):
        act.wait_ge(self.turned, u + 1)
        nc.scalar.activation(self.hi[:, :, :].rearrange("p k n -> p (k n)"), bank, ACT.Copy).then_inc(self.hi_done, 1)

    def lo_of(self, nc, dve, u, bank):
        dve.wait_ge(self.hi_done, u + 1)
        nc.vector.tensor_tensor(self.lo[:, :, :].rearrange("p k n -> p (k n)"), bank,
                                self.hi[:, :, :].rearrange("p k n -> p (k n)").bitcast(F32), ALU.subtract
                                ).then_inc(self.done, 1)

    def queries(self, nc, pe, w, u, bank):
        pe.wait_ge(self.done, u + 1)
        for m in range(self.KD):
            cols = slice(m * P, (m + 1) * P)
            pairs = [pair for k in range(self.KD) for pair in
                     ((w["wq_hi"][:, k, cols], self.hi[:, k, :]), (w["wq_lo"][:, k, cols], self.hi[:, k, :]),
                      (w["wq_hi"][:, k, cols], self.lo[:, k, :]))]
            for n, (stationary, moving) in enumerate(pairs):
                ins = nc.tensor.matmul(bank[:, m * self.UTOK:(m + 1) * self.UTOK], stationary, moving,
                                       start=n == 0, stop=n == len(pairs) - 1)
        ins.then_inc(self.q_full, 1)

    def q_hi_of(self, nc, act, w, u, bank):
        act.wait_ge(self.q_full, u + 1)
        for k in range(self.KD):
            nc.scalar.activation(self.q_hi[:, k, :], bank[:, k * self.UTOK:(k + 1) * self.UTOK], ACT.Identity,
                                 bias=w["bias_cols"][:, 0, k:k + 1]).then_inc(self.q_hi_done, 1)

    def q_lo_of(self, nc, dve, w, u, bank):
        dve.wait_ge(self.q_hi_done, self.KD * u + self.KD)
        for k in range(self.KD):
            nc.vector.scalar_tensor_tensor(out=self.q_lo[:, k, :], in0=bank[:, k * self.UTOK:(k + 1) * self.UTOK],
                                           scalar=w["bias_cols"][:, 0, k:k + 1], in1=self.q_hi[:, k, :].bitcast(F32),
                                           op0=ALU.add, op1=ALU.subtract).then_inc(self.q_done, 1)


def linear_attention_weights(nc, stack, D, H, F):
    KD = D // P
    w = {}
    for name, cols in (("wq", D), ("wk", D), ("wv", D), ("wo", D), ("rw", H // KD * F)):
        for part in ("hi", "lo"):
            w[f"{name}_{part}"] = stack.enter_context(nc.sbuf_tensor(f"la_{name}_{part}", [P, KD, cols], F32R))
    w["bias_cols"] = stack.enter_context(nc.sbuf_tensor("la_bias_cols", [P, 2, KD], F32))
    w["bias_raw"] = stack.enter_context(nc.sbuf_tensor("la_bias_raw", [P, D], F32))
    w["bias_rows"] = stack.enter_context(nc.sbuf_tensor("la_bias_rows", [P, D], F32R))
    w["bo_all"] = stack.enter_context(nc.sbuf_tensor("la_bo_all", [P, D], F32))
    for name in ("rw_zeroed", "rows_zeroed", "here", "hi_done", "lo_done"):
        w[name] = stack.enter_context(nc.semaphore("la_w_" + name))
    return w


LA_PIECES = ("wq", "wk", "wv", "wo", "rw")


def la_raw(raw, n, w):
    start = sum(w[name + "_hi"].shape[1] * w[name + "_hi"].shape[2] for name in LA_PIECES[:n])
    _, kd, cols = w[LA_PIECES[n] + "_hi"].shape
    return raw[:, start:start + kd * cols].rearrange("p (k n) -> p k n", k=kd)


def linear_attention_loads(sp, raw, w, Wq, bq, Wk, bk, Wv, bv, Wo, bo, rw):
    H, DK, F = rw.shape
    KD = Wq.shape[0] // P

    def matrices():
        for n, src in enumerate((Wq, Wk, Wv, Wo)):
            sp.dma_start(la_raw(raw, n, w), src.rearrange("(k p) n -> p k n", p=P)).then_inc(w["here"], 16)

    def biases():
        for i, b in enumerate((bq, bk)):
            sp.dma_start(w["bias_cols"][:, i, :], b.rearrange("(k p) -> p k", p=P), allow_slow_non_contiguous=True
                         ).then_inc(w["here"], 16)
        for row in (0, 32):
            sp.dma_start(w["bias_raw"][row:row + 1, :], bv.rearrange("(a n) -> a n", a=1)).then_inc(w["here"], 16)
        sp.dma_start(w["bo_all"][:, :], bo.rearrange("(a n) -> a n", a=1).to_broadcast([P, bo.shape[0]])
                     ).then_inc(w["here"], 16)

    def features(k):
        sp.wait_ge(w["rw_zeroed"], 1)
        for i in range(H // KD):
            sp.dma_start(la_raw(raw, 4, w)[i * DK:(i + 1) * DK, k, i * F:(i + 1) * F], rw[k * (H // KD) + i, :, :]
                         ).then_inc(w["here"], 16)

    return [matrices, biases] + [lambda k=k: features(k) for k in range(KD)]


def zero_linear_attention(nc, raw, w):
    nc.vector.memset(la_raw(raw, 4, w), 0.0).then_inc(w["rw_zeroed"], 1)
    nc.vector.memset(w["bias_rows"][:, :].bitcast(F32), 0.0).then_inc(w["rows_zeroed"], 1)


def split_linear_attention_hi(nc, act, raw, w, here):
    act.wait_ge(w["here"], here)
    act.wait_ge(w["rw_zeroed"], 1)
    for n, name in enumerate(LA_PIECES):
        nc.scalar.activation(w[name + "_hi"][:, :, :], la_raw(raw, n, w), ACT.Copy
                             ).then_inc(w["hi_done"], 1)
    act.wait_ge(w["rows_zeroed"], 1)
    for row in (0, 32):
        nc.scalar.activation(w["bias_rows"][row:row + 1, :], w["bias_raw"][row:row + 1, :], ACT.Copy
                             ).then_inc(w["hi_done"], 1)


def split_linear_attention_lo(nc, dve, raw, w, here, pieces):
    dve.wait_ge(w["here"], here)
    for n in pieces:
        name = LA_PIECES[n]
        dve.wait_ge(w["hi_done"], n + 1)
        nc.vector.tensor_tensor(w[name + "_lo"][:, :, :], la_raw(raw, n, w), w[name + "_hi"][:, :, :].bitcast(F32),
                                ALU.subtract).then_inc(w["lo_done"], 1)
    if pieces[-1] == len(LA_PIECES) - 1:
        dve.wait_ge(w["hi_done"], len(LA_PIECES) + 2)
        nc.vector.tensor_tensor(w["bias_rows"][32:33, :], w["bias_raw"][32:33, :], w["bias_rows"][32:33, :].bitcast(F32),
                                ALU.subtract).then_inc(w["lo_done"], 1)



def cross_attention(nc, x, ctx_in, Wq, Wk, Wv, Wo, bo, xres, ident, norm, next_norm, next_tokens, next_weights, next_inputs):
    NB, NQ, D = x.shape
    _, NC, DC = ctx_in.shape
    INNER = Wq.shape[1]
    DH = 64
    SCALE = DH ** -0.5
    TB = P // NQ
    NT = NB // TB
    UT = norm.UT
    NU = NT // UT
    UTOK = UT * P
    CB = TB * NC // P
    JT = NC // P
    HP = INNER // P
    KD = D // P
    DR = DC - P
    assert NQ == DH == DR == 64 and HP * P == BANK and CB * P == BANK

    x_tiles = x.rearrange("(t b) q d -> (b q) t d", b=TB)
    ctx_tiles = ctx_in.rearrange("(t b) (j p) d -> t p (b j) d", b=TB, p=P)

    with ExitStack() as stack:
        def sb(name, shape, dt=F32):
            return stack.enter_context(nc.sbuf_tensor(name, shape, dt))

        def sem(name):
            return stack.enter_context(nc.semaphore(name))

        raw = sb("xa_raw", [P, 8, BANK])
        wq_hi = sb("wq_hi", [P, KD, INNER], F32R)
        wq_lo = sb("wq_lo", [P, KD, INNER], F32R)
        wk_hi = sb("wk_hi", [P, 2, INNER], F32R)
        wk_lo = sb("wk_lo", [P, 2, INNER], F32R)
        wv_hi = sb("wv_hi", [P, 2, INNER], F32R)
        wv_lo = sb("wv_lo", [P, 2, INNER], F32R)
        wo_hi = sb("wo_hi", [P, HP, D], F32R)
        wo_lo = sb("wo_lo", [P, HP, D], F32R)
        bo_all = sb("bo_all", [P, D])

        ctx_nat = [sb(f"ctx_nat{i}", [P, CB, 2 * P]) for i in range(2)]
        ctxT_hi = sb("ctxT_hi", [P, BANK], F32R)
        ctxT_lo = sb("ctxT_lo", [P, BANK], F32R)
        ctxT_rest = sb("ctxT_rest", [P, BANK], F32R)
        kT_hi = sb("kT_hi", [P, HP, BANK], F32R)
        kT_lo = sb("kT_lo", [P, HP, BANK], F32R)
        v_nat = [sb(f"v_nat{i}", [P, CB, INNER]) for i in range(2)]
        xnT_hi = sb("xa_xnT_hi", [P, KD, UTOK], F32R)
        xnT_lo = sb("xa_xnT_lo", [P, KD, UTOK], F32R)
        q_hi = sb("q_hi", [P, HP, UT * TB, P], F32R)
        q_lo = sb("q_lo", [P, HP, UT * TB, P], F32R)
        neg_max = sb("neg_max", [P, TB, HP])
        row_sum = sb("row_sum", [P, TB, HP])
        inv_sum = sb("inv_sum", [P, TB, HP])
        probs = sb("probs", [P, TB, HP, NC])
        probsT = sb("probsT", [P, TB * 2, BANK])
        oT_hi = sb("oT_hi", [P, HP, P], F32R)
        oT_lo = sb("oT_lo", [P, HP, P], F32R)

        score_ps = stack.enter_context(nc.psum_tensor("score_ps", [P, 4, BANK], F32))
        proj_ps = stack.enter_context(nc.psum_tensor("proj_ps", [P, 3, BANK], F32))
        turn_ps = stack.enter_context(nc.psum_tensor("turn_ps", [P, BANK], F32))

        x_here = sem("x_here")
        w_in = [sem(f"w_in_{n}") for n in ("wk", "wq", "wv", "wo")]
        ctx_here = [sem("ctx_here0"), sem("ctx_here1")]
        w_hi_done = sem("w_hi_done")
        w_lo_done = sem("w_lo_done")
        consts_done = sem("xa_consts_done")
        ident_zeroed = sem("ident_zeroed")
        ident_done = sem("ident_done")
        bo_here = sem("bo_here")
        bias_added = sem("xa_bias_added")
        ctx_turned = sem("ctx_turned")
        ctxT_hi_done = sem("ctxT_hi_done")
        ctxT_done = sem("ctxT_done")
        k_full = sem("k_full")
        kT_hi_done = sem("kT_hi_done")
        kT_done = sem("kT_done")
        v_full = sem("v_full")
        v_even_done = sem("v_even_done")
        v_odd_done = sem("v_odd_done")
        xn_turned = sem("xa_xn_turned")
        xnT_hi_done = sem("xa_xnT_hi_done")
        xnT_done = sem("xa_xnT_done")
        q_full = sem("q_full")
        q_hi_done = sem("q_hi_done")
        q_done = sem("q_done")
        score_full = sem("score_full")
        max_done = sem("max_done")
        exp_done = sem("exp_done")
        inv_done = sem("inv_done")
        probs_done = sem("probs_done")
        pt_full = sem("pt_full")
        pt_even_done = sem("pt_even_done")
        pt_odd_done = sem("pt_odd_done")
        o_full = sem("o_full")
        oT_hi_done = sem("oT_hi_done")
        oT_done = sem("oT_done")
        out_full = sem("xa_out_full")
        x_done = sem("xa_x_done")

        NEXT_HERE = 16 * (4 + 2 + 3 + next_inputs[-1].shape[0])
        raw_flat = raw[:, :, :].rearrange("p a n -> p (a n)")
        CONSTS = 2
        CTX_BANK = [2, 0]
        KEY_BANK = [1, 2, 0, 1]
        VALUE_BANK = [2, 0, 1, 2]

        def probsT_bank(t, g):
            if g in (1, 2) and isinstance(t, int) and t == NT - 1:
                return proj_ps[:, g - 1, :]
            return turn_ps[:, :]

        next_turned, next_queries = proj_ps[:, 0, :], proj_ps[:, 2, :]
        WEIGHTS = 4

        block = stack.enter_context(nc.Block())

        weight_views = [(hi[:, :, :], lo[:, :, :], raw[:, 2 * n:2 * n + 2, :], loads) for n, (hi, lo, loads) in
                        enumerate(((wk_hi, wk_lo, 3), (wq_hi, wq_lo, 1), (wv_hi, wv_lo, 3)))]
        weight_views.append((wo_hi[:, :, :], wo_lo[:, :, :], raw[:, 6:8, :].rearrange("p a (b n) -> p (a b) n", b=2), 1))

        def load_split_rows(queue, n, w):
            queue.dma_start(raw[:, 2 * n, :], w[0:P, :]).then_inc(w_in[n], 16)
            for half in range(2):
                queue.dma_start(raw[half * DR:(half + 1) * DR, 2 * n + 1, :], w[P:DC, :]).then_inc(w_in[n], 16)

        @block.sync
        def _(sp):
            def load_ctx(t, buf):
                src = ctx_tiles[bass.ds(t, 1), :, :, :].rearrange("a p m d -> p (a m) d")
                sp.dma_start(ctx_nat[buf][:, :, 0:DC], src).then_inc(ctx_here[buf], 16)
                sp.dma_start(ctx_nat[buf][:, :, DC:2 * P], src[:, :, P:DC]).then_inc(ctx_here[buf], 16)

            def load_x(u):
                sp.dma_start(xres[:, bass.ds(UT * u, UT), :], x_tiles[:, bass.ds(UT * u, UT), :]).then_inc(x_here, 16)

            load_x(0)
            load_ctx(0, 0)
            sp.dma_start(raw[:, 2:4, :], Wq.rearrange("(k p) n -> p k n", p=P)).then_inc(w_in[1], 16)
            load_split_rows(sp, 2, Wv)
            sp.dma_start(weight_views[3][2], Wo.rearrange("(k p) n -> p k n", p=P)).then_inc(w_in[3], 16)
            sp.dma_start(bo_all[:, :], bo.rearrange("(a n) -> a n", a=1).to_broadcast([P, D])).then_inc(bo_here, 16)
            load_ctx(1, 1)
            sp.wait_ge(x_here, 16)
            load_x(1)
            def loads(u):
                for a in range(2):
                    sp.wait_ge(ctxT_done, 4 * u + 2 * a - 2)
                    load_ctx(UT * u + a, a)

            def unit(u):
                loads(u)
                sp.wait_ge(x_here, 16 * u + 16)
                load_x(u + 1)

            parts = linear_attention_loads(sp, raw_flat, next_weights, *next_inputs)
            for n, part in enumerate(parts):
                unit(n + 1)
                sp.wait_ge(w_hi_done, WEIGHTS)
                sp.wait_ge(w_lo_done, WEIGHTS)
                part()
            with sp.Fori(len(parts) + 1, NU - 1) as u:
                unit(u)
            loads(NU - 1)

        @block.gpsimd
        def _(pool):
            nc.gpsimd.memset(ident[:, :], 0.0).then_inc(ident_zeroed, 1)
            pool.wait_ge(ident_zeroed, 1)
            nc.gpsimd.affine_select(out=ident[:, :], in_=ident[:, :], compare_op=ALU.not_equal, fill=1.0,
                                    base=0, pattern=[[-1, P]], channel_multiplier=1).then_inc(ident_done, 1)
            pool.wait_ge(ident_done, 1)

            def rstd_of(u):
                norm.rstd_of(nc, pool, u)

            def normalise(t):
                for b in range(TB):
                    pool.wait_ge(inv_done, TB * t + b + 1)
                    nc.gpsimd.tensor_tensor(probs[:, b, :, :], probs[:, b, :, :],
                                            inv_sum[:, b, :].unsqueeze(2).to_broadcast([P, HP, NC]), ALU.mult
                                            ).then_inc(probs_done, 1)

            def add_bias(u):
                pool.wait_ge(norm.xn_done, UT * u + UT)
                dst = xres[:, bass.ds(UT * u, UT), :]
                nc.gpsimd.tensor_tensor(dst, dst, bo_all[:, :].unsqueeze(1).to_broadcast([P, UT, D]), ALU.add
                                        ).then_inc(bias_added, 1)

            pool.wait_ge(norm.exponent_done, 1)
            rstd_of(0)
            pool.wait_ge(norm.rstd_done, 1)
            for n, q in enumerate((q_hi, q_lo)):
                after(pool, consts_done, n)
                nc.gpsimd.memset(q[:, :, :, :].bitcast(F32), 0.0).then_inc(consts_done, 1)
            pool.wait_ge(consts_done, CONSTS)
            pool.wait_ge(bo_here, 16)
            add_bias(0)
            with pool.Fori(0, NU - 1) as u:
                normalise(UT * u)
                rstd_of(u + 1)
                normalise(UT * u + 1)
                add_bias(u + 1)
            normalise(NT - 2)
            pool.wait_ge(next_norm.exponent_done, 1)
            next_norm.rstd_of(nc, pool, 0)

        @block.scalar
        def _(act):
            def ctxT_of(t):
                act.wait_ge(ctx_turned, 2 * t + 1)
                nc.scalar.activation(ctxT_hi[:, :], proj_ps[:, CTX_BANK[0], :], ACT.Copy).then_inc(ctxT_hi_done, 1)
                act.wait_ge(ctx_turned, 2 * t + 2)
                nc.scalar.activation(ctxT_rest[:, :], proj_ps[:, CTX_BANK[1], :], ACT.Copy).then_inc(ctxT_hi_done, 1)

            def kT_of(t, hp):
                act.wait_ge(k_full, HP * t + hp + 1)
                nc.scalar.activation(kT_hi[:, hp, :], proj_ps[:, KEY_BANK[hp], :], ACT.Copy).then_inc(kT_hi_done, 1)

            def v_of(t, buf, m):
                act.wait_ge(v_full, CB * t + m + 1)
                nc.scalar.activation(v_nat[buf][:, m, :], proj_ps[:, VALUE_BANK[m], :], ACT.Copy).then_inc(v_even_done, 1)

            def xnT_of(u):
                act.wait_ge(xn_turned, u + 1)
                nc.scalar.activation(xnT_hi[:, :, :].rearrange("p k n -> p (k n)"), turn_ps[:, :], ACT.Copy
                                     ).then_inc(xnT_hi_done, 1)

            def q_of(u, g):
                act.wait_ge(q_full, 2 * u + g + 1)
                src = turn_ps[:, :].rearrange("p (c i) -> p c i", i=NQ)
                for h in range(2):
                    rows = slice(h * DH, (h + 1) * DH)
                    dst = q_hi[rows, 2 * g:2 * g + 2, :, h * NQ:(h + 1) * NQ].rearrange("p a c i -> p (a c) i")
                    nc.scalar.activation(dst, src[rows], ACT.Copy, scale=SCALE).then_inc(q_hi_done, 1)

            def exp_of(t, b, hp):
                act.wait_ge(max_done, 4 * t + 2 * b + hp // 2 + 1)
                nc.scalar.activation(probs[:, b, hp, :], score_ps[:, 2 * b + hp // 2, (hp % 2) * NC:(hp % 2 + 1) * NC],
                                     ACT.Exp, bias=neg_max[:, b, hp:hp + 1], accum_out=row_sum[:, b, hp:hp + 1]
                                     ).then_inc(exp_done, 1)

            def probsT_of(t, g):
                act.wait_ge(pt_full, 4 * t + g + 1)
                nc.scalar.activation(probsT[:, g, :], probsT_bank(t, g), ACT.Copy).then_inc(pt_even_done, 1)

            def oT_of(t):
                for b in range(TB):
                    act.wait_ge(o_full, TB * t + b + 1)
                    for h in range(2):
                        rows = slice(h * DH, (h + 1) * DH)
                        src = score_ps[rows, b, :].rearrange("p (a n) -> p a n", n=P)[:, :, h * NQ:(h + 1) * NQ]
                        nc.scalar.activation(oT_hi[rows, :, b * NQ:(b + 1) * NQ], src, ACT.Copy).then_inc(oT_hi_done, 1)

            def weight_hi(n):
                hi, _, src, loads = weight_views[n]
                act.wait_ge(w_in[n], 16 * loads)
                nc.scalar.activation(hi, src, ACT.Copy).then_inc(w_hi_done, 1)

            load_split_rows(act, 0, Wk)
            weight_hi(0)
            ctxT_of(0)
            xnT_of(0)
            weight_hi(1)
            kT_of(0, 0)
            kT_of(0, 1)
            weight_hi(2)
            act.wait_ge(consts_done, CONSTS)
            q_of(0, 0)
            kT_of(0, 2)
            weight_hi(3)
            kT_of(0, 3)
            q_of(0, 1)
            v_of(0, 0, 0)
            v_of(0, 0, 2)

            def tile(u, a, last):
                t = UT * u + a
                nxt = (a + 1) % 2
                more = not (last and a == 1)
                if more:
                    ctxT_of(t + 1)
                for hp in range(HP):
                    if a == 1 and hp == 2:
                        if last:
                            next_tokens.hi_of(nc, act, 0, next_turned)
                        else:
                            xnT_of(u + 1)
                    exp_of(t, 0, hp)
                if more:
                    kT_of(t + 1, 0)
                if not last and a == 1:
                    q_of(u + 1, 0)
                exp_of(t, 1, 0)
                if more:
                    kT_of(t + 1, 1)
                exp_of(t, 1, 1)
                if more:
                    kT_of(t + 1, 2)
                if not last and a == 1:
                    q_of(u + 1, 1)
                exp_of(t, 1, 2)
                exp_of(t, 1, 3)
                if more:
                    kT_of(t + 1, 3)
                    v_of(t + 1, nxt, 0)
                if last and a == 1:
                    next_tokens.q_hi_of(nc, act, next_weights, 0, next_queries)
                probsT_of(t, 0)
                if more:
                    v_of(t + 1, nxt, 2)
                probsT_of(t, 2)
                if last and a == 0:
                    split_linear_attention_hi(nc, act, raw_flat, next_weights, NEXT_HERE)
                oT_of(t)

            tile(0, 0, False)
            tile(0, 1, False)
            with act.Fori(1, NU - 1) as u:
                tile(u, 0, False)
                tile(u, 1, False)
            tile(NU - 1, 0, True)
            tile(NU - 1, 1, True)

        @block.vector
        def _(dve):
            def moments_of(u):
                dve.wait_ge(x_here, 16 * u + 16)
                norm.moments_of(nc, dve, xres, u)

            def xn_of(u):
                norm.xn_of(nc, dve, xres, u)

            def ctxT_of(t):
                dve.wait_ge(ctxT_hi_done, 2 * t + 1)
                nc.vector.tensor_tensor(ctxT_lo[:, :], proj_ps[:, CTX_BANK[0], :], ctxT_hi[:, :].bitcast(F32), ALU.subtract
                                        ).then_inc(ctxT_done, 1)
                dve.wait_ge(ctxT_hi_done, 2 * t + 2)
                nc.vector.tensor_tensor(ctxT_rest[DR:P, :], proj_ps[DR:P, CTX_BANK[1], :], ctxT_rest[DR:P, :].bitcast(F32),
                                        ALU.subtract).then_inc(ctxT_done, 1)

            def kT_of(t, hp):
                dve.wait_ge(kT_hi_done, HP * t + hp + 1)
                nc.vector.tensor_tensor(kT_lo[:, hp, :], proj_ps[:, KEY_BANK[hp], :], kT_hi[:, hp, :].bitcast(F32),
                                        ALU.subtract).then_inc(kT_done, 1)

            def v_of(t, buf, m):
                dve.wait_ge(v_full, CB * t + m + 1)
                nc.vector.tensor_copy(v_nat[buf][:, m, :], proj_ps[:, VALUE_BANK[m], :]).then_inc(v_odd_done, 1)

            def xnT_of(u):
                dve.wait_ge(xnT_hi_done, u + 1)
                nc.vector.tensor_tensor(xnT_lo[:, :, :].rearrange("p k n -> p (k n)"), turn_ps[:, :],
                                        xnT_hi[:, :, :].rearrange("p k n -> p (k n)").bitcast(F32), ALU.subtract
                                        ).then_inc(xnT_done, 1)

            def q_of(u, g):
                src = turn_ps[:, :].rearrange("p (c i) -> p c i", i=NQ)
                for h in range(2):
                    rows = slice(h * DH, (h + 1) * DH)
                    part = [q[rows, 2 * g:2 * g + 2, :, h * NQ:(h + 1) * NQ].rearrange("p a c i -> p (a c) i")
                            for q in (q_hi, q_lo)]
                    dve.wait_ge(q_hi_done, 4 * u + 2 * g + h + 1)
                    nc.vector.scalar_tensor_tensor(out=part[1], in0=src[rows], scalar=SCALE, in1=part[0].bitcast(F32),
                                                   op0=ALU.mult, op1=ALU.subtract).then_inc(q_done, 1)

            def max_of(t, n):
                dve.wait_ge(score_full, 4 * t + n + 1)
                nc.vector.tensor_reduce(neg_max[:, n // 2, 2 * (n % 2):2 * (n % 2) + 2],
                                        score_ps[:, n, :].rearrange("p (h j) -> p h j", j=NC), AX.X, ALU.max,
                                        negate=True).then_inc(max_done, 1)

            def inverse_of(t, b):
                dve.wait_ge(exp_done, TB * HP * t + HP * (b + 1))
                nc.vector.reciprocal(inv_sum[:, b, :], row_sum[:, b, :]).then_inc(inv_done, 1)
                if isinstance(t, int) and t == NT - 1:
                    dve.wait_ge(inv_done, TB * t + b + 1)
                    nc.vector.tensor_tensor(probs[:, b, :, :], probs[:, b, :, :],
                                            inv_sum[:, b, :].unsqueeze(2).to_broadcast([P, HP, NC]), ALU.mult
                                            ).then_inc(probs_done, 1)

            def probsT_of(t, g):
                dve.wait_ge(pt_full, 4 * t + g + 1)
                nc.vector.tensor_copy(probsT[:, g, :], probsT_bank(t, g)).then_inc(pt_odd_done, 1)

            def oT_of(t):
                for b in range(TB):
                    for h in range(2):
                        rows = slice(h * DH, (h + 1) * DH)
                        cols = slice(b * NQ, (b + 1) * NQ)
                        src = score_ps[rows, b, :].rearrange("p (a n) -> p a n", n=P)[:, :, h * NQ:(h + 1) * NQ]
                        dve.wait_ge(oT_hi_done, 2 * TB * t + 2 * b + h + 1)
                        nc.vector.tensor_tensor(oT_lo[rows, :, cols], src, oT_hi[rows, :, cols].bitcast(F32),
                                                ALU.subtract).then_inc(oT_done, 1)

            def x_of(t, u, first_of_unit=False):
                dve.wait_ge(out_full, t + 1)
                if first_of_unit:
                    dve.wait_ge(bias_added, u + 1)
                dst = slot(xres, t)
                nc.vector.tensor_tensor(dst, turn_ps[:, 0:D].unsqueeze(1), dst, ALU.add).then_inc(x_done, 1)

            norm.set_exponent(nc)
            next_norm.set_exponent(nc)
            moments_of(0)
            xn_of(0)
            def weight_lo(n):
                hi, lo, src, loads = weight_views[n]
                dve.wait_ge(w_in[n], 16 * loads)
                dve.wait_ge(w_hi_done, n + 1)
                nc.vector.tensor_tensor(lo, src, hi.bitcast(F32), ALU.subtract).then_inc(w_lo_done, 1)

            weight_lo(0)
            ctxT_of(0)
            xnT_of(0)
            weight_lo(1)
            kT_of(0, 0)
            kT_of(0, 1)
            weight_lo(2)
            dve.wait_ge(consts_done, CONSTS)
            q_of(0, 0)
            kT_of(0, 2)
            weight_lo(3)
            kT_of(0, 3)
            q_of(0, 1)
            v_of(0, 0, 1)
            v_of(0, 0, 3)

            def tile(u, a, last):
                t = UT * u + a
                nxt = (a + 1) % 2
                more = not (last and a == 1)
                if more:
                    ctxT_of(t + 1)
                max_of(t, 0)
                if not (isinstance(t, int) and t == 0):
                    if a == 0:
                        x_of(t - 1, u - 1)
                    else:
                        x_of(t - 1, u, True)
                if last and a == 1:
                    next_norm.xn_of(nc, dve, xres, 0)
                max_of(t, 1)
                max_of(t, 2)
                if a == 1:
                    if last:
                        next_tokens.lo_of(nc, dve, 0, next_turned)
                    else:
                        xnT_of(u + 1)
                max_of(t, 3)
                if more:
                    kT_of(t + 1, 0)
                if not last and a == 1:
                    q_of(u + 1, 0)
                inverse_of(t, 0)
                if more:
                    kT_of(t + 1, 1)
                    kT_of(t + 1, 2)
                if not last and a == 1:
                    q_of(u + 1, 1)
                inverse_of(t, 1)
                if more:
                    kT_of(t + 1, 3)
                if more:
                    v_of(t + 1, nxt, 1)
                probsT_of(t, 1)
                if last and a == 1:
                    next_tokens.q_lo_of(nc, dve, next_weights, 0, next_queries)
                if not last and a == 0:
                    moments_of(u + 1)
                if more:
                    v_of(t + 1, nxt, 3)
                probsT_of(t, 3)
                if last and a == 1:
                    split_linear_attention_lo(nc, dve, raw_flat, next_weights, NEXT_HERE, (2, 3))
                if not last and a == 0:
                    xn_of(u + 1)
                if last and a == 0:
                    next_norm.moments_of(nc, dve, xres, 0)
                    split_linear_attention_lo(nc, dve, raw_flat, next_weights, NEXT_HERE, (0, 1))
                oT_of(t)
                if last and a == 1:
                    split_linear_attention_lo(nc, dve, raw_flat, next_weights, NEXT_HERE, (4,))

            tile(0, 0, False)
            zero_linear_attention(nc, raw_flat, next_weights)
            tile(0, 1, False)
            with dve.Fori(1, NU - 1) as u:
                tile(u, 0, False)
                tile(u, 1, False)
            tile(NU - 1, 0, True)
            tile(NU - 1, 1, True)
            x_of(NT - 1, NU - 1)

        @block.tensor
        def _(pe):
            def products(out, pairs):
                for n, (w, m) in enumerate(pairs):
                    ins = nc.tensor.matmul(out, w, m, start=n == 0, stop=n == len(pairs) - 1)
                return ins

            def turn_ctx(u, buf):
                t = UT * u + buf
                pe.wait_ge(ctx_here[buf], 32 * u + 32)
                after(pe, v_odd_done, 2 * t)
                for m in range(CB):
                    ins = nc.tensor.transpose(proj_ps[:, CTX_BANK[0], m * P:(m + 1) * P], ctx_nat[buf][:, m, 0:P], ident[:, :])
                ins.then_inc(ctx_turned, 1)
                for m in range(CB):
                    ins = nc.tensor.transpose(proj_ps[:, CTX_BANK[1], m * P:(m + 1) * P], ctx_nat[buf][:, m, P:2 * P], ident[:, :])
                ins.then_inc(ctx_turned, 1)

            def context_pairs(hi, lo, moving_context, cols):
                pairs = [(ctxT_hi, hi[:, 0, :]), (ctxT_lo, hi[:, 0, :]), (ctxT_hi, lo[:, 0, :]),
                         (ctxT_rest, hi[:, 1, :]), (ctxT_rest, lo[:, 1, :])]
                return [(w[:, cols], c[:, :]) if moving_context else (c[:, cols], w) for c, w in pairs]

            def keys(t, hp):
                if hp == 0:
                    pe.wait_ge(ctxT_done, 2 * t + 2)
                if hp == 0:
                    after(pe, v_even_done, 2 * t)
                elif hp == 3:
                    pe.wait_ge(kT_done, HP * t + 1)
                products(proj_ps[:, KEY_BANK[hp], :], context_pairs(wk_hi, wk_lo, True, slice(hp * P, (hp + 1) * P))
                         ).then_inc(k_full, 1)

            def values(t, m):
                if m < 3:
                    pe.wait_ge(kT_done, HP * t + m + 2)
                else:
                    pe.wait_ge(v_even_done, 2 * t + 1)
                products(proj_ps[:, VALUE_BANK[m], :], context_pairs(wv_hi, wv_lo, False, slice(m * P, (m + 1) * P))
                         ).then_inc(v_full, 1)

            def turn_xn(u):
                pe.wait_ge(norm.xn_done, UT * u + UT)
                after(pe, x_done, UT * u - 1)
                for k in range(KD):
                    for a in range(UT):
                        c = k * UTOK + a * P
                        ins = nc.tensor.transpose(turn_ps[:, c:c + P], norm.xn[:, a, k * P:(k + 1) * P], ident[:, :])
                ins.then_inc(xn_turned, 1)

            def queries(u, g):
                if g == 0:
                    pe.wait_ge(xnT_done, u + 1)
                else:
                    pe.wait_ge(q_done, 4 * u + 2)
                for i in range(2):
                    cols = slice((2 * g + i) * P, (2 * g + i + 1) * P)
                    ins = products(turn_ps[:, i * UTOK:(i + 1) * UTOK],
                                   [(w[:, k, cols], m[:, k, :]) for k in range(KD)
                                    for w, m in ((wq_hi, xnT_hi), (wq_hi, xnT_lo), (wq_lo, xnT_hi))])
                ins.then_inc(q_full, 1)

            def scores(u, a, n):
                t, b = UT * u + a, n // 2
                if n == 0:
                    pe.wait_ge(q_done, 4 * u + 4)
                    pe.wait_ge(kT_done, HP * t + HP)
                if n < TB:
                    after(pe, oT_done, 2 * TB * (t - 1) + 2 * n + 2)
                for i in range(2):
                    hp = 2 * (n % 2) + i
                    ins = products(score_ps[:, n, i * NC:(i + 1) * NC],
                                   [(q[:, hp, TB * a + b, :], k[:, hp, b * NC:(b + 1) * NC])
                                    for q, k in ((q_hi, kT_hi), (q_lo, kT_hi), (q_hi, kT_lo))])
                ins.then_inc(score_full, 1)

            def turn_probs(t, g):
                b = g // 2
                if g % 2 == 0:
                    pe.wait_ge(probs_done, TB * t + b + 1)
                if g == 0:
                    after(pe, x_done, t)
                elif isinstance(t, int) and t == NT - 1:
                    if g == 3:
                        pe.wait_ge(pt_even_done, 2 * t + 1)
                else:
                    pe.wait_ge(pt_even_done if g % 2 else pt_odd_done, 2 * t + (g + 1) // 2)
                for i in range(2):
                    for j in range(JT):
                        c = (2 * i + j) * P
                        ins = nc.tensor.transpose(probsT_bank(t, g)[:, c:c + P],
                                                  probs[:, b, 2 * (g % 2) + i, j * P:(j + 1) * P], ident[:, :])
                ins.then_inc(pt_full, 1)

            def mix_values(t, buf):
                pe.wait_ge(v_even_done, 2 * t + 2)
                pe.wait_ge(v_odd_done, 2 * t + 2)
                for b in range(TB):
                    pe.wait_ge(pt_even_done, 2 * t + b + 1)
                    pe.wait_ge(pt_odd_done, 2 * t + b + 1)
                    for hp in range(HP):
                        ins = products(score_ps[:, b, hp * P:(hp + 1) * P],
                                       [(v_nat[buf][:, JT * b + j, hp * P:(hp + 1) * P],
                                         probsT[:, 2 * b + hp // 2, (2 * (hp % 2) + j) * P:(2 * (hp % 2) + j + 1) * P])
                                        for j in range(JT)])
                    ins.then_inc(o_full, 1)

            def project_out(t):
                pe.wait_ge(oT_done, 2 * TB * t + 2 * TB)
                products(turn_ps[:, 0:D],
                         [(o[:, hp, :], w[:, hp, :]) for hp in range(HP)
                          for o, w in ((oT_hi, wo_hi), (oT_lo, wo_hi), (oT_hi, wo_lo))]).then_inc(out_full, 1)

            pe.wait_ge(ident_done, 1)
            turn_ctx(0, 0)
            turn_xn(0)
            pe.wait_ge(w_lo_done, 1)
            keys(0, 0)
            keys(0, 1)
            pe.wait_ge(w_lo_done, 2)
            queries(0, 0)
            keys(0, 2)
            keys(0, 3)
            queries(0, 1)
            pe.wait_ge(w_lo_done, 3)
            for m in range(CB):
                values(0, m)

            pe.wait_ge(w_lo_done, WEIGHTS)

            def tile(u, a, last):
                t = UT * u + a
                more = not (last and a == 1)
                if more:
                    turn_ctx(u + (a + 1) // 2, (a + 1) % 2)
                scores(u, a, 0)
                if not (isinstance(t, int) and t == 0):
                    project_out(t - 1)
                scores(u, a, 1)
                scores(u, a, 2)
                if a == 1:
                    if last:
                        pe.wait_ge(v_even_done, 2 * NT)
                        pe.wait_ge(v_odd_done, 2 * NT)
                        next_tokens.turn(nc, pe, next_norm, ident, 0, next_turned)
                    else:
                        turn_xn(u + 1)
                scores(u, a, 3)
                if last and a == 1:
                    pe.wait_ge(next_weights["lo_done"], 1)
                    next_tokens.queries(nc, pe, next_weights, 0, next_queries)
                if more:
                    keys(t + 1, 0)
                if not last and a == 1:
                    queries(u + 1, 0)
                if more:
                    keys(t + 1, 1)
                    keys(t + 1, 2)
                if not last and a == 1:
                    queries(u + 1, 1)
                if more:
                    keys(t + 1, 3)
                for g in range(4):
                    if more:
                        values(t + 1, g)
                    if g == 0 and not last and a == 1:
                        pe.wait_ge(q_done, 4 * u + 8)
                    turn_probs(t, g)
                mix_values(t, a)

            tile(0, 0, False)
            tile(0, 1, False)
            with pe.Fori(1, NU - 1) as u:
                tile(u, 0, False)
                tile(u, 1, False)
            tile(NU - 1, 0, True)
            tile(NU - 1, 1, True)
            project_out(NT - 1)


MOE_LANE = 32


def mixture_weights(nc, stack, raw_stack, E, D, H):
    KD, KH = D // P, H // P
    w = {}

    def sb(name, shape, dt=F32, until=stack):
        w[name] = until.enter_context(nc.sbuf_tensor("moe_" + name, shape, dt))

    for part in ("hi", "lo"):
        sb("win_" + part, [P, E, KD, H], F32R)
        sb("wout_" + part, [P, E, KH, D], F32R)
    sb("raw_router", [P, KD, E])
    sb("router", [P, KD, 2 * E], F32R)
    sb("b_in_cols", [P, E, KH])
    sb("b_out_raw", [P, D])
    sb("b_out_rows", [P, D], F32R)
    sb("raw_in", [P, 2, KD, H], until=raw_stack)
    sb("raw_out", [P, 2, KH, D], until=raw_stack)
    for name in ("here", "zeroed", "hi_done", "lo_done", "small_hi_done", "small_lo_done"):
        w[name] = stack.enter_context(nc.semaphore("moe_w_" + name))
    w["expert_here"] = [stack.enter_context(nc.semaphore(f"moe_w_expert_here{i}")) for i in range(2)]
    w["HERE"] = 16 * (E + KD + 3)
    return w


def load_mixture(sp, w, router_w, w_in, b_in, w_out, b_out):
    E, KD = w_in.shape[0], w_in.shape[1] // P
    for k in range(KD):
        sp.dma_start(w["raw_router"][:, k, :], router_w[k * P:(k + 1) * P, :]).then_inc(w["here"], 16)
    for e in range(E):
        sp.dma_start(w["b_in_cols"][:, e, :], b_in[e].rearrange("(k p) -> p k", p=P),
                     allow_slow_non_contiguous=True).then_inc(w["here"], 16)
    sp.wait_ge(w["zeroed"], 1)
    for n in range(3):
        sp.dma_start(w["b_out_raw"][n * MOE_LANE:n * MOE_LANE + E, :], b_out).then_inc(w["here"], 16)
    for e in range(E):
        after(sp, w["lo_done"], 2 * (e - 1))
        for raw, src in (("raw_in", w_in), ("raw_out", w_out)):
            sp.dma_start(w[raw][:, e % 2, :, :], src[e].rearrange("(k p) n -> p k n", p=P)
                         ).then_inc(w["expert_here"][e % 2], 16)


def split_expert_hi(nc, act, w, pair, i):
    act.wait_ge(w["expert_here"][i], 32 * pair + 32)
    for part, raw in (("win_hi", "raw_in"), ("wout_hi", "raw_out")):
        nc.scalar.activation(w[part][:, bass.ds(2 * pair + i, 1), :, :].rearrange("p e k n -> p (e k n)"),
                             w[raw][:, i, :, :].rearrange("p k n -> p (k n)"), ACT.Copy).then_inc(w["hi_done"], 1)


def split_expert_lo(nc, pool, w, pair, i):
    e = 2 * pair + i
    for n, (hi, lo, raw) in enumerate((("win_hi", "win_lo", "raw_in"), ("wout_hi", "wout_lo", "raw_out"))):
        pool.wait_ge(w["hi_done"], 2 * e + n + 1)
        lo_view, hi_view = (w[name][:, bass.ds(e, 1), :, :].rearrange("p e k n -> p (e k n)") for name in (lo, hi))
        nc.gpsimd.tensor_tensor(lo_view, w[raw][:, i, :, :].rearrange("p k n -> p (k n)"), hi_view.bitcast(F32),
                                ALU.subtract).then_inc(w["lo_done"], 1)


def split_small_hi(nc, act, w):
    E = w["raw_router"].shape[2]
    act.wait_ge(w["here"], w["HERE"])
    nc.scalar.activation(w["router"][:, :, 0:E], w["raw_router"][:, :, :], ACT.Copy).then_inc(w["small_hi_done"], 1)
    act.wait_ge(w["zeroed"], 1)
    nc.scalar.activation(w["b_out_rows"][:, :], w["b_out_raw"][:, :], ACT.Copy).then_inc(w["small_hi_done"], 1)


def split_small_lo(nc, dve, w):
    E = w["raw_router"].shape[2]
    dve.wait_ge(w["small_hi_done"], 2)
    nc.vector.tensor_tensor(w["router"][:, :, E:2 * E], w["raw_router"][:, :, :], w["router"][:, :, 0:E].bitcast(F32),
                            ALU.subtract).then_inc(w["small_lo_done"], 1)
    rows = slice(2 * MOE_LANE, 3 * MOE_LANE)
    nc.vector.tensor_tensor(w["b_out_rows"][rows, :], w["b_out_raw"][rows, :], w["b_out_rows"][rows, :].bitcast(F32),
                            ALU.subtract).then_inc(w["small_lo_done"], 1)


def linear_attention(nc, weights, D, H, DK, F, xres, ident, norm, tokens, next_norm, next_weights, next_inputs, next_tokens):
    NT = xres.shape[1]
    UT = norm.UT
    NU = NT // UT
    UTOK = UT * P
    TB = 2
    ROWS = P // TB
    KD = D // P
    HP = H // 2
    GP = HP // KD
    DV = DK + 1
    PAIR = TB * 2 * DV
    assert GP * P == BANK and 2 * F == P and KD * UTOK == BANK

    with ExitStack() as stack:
        def sb(name, shape, dt=F32):
            return stack.enter_context(nc.sbuf_tensor("la_" + name, shape, dt))

        def sem(name):
            return stack.enter_context(nc.semaphore("la_" + name))

        split = {n: (weights[n + "_hi"], weights[n + "_lo"]) for n in ("wq", "wk", "wv", "wo")}
        rw_hi, rw_lo = weights["rw_hi"], weights["rw_lo"]
        bias_cols, bias_rows = weights["bias_cols"], weights["bias_rows"]
        ones_rows = sb("ones_rows", [P, P], F32R)

        qk_hi = [tokens.q_hi, sb("k_hi", [P, KD, UTOK], F32R)]
        qk_lo = [tokens.q_lo, sb("k_lo", [P, KD, UTOK], F32R)]
        v_ones = sb("v_ones", [P, UT, HP, TB, 2, DV])
        k_feat = sb("k_feat", [P, UT, KD, BANK])
        q_feat = sb("q_feat", [P, HP, UTOK])
        kv = sb("kv", [P, UT, HP, TB, 2, DV])
        den = sb("den", [P, UT, H])
        inv_den = sb("inv_den", [P, UT, H])
        o_nat = sb("o_nat", [P, UT, D])
        oT_hi = sb("oT_hi", [P, UT, KD, P], F32R)
        oT_lo = sb("oT_lo", [P, UT, KD, P], F32R)

        turn_ps = stack.enter_context(nc.psum_tensor("la_turn_ps", [P, BANK], F32))
        q_ps = stack.enter_context(nc.psum_tensor("la_q_ps", [P, BANK], F32))
        k_ps = stack.enter_context(nc.psum_tensor("la_k_ps", [P, BANK], F32))
        feat_ps = stack.enter_context(nc.psum_tensor("la_feat_ps", [P, 2, BANK], F32))
        sum_ps = stack.enter_context(nc.psum_tensor("la_sum_ps", [P, 2, BANK], F32))
        ends_ps = stack.enter_context(nc.psum_tensor("la_ends_ps", [P, BANK], F32))

        consts_done = sem("consts_done")
        k_full = sem("k_full")
        k_hi_done = sem("k_hi_done")
        k_done = sem("k_done")
        v_full = sem("v_full")
        v_done = sem("v_done")
        feat_full = sem("feat_full")
        feat_done = sem("feat_done")
        kv_full = sem("kv_full")
        kv_done = sem("kv_done")
        num_full = sem("num_full")
        den_done = sem("den_done")
        inv_done = sem("inv_done")
        o_done = sem("o_done")
        o_turned = sem("o_turned")
        oT_hi_done = sem("oT_hi_done")
        oT_done = sem("oT_done")
        out_full = sem("out_full")
        bias_added = sem("bias_added")
        x_done = sem("x_done")

        CONSTS = 3 + 2 + UT * TB
        FEATS = 2 * UT + HP // 2
        block = stack.enter_context(nc.Block())

        token_banks = [turn_ps[:, :], k_ps[:, :]]
        E = next_inputs[1].shape[0]
        assert E + 1 < NU - 1

        @block.sync
        def _(sp):
            load_mixture(sp, next_weights, *next_inputs)

        @block.gpsimd
        def _(pool):
            def rstd_of(u):
                norm.rstd_of(nc, pool, u)

            def add_bias(u):
                pool.wait_ge(norm.xn_done, UT * u + UT)
                dst = xres[:, bass.ds(UT * u, UT), :]
                nc.gpsimd.tensor_tensor(dst, dst, weights["bo_all"][:, :].unsqueeze(1).to_broadcast([P, UT, D]), ALU.add
                                        ).then_inc(bias_added, 1)

            fills = [(ones_rows[:, :].bitcast(F32), 0.0)]
            fills += [(ones_rows[row:row + 1, :].bitcast(F32), 1.0) for row in (0, 32)]
            fills.append((v_ones[:, :, :, :, :, :].rearrange("p a c b h d -> p (a c b h d)"), 0.0))
            fills += [(v_ones[b * ROWS:(b + 1) * ROWS, a, :, b, :, DK:DV], 1.0) for a in range(UT) for b in range(TB)]
            fills.append((kv[:, :, :, :, :, :].rearrange("p a c b h d -> p (a c b h d)"), 0.0))
            for n, (dst, value) in enumerate(fills):
                after(pool, consts_done, n)
                nc.gpsimd.memset(dst, value).then_inc(consts_done, 1)
            pool.wait_ge(consts_done, CONSTS)
            add_bias(0)
            rstd_of(1)
            add_bias(1)
            with pool.Fori(0, E // 2) as pair:
                for i in range(2):
                    rstd_of(2 * pair + i + 2)
                    add_bias(2 * pair + i + 2)
                    split_expert_lo(nc, pool, next_weights, pair, i)
            pool.wait_ge(next_weights["lo_done"], 2 * E)
            with pool.Fori(E + 2, NU) as u:
                rstd_of(u)
                add_bias(u)
            pool.wait_ge(next_norm.exponent_done, 1)
            next_norm.rstd_of(nc, pool, 0)

        @block.scalar
        def _(act):
            def xnT_of(u):
                tokens.hi_of(nc, act, u, turn_ps[:, :])

            def qk_of(u, i):
                if i == 0:
                    return tokens.q_hi_of(nc, act, weights, u, q_ps[:, :])
                act.wait_ge(k_full, u + 1)
                for k in range(KD):
                    nc.scalar.activation(qk_hi[1][:, k, :], k_ps[:, k * UTOK:(k + 1) * UTOK], ACT.Identity,
                                         bias=bias_cols[:, 1, k:k + 1]).then_inc(k_hi_done, 1)

            def v_of(u):
                act.wait_ge(v_full, u + 1)
                for a in range(UT):
                    for b in range(TB):
                        rows = slice(b * ROWS, (b + 1) * ROWS)
                        src = ends_ps[rows, a * D:(a + 1) * D].rearrange("p (c h d) -> p c h d", h=2, d=DK)
                        nc.scalar.activation(v_ones[rows, a, :, b, :, 0:DK], src, ACT.Copy).then_inc(v_done, 1)

            def kv_of(t, a):
                act.wait_ge(kv_full, t + 1)
                for h in range(2):
                    rows = slice(h * F, (h + 1) * F)
                    src = sum_ps[rows, :, 0:GP * PAIR].rearrange("p g (c n) -> p g c n", n=2 * DV)[:, :, :, h * DV:(h + 1) * DV]
                    dst = kv[rows, a, :, :, h, :].rearrange("p (g c) b d -> p g (c b) d", g=2)
                    nc.scalar.activation(dst, src, ACT.Copy).then_inc(kv_done, 1)

            def oT_of(t, a):
                act.wait_ge(o_turned, t + 1)
                nc.scalar.activation(oT_hi[:, a, :, :].rearrange("p k n -> p (k n)"), (turn_ps, q_ps)[a][:, 0:D],
                                     ACT.Copy).then_inc(oT_hi_done, 1)

            qk_of(0, 1)
            act.wait_ge(consts_done, CONSTS)
            v_of(0)

            def unit(u, first, last):
                if not first:
                    oT_of(UT * u - 1, 1)
                kv_of(UT * u, 0)
                if not last:
                    xnT_of(u + 1)
                kv_of(UT * u + 1, 1)
                if last:
                    next_tokens.hi_of(nc, act, 0, 0, token_banks)
                    act.wait_ge(next_tokens.zeroed, 1)
                    next_tokens.logitsT_of(nc, act, 0, token_banks[1])
                else:
                    qk_of(u + 1, 0)
                    qk_of(u + 1, 1)
                oT_of(UT * u, 0)
                if not last:
                    v_of(u + 1)

            unit(0, True, False)
            with act.Fori(0, E // 2) as pair:
                for i in range(2):
                    unit(2 * pair + i + 1, False, False)
                    split_expert_hi(nc, act, next_weights, pair, i)
            split_small_hi(nc, act, next_weights)
            with act.Fori(E + 1, NU - 1) as u:
                unit(u, False, False)
            unit(NU - 1, False, True)
            oT_of(UT * NU - 1, 1)

        @block.vector
        def _(dve):
            def moments_of(u):
                norm.moments_of(nc, dve, xres, u)

            def xn_of(u):
                norm.xn_of(nc, dve, xres, u)

            def xnT_of(u):
                tokens.lo_of(nc, dve, u, turn_ps[:, :])

            def qk_of(u, i):
                if i == 0:
                    return tokens.q_lo_of(nc, dve, weights, u, q_ps[:, :])
                dve.wait_ge(k_hi_done, KD * u + KD)
                for k in range(KD):
                    nc.vector.scalar_tensor_tensor(out=qk_lo[1][:, k, :], in0=k_ps[:, k * UTOK:(k + 1) * UTOK],
                                                   scalar=bias_cols[:, 1, k:k + 1], in1=qk_hi[1][:, k, :].bitcast(F32),
                                                   op0=ALU.add, op1=ALU.subtract).then_inc(k_done, 1)

            def feat_of(u, n, dst):
                dve.wait_ge(feat_full, FEATS * u + n + 1)
                nc.vector.tensor_scalar(dst, feat_ps[:, n % 2, :], 0.0, PHI_EPS, ALU.max, ALU.add).then_inc(feat_done, 1)

            def k_feat_of(u, a):
                for k in range(KD):
                    feat_of(u, KD * a + k, k_feat[:, a, k, :])

            def q_feat_of(u, c):
                feat_of(u, UT * KD + c, q_feat[:, 2 * c:2 * c + 2, :].rearrange("p c n -> p (c n)"))

            def divide(t, a):
                dve.wait_ge(num_full, t + 1)
                for b in range(TB):
                    rows = slice(b * ROWS, (b + 1) * ROWS)
                    src = sum_ps[rows, :, 0:GP * PAIR].rearrange("p g (c b h d) -> p g c b h d", b=TB, h=2, d=DV)
                    nc.vector.tensor_scalar(den[rows, a, :].rearrange("p (g c h) -> p g c h", g=2, h=2),
                                            src[:, :, :, b, :, DK], PHI_EPS, None, ALU.add).then_inc(den_done, 1)
                dve.wait_ge(den_done, TB * t + TB)
                nc.vector.reciprocal(inv_den[:, a, :], den[:, a, :]).then_inc(inv_done, 1)
                dve.wait_ge(inv_done, t + 1)
                for b in range(TB):
                    rows = slice(b * ROWS, (b + 1) * ROWS)
                    for g in range(2):
                        src = sum_ps[rows, g, 0:GP * PAIR].rearrange("p (c b h d) -> p c b h d", b=TB, h=2, d=DV)
                        inv = inv_den[rows, a, g * 2 * GP:(g + 1) * 2 * GP].rearrange("p (c h) -> p c h", h=2)
                        dst = o_nat[rows, a, g * P:(g + 1) * P].rearrange("p (c h d) -> p c h d", h=2, d=DK)
                        nc.vector.tensor_tensor(dst, src[:, :, b, :, 0:DK], inv.unsqueeze(3).to_broadcast([ROWS, GP, 2, DK]),
                                                ALU.mult).then_inc(o_done, 1)

            def oT_of(t, a):
                dve.wait_ge(oT_hi_done, t + 1)
                nc.vector.tensor_tensor(oT_lo[:, a, :, :].rearrange("p k n -> p (k n)"), (turn_ps, q_ps)[a][:, 0:D],
                                        oT_hi[:, a, :, :].rearrange("p k n -> p (k n)").bitcast(F32), ALU.subtract
                                        ).then_inc(oT_done, 1)

            def x_of(u):
                dve.wait_ge(out_full, u + 1)
                dve.wait_ge(bias_added, u + 1)
                dst = xres[:, bass.ds(UT * u, UT), :]
                nc.vector.tensor_tensor(dst, ends_ps[:, :].rearrange("p (a n) -> p a n", a=UT), dst, ALU.add
                                        ).then_inc(x_done, 1)

            next_norm.set_exponent(nc)
            next_tokens.zero(nc)
            qk_of(0, 1)

            def unit(u, first, last):
                k_feat_of(u, 0)
                if not first:
                    oT_of(UT * u - 1, 1)
                k_feat_of(u, 1)
                if last:
                    next_norm.moments_of(nc, dve, xres, 0)
                else:
                    moments_of(u + 1)
                    xn_of(u + 1)
                q_feat_of(u, 0)
                q_feat_of(u, 1)
                if last:
                    next_norm.xn_of(nc, dve, xres, 0)
                if not first:
                    x_of(u - 1)
                if not last:
                    xnT_of(u + 1)
                q_feat_of(u, 2)
                q_feat_of(u, 3)
                if last:
                    next_tokens.lo_of(nc, dve, 0, 0, token_banks)
                else:
                    qk_of(u + 1, 0)
                divide(UT * u, 0)
                if not last:
                    qk_of(u + 1, 1)
                oT_of(UT * u, 0)
                divide(UT * u + 1, 1)

            unit(0, True, False)
            nc.vector.memset(next_weights["b_out_raw"][:, :], 0.0).then_inc(next_weights["zeroed"], 1)
            with dve.Fori(1, E + 1) as u:
                unit(u, False, False)
            with dve.Fori(E + 1, NU - 1) as u:
                unit(u, False, False)
            split_small_lo(nc, dve, next_weights)
            unit(NU - 1, False, True)
            oT_of(UT * NU - 1, 1)
            x_of(NU - 1)

        @block.tensor
        def _(pe):
            def products(out, pairs):
                for n, (w, m) in enumerate(pairs):
                    ins = nc.tensor.matmul(out, w, m, start=n == 0, stop=n == len(pairs) - 1)
                return ins

            def three(w_hi, w_lo, m_hi, m_lo):
                return [(w_hi, m_hi), (w_lo, m_hi), (w_hi, m_lo)]

            def turn_xn(u):
                after(pe, oT_done, UT * (u - 1))
                tokens.turn(nc, pe, norm, ident, u, turn_ps[:, :])

            def project_qk(u, i):
                if i == 0:
                    after(pe, oT_done, UT * (u - 1))
                    return tokens.queries(nc, pe, weights, u, q_ps[:, :])
                pe.wait_ge(tokens.done, u + 1)
                w_hi, w_lo = split["wk"]
                for m in range(KD):
                    cols = slice(m * P, (m + 1) * P)
                    ins = products(k_ps[:, m * UTOK:(m + 1) * UTOK],
                                   [pair for k in range(KD) for pair in
                                    three(w_hi[:, k, cols], w_lo[:, k, cols], tokens.hi[:, k, :], tokens.lo[:, k, :])])
                ins.then_inc(k_full, 1)

            def project_v(u, a):
                if a == 0:
                    after(pe, x_done, u - 1)
                w_hi, w_lo = split["wv"]
                tok = slice(a * P, (a + 1) * P)
                ins = products(ends_ps[:, a * D:(a + 1) * D],
                               [(ones_rows[:, :], bias_rows[:, :])] +
                               [pair for k in range(KD) for pair in
                                three(tokens.hi[:, k, tok], tokens.lo[:, k, tok], w_hi[:, k, :], w_lo[:, k, :])])
                if a == UT - 1:
                    ins.then_inc(v_full, 1)

            def k_features(u, a):
                pe.wait_ge(k_done, KD * u + KD)
                tok = slice(a * P, (a + 1) * P)
                for k in range(KD):
                    n = KD * a + k
                    after(pe, feat_done, FEATS * u + max(n - 1, 0))
                    products(feat_ps[:, n % 2, :], three(qk_hi[1][:, k, tok], qk_lo[1][:, k, tok],
                                                         rw_hi[:, k, :], rw_lo[:, k, :])).then_inc(feat_full, 1)

            def q_features(u, c):
                if c == 0:
                    pe.wait_ge(tokens.q_done, KD * u + KD)
                n = UT * KD + c
                pe.wait_ge(feat_done, FEATS * u + n - 1)
                for i in range(2):
                    k, pair = (2 * c + i) // GP, (2 * c + i) % GP
                    cols = slice(pair * P, (pair + 1) * P)
                    ins = products(feat_ps[:, n % 2, i * UTOK:(i + 1) * UTOK],
                                   three(rw_hi[:, k, cols], rw_lo[:, k, cols], qk_hi[0][:, k, :], qk_lo[0][:, k, :]))
                ins.then_inc(feat_full, 1)

            def sum_kv(u, a):
                t = UT * u + a
                if a == 0:
                    pe.wait_ge(v_done, UT * TB * u + UT * TB)
                    after(pe, o_done, 2 * TB * t)
                else:
                    pe.wait_ge(kv_done, 2 * t)
                pe.wait_ge(feat_done, FEATS * u + KD * (a + 1))
                for c in range(HP):
                    out = sum_ps[:, c // GP, (c % GP) * PAIR:(c % GP + 1) * PAIR]
                    ins = nc.tensor.matmul(out, k_feat[:, a, c // GP, (c % GP) * P:(c % GP + 1) * P],
                                           v_ones[:, a, c, :, :, :].rearrange("p b h d -> p (b h d)"), start=True, stop=True)
                ins.then_inc(kv_full, 1)

            def numerators(u, a):
                t = UT * u + a
                if a == 0:
                    pe.wait_ge(feat_done, FEATS * u + FEATS)
                    pe.wait_ge(kv_done, 2 * t + 4)
                else:
                    pe.wait_ge(o_done, 2 * TB * t)
                tok = slice(a * P, (a + 1) * P)
                for c in range(HP):
                    out = sum_ps[:, c // GP, (c % GP) * PAIR:(c % GP + 1) * PAIR]
                    ins = nc.tensor.matmul(out, q_feat[:, c, tok],
                                           kv[:, a, c, :, :, :].rearrange("p b h d -> p (b h d)"), start=True, stop=True)
                ins.then_inc(num_full, 1)

            def turn_o(u, a, q_done_next=None):
                t = UT * u + a
                pe.wait_ge(o_done, 2 * TB * t + 2 * TB)
                if a == 1:
                    pe.wait_ge(tokens.q_done, q_done_next)
                for k in range(KD):
                    ins = nc.tensor.transpose((turn_ps, q_ps)[a][:, k * P:(k + 1) * P], o_nat[:, a, k * P:(k + 1) * P], ident[:, :])
                ins.then_inc(o_turned, 1)

            def project_out(u, a, last_v):
                t = UT * u + a
                pe.wait_ge(oT_done, t + 1)
                if a == 0:
                    pe.wait_ge(v_done, last_v)
                w_hi, w_lo = split["wo"]
                ins = products(ends_ps[:, a * D:(a + 1) * D],
                         [pair for k in range(KD) for pair in
                          three(oT_hi[:, a, k, :], oT_lo[:, a, k, :], w_hi[:, k, :], w_lo[:, k, :])])
                if a == UT - 1:
                    ins.then_inc(out_full, 1)

            pe.wait_ge(weights["lo_done"], len(LA_PIECES) + 1)
            project_qk(0, 1)
            pe.wait_ge(consts_done, 3)
            project_v(0, 0)
            project_v(0, 1)

            def unit(u, first, last):
                V_DONE = UT * TB * (u + 1)
                k_features(u, 0)
                if not first:
                    turn_o(u - 1, 1, KD * u + KD)
                    project_out(u - 1, 0, V_DONE)
                k_features(u, 1)
                sum_kv(u, 0)
                if not first:
                    project_out(u - 1, 1, V_DONE)
                q_features(u, 0)
                q_features(u, 1)
                if not last:
                    turn_xn(u + 1)
                sum_kv(u, 1)
                q_features(u, 2)
                q_features(u, 3)
                if last:
                    pe.wait_ge(oT_done, UT * u)
                    for k in range(KD):
                        next_tokens.turn(nc, pe, next_norm, ident, 0, k, token_banks[k])
                else:
                    project_qk(u + 1, 0)
                numerators(u, 0)
                if last:
                    pe.wait_ge(next_weights["small_lo_done"], 2)
                    next_tokens.logits(nc, pe, next_weights["router"], 0, 0, token_banks[1])
                if not last:
                    project_qk(u + 1, 1)
                    project_v(u + 1, 0)
                turn_o(u, 0)
                numerators(u, 1)
                if not last:
                    project_v(u + 1, 1)

            unit(0, True, False)
            with pe.Fori(1, NU - 1) as u:
                unit(u, False, False)
            unit(NU - 1, False, True)
            project_out(NU - 1, 0, UT * TB * NU)
            turn_o(NU - 1, 1, KD * NU)
            project_out(NU - 1, 1, UT * TB * NU)


def mixture(nc, weights, xres, ident, norm, tokens, out):
    _, E, KD, H = weights["win_hi"].shape
    D = KD * P
    TOP = 2
    NT = xres.shape[1]
    UT = norm.UT
    NU = NT // UT
    UTOK = UT * P
    KH = H // P
    LANE = MOE_LANE
    assert UTOK == BANK and 2 * D == BANK and TOP == 2

    out_tiles = out.rearrange("(t b) q d -> (b q) t d", b=P // out.shape[1])

    with ExitStack() as stack:
        def sb(name, shape, dt=F32):
            return stack.enter_context(nc.sbuf_tensor("moe_" + name, shape, dt))

        def sem(name):
            return stack.enter_context(nc.semaphore("moe_" + name))

        win_hi, win_lo, wout_hi, wout_lo = (weights[n] for n in ("win_hi", "win_lo", "wout_hi", "wout_lo"))
        router = weights["router"]
        b_in_cols, b_out_rows = weights["b_in_cols"], weights["b_out_rows"]
        expert_ids = sb("expert_ids", [P, UT, E])

        part_sums = sb("part_sums", [P, UT, 2 * E])
        logit_sums = sb("logit_sums", [P, UT, E])
        neg_max = sb("neg_max", [P, UT, 1])
        shifted = sb("shifted", [P, UT, E])
        exps = sb("exps", [P, UT, E])
        exp_sum = sb("exp_sum", [P, UT, 1])
        inv_sum = sb("inv_sum", [P, UT, 1])
        probs = sb("probs", [P, UT, E])
        top_p = sb("top_p", [P, UT, 8])
        top_id = sb("top_id", [P, UT, 8], U32)
        top_idf = sb("top_idf", [P, UT, 8])
        is_first = sb("is_first", [P, UT, E])
        is_second = sb("is_second", [P, UT, E])
        chosen = sb("chosen", [P, UT, E])
        gates = [sb(f"gates{i}", [P, UT, E]) for i in range(2)]
        gate_parts = sb("gate_parts", [P, UT, P])
        gatesT = [sb(f"gatesT{i}", [P, UTOK], F32R) for i in range(2)]
        h = [sb(f"h{i}", [P, KH, UTOK]) for i in range(2)]
        h_hi = [sb(f"h_hi{i}", [P, KH, UTOK], F32R) for i in range(2)]
        h_lo = [sb(f"h_lo{i}", [P, KH, UTOK], F32R) for i in range(2)]

        h_ps = stack.enter_context(nc.psum_tensor("moe_h_ps", [P, 4, BANK], F32))
        y_ps = stack.enter_context(nc.psum_tensor("moe_y_ps", [P, 2, BANK], F32))
        aux_ps = stack.enter_context(nc.psum_tensor("moe_aux_ps", [P, 2, BANK], F32))
        aux = [aux_ps[:, k, :] for k in range(2)]

        zeroed = sem("zeroed")
        ids_done = sem("ids_done")
        logits_turned = sem("logits_turned")
        shifted_done = sem("shifted_done")
        exps_done = sem("exps_done")
        route = sem("route")
        gates_turned = sem("gates_turned")
        gatesT_done = sem("gatesT_done")
        h_full = sem("h_full")
        gelu_done = sem("gelu_done")
        h_hi_done = sem("h_hi_done")
        h_done = sem("h_done")
        y_full = sem("y_full")
        y_done = sem("y_done")
        biases_full = sem("biases_full")
        biases_done = sem("biases_done")
        stored = sem("stored")

        ROUTE = 7 + 2 * UT + 7
        block = stack.enter_context(nc.Block())

        @block.sync
        def _(sp):
            with sp.Fori(0, NU - 1) as u:
                sp.wait_ge(y_done, 2 * E * u + 2 * E)
                sp.dma_start(out_tiles[:, bass.ds(UT * u, UT), :], xres[:, bass.ds(UT * u, UT), :]).then_inc(stored, 16)
            for j in range(2):
                t = UT * (NU - 1) + j * UT // 2
                sp.wait_ge(y_done, 2 * E * NU - 1 + j)
                sp.dma_start(out_tiles[:, t:t + UT // 2, :], xres[:, t:t + UT // 2, :]).then_inc(stored, 16)
            sp.wait_ge(stored, 16 * (NU + 1))

        @block.gpsimd
        def _(pool):
            nc.gpsimd.iota(expert_ids[:, :, :], pattern=[[0, UT], [1, E]], base=0, channel_multiplier=0,
                           allow_small_or_imprecise_dtypes=True).then_inc(ids_done, 1)
            pool.wait_ge(ids_done, 1)
            with pool.Fori(1, NU) as u:
                norm.rstd_of(nc, pool, u)

        @block.scalar
        def _(act):
            def xnT_of(u, u_parity):
                tokens.hi_of(nc, act, u, u_parity, aux)

            def exps_of(u):
                act.wait_ge(shifted_done, u + 1)
                nc.scalar.activation(exps[:, :, :], shifted[:, :, :], ACT.Exp).then_inc(exps_done, 1)

            def logitsT_of(u):
                tokens.logitsT_of(nc, act, u, aux[0])

            def gatesT_of(u, u_parity):
                act.wait_ge(gates_turned, u + 1)
                nc.scalar.activation(gatesT[u_parity][:, :], aux_ps[:, 0, :], ACT.Copy).then_inc(gatesT_done, 1)

            def hidden_of(u, e):
                i = e % 2
                for m in range(KH):
                    act.wait_ge(h_full, KH * (E * u + e) + m + 1)
                    nc.scalar.activation(h[i][:, m, :], h_ps[:, 2 * i + m, :], ACT.Gelu_apprx_tanh,
                                         bias=b_in_cols[:, e, m:m + 1]).then_inc(gelu_done, 1)
                    act.wait_ge(gelu_done, KH * (E * u + e) + m + 1)
                    nc.scalar.activation(h_hi[i][:, m, :], h[i][:, m, :], ACT.Copy).then_inc(h_hi_done, 1)

            exps_of(0)
            hidden_of(0, 0)
            gatesT_of(0, 0)

            def unit(u, i, last):
                for e in range(1, E):
                    hidden_of(u, e)
                    if not last:
                        if e == 4:
                            xnT_of(u + 1, 1 - i)
                        if e == 5:
                            logitsT_of(u + 1)
                        if e == 6:
                            exps_of(u + 1)
                if not last:
                    hidden_of(u + 1, 0)
                    gatesT_of(u + 1, 1 - i)

            unit(0, 0, False)
            unit(1, 1, False)
            with act.Fori(1, NU // 2 - 1) as v:
                unit(2 * v, 0, False)
                unit(2 * v + 1, 1, False)
            unit(NU - 2, 0, False)
            unit(NU - 1, 1, True)

        @block.vector
        def _(dve):
            def moments_of(u):
                norm.moments_of(nc, dve, xres, u)

            def xn_of(u):
                norm.xn_of(nc, dve, xres, u)

            def xnT_of(u, u_parity):
                tokens.lo_of(nc, dve, u, u_parity, aux)

            def shift_of(u):
                dve.wait_ge(logits_turned, u + 1)
                nc.vector.tensor_copy(part_sums[:, :, :], aux_ps[:, 1, :].rearrange("p (a n) -> p a n", a=UT)[:, :, 0:2 * E]
                                      ).then_inc(route, 1)
                dve.wait_ge(route, ROUTE * u + 1)
                lg = logit_sums[:, :, :]
                nc.vector.tensor_tensor(lg, part_sums[:, :, 0:E], part_sums[:, :, E:2 * E], ALU.add).then_inc(route, 1)
                dve.wait_ge(route, ROUTE * u + 2)
                nc.vector.tensor_reduce(neg_max[:, :, :].rearrange("p a o -> p (a o)"), lg, AX.X, ALU.max, negate=True
                                        ).then_inc(route, 1)
                dve.wait_ge(route, ROUTE * u + 3)
                nc.vector.tensor_tensor(shifted[:, :, :], lg, neg_max[:, :, :].to_broadcast([P, UT, E]), ALU.add
                                        ).then_inc(shifted_done, 1)

            def gates_of(u, u_parity):
                step = ROUTE * u + 3
                dve.wait_ge(exps_done, u + 1)
                nc.vector.tensor_reduce(exp_sum[:, :, :].rearrange("p a o -> p (a o)"), exps[:, :, :], AX.X, ALU.add
                                        ).then_inc(route, 1)
                dve.wait_ge(route, step + 1)
                nc.vector.reciprocal(inv_sum[:, :, :], exp_sum[:, :, :]).then_inc(route, 1)
                dve.wait_ge(route, step + 2)
                nc.vector.tensor_tensor(probs[:, :, :], exps[:, :, :], inv_sum[:, :, :].to_broadcast([P, UT, E]), ALU.mult
                                        ).then_inc(route, 1)
                settle(nc, route, step + 3, norm.scratch[:, :])
                for a in range(UT):
                    nc.vector.max(top_p[:, a, :], probs[:, a, :]).then_inc(route, 1)
                settle(nc, route, step + 3 + UT, norm.scratch[:, :])
                for a in range(UT):
                    nc.vector.max_index(top_id[:, a, :], top_p[:, a, :], probs[:, a, :]).then_inc(route, 1)
                dve.wait_ge(route, step + 3 + 2 * UT)
                nc.vector.tensor_copy(top_idf[:, :, :], top_id[:, :, :]).then_inc(route, 1)
                dve.wait_ge(route, step + 4 + 2 * UT)
                for n, same in enumerate((is_first, is_second)):
                    nc.vector.tensor_tensor(same[:, :, :], expert_ids[:, :, :],
                                            top_idf[:, :, n:n + 1].to_broadcast([P, UT, E]), ALU.is_equal).then_inc(route, 1)
                dve.wait_ge(route, step + 6 + 2 * UT)
                nc.vector.tensor_tensor(chosen[:, :, :], is_first[:, :, :], is_second[:, :, :], ALU.add).then_inc(route, 1)
                dve.wait_ge(route, step + 7 + 2 * UT)
                nc.vector.tensor_tensor(gates[u_parity][:, :, :], probs[:, :, :], chosen[:, :, :], ALU.mult).then_inc(route, 1)
                dve.wait_ge(route, step + 8 + 2 * UT)
                for lane in (0, 2):
                    nc.vector.tensor_copy(gate_parts[:, :, lane * LANE:lane * LANE + E].bitcast(F32R), gates[u_parity][:, :, :]
                                          ).then_inc(route, 1)
                dve.wait_ge(route, step + 10 + 2 * UT)
                nc.vector.tensor_tensor(gate_parts[:, :, LANE:LANE + E], gates[u_parity][:, :, :], gate_parts[:, :, 0:E], ALU.subtract
                                        ).then_inc(route, 1)

            def hidden_of(u, e):
                i = e % 2
                for m in range(KH):
                    dve.wait_ge(h_hi_done, KH * (E * u + e) + m + 1)
                    nc.vector.tensor_tensor(h_lo[i][:, m, :], h[i][:, m, :], h_hi[i][:, m, :].bitcast(F32), ALU.subtract
                                            ).then_inc(h_done, 1)

            def add_expert(u, u_parity, e):
                if e == 2:
                    dve.wait_ge(biases_done, u + 1)
                for j in range(2):
                    dve.wait_ge(y_full, 2 * (E * u + e) + j + 1)
                    after(dve, y_done, 2 * E * u + 2 * e + j - 1)
                    for i in range(2):
                        a = 2 * j + i
                        dst = slot(xres, UT * u + a)
                        ins = nc.vector.scalar_tensor_tensor(out=dst, in0=y_ps[:, j, i * D:(i + 1) * D].unsqueeze(1),
                                                             scalar=gates[u_parity][:, a, e:e + 1], in1=dst,
                                                             op0=ALU.mult, op1=ALU.add)
                    ins.then_inc(y_done, 1)

            def add_biases(u):
                dve.wait_ge(biases_full, u + 1)
                dve.wait_ge(y_done, 2 * E * u + 4)
                dst = xres[:, bass.ds(UT * u, UT), :]
                nc.vector.tensor_tensor(dst, aux_ps[:, :, :].rearrange("p j (i n) -> p (j i) n", i=2), dst, ALU.add
                                        ).then_inc(biases_done, 1)

            nc.vector.memset(gate_parts[:, :, :], 0.0).then_inc(zeroed, 1)
            shift_of(0)
            dve.wait_ge(ids_done, 1)
            dve.wait_ge(zeroed, 1)
            gates_of(0, 0)

            def unit(u, i, last):
                hidden_of(u, 0)
                hidden_of(u, 1)
                add_expert(u, i, 0)
                hidden_of(u, 2)
                add_expert(u, i, 1)
                add_biases(u)
                for e in range(3, E):
                    hidden_of(u, e)
                    add_expert(u, i, e - 1)
                    if not last:
                        if e == 3:
                            moments_of(u + 1)
                            xn_of(u + 1)
                        if e == 4:
                            xnT_of(u + 1, 1 - i)
                        if e == 5:
                            shift_of(u + 1)
                        if e == 6:
                            gates_of(u + 1, 1 - i)
                add_expert(u, i, E - 1)

            unit(0, 0, False)
            unit(1, 1, False)
            with dve.Fori(1, NU // 2 - 1) as v:
                unit(2 * v, 0, False)
                unit(2 * v + 1, 1, False)
            unit(NU - 2, 0, False)
            unit(NU - 1, 1, True)

        @block.tensor
        def _(pe):
            def products(out, pairs):
                for n, (w, m) in enumerate(pairs):
                    ins = nc.tensor.matmul(out, w, m, start=n == 0, stop=n == len(pairs) - 1)
                return ins

            def three(w_hi, w_lo, m_hi, m_lo):
                return [(w_hi, m_hi), (w_lo, m_hi), (w_hi, m_lo)]

            def turn_xn(u, k):
                if k == 0:
                    after(pe, biases_done, u)
                tokens.turn(nc, pe, norm, ident, u, k, aux[k])

            def logits(u, i):
                tokens.logits(nc, pe, router, u, i, aux[0])

            def turn_logits(u):
                pe.wait_ge(tokens.logitsT_done, u + 1)
                for a in range(UT):
                    ins = nc.tensor.transpose(aux_ps[:, 1, a * P:(a + 1) * P], tokens.logitsT[:, a * P:(a + 1) * P], ident[:, :])
                ins.then_inc(logits_turned, 1)

            def turn_gates(u):
                pe.wait_ge(route, ROUTE * u + ROUTE)
                for a in range(UT):
                    ins = nc.tensor.transpose(aux_ps[:, 0, a * P:(a + 1) * P], gate_parts[:, a, :], ident[:, :])
                ins.then_inc(gates_turned, 1)

            def hidden(u, u_parity, e):
                i = e % 2
                if e == 0:
                    pe.wait_ge(tokens.done, KD * u + KD)
                for m in range(KH):
                    after(pe, gelu_done, KH * E * u + max(KH * (e - 2) + m + 1, 0))
                    cols = slice(m * P, (m + 1) * P)
                    products(h_ps[:, 2 * i + m, :],
                             [pair for k in range(KD) for pair in
                              three(win_hi[:, e, k, cols], win_lo[:, e, k, cols], tokens.hi[u_parity][:, k, :],
                                    tokens.lo[u_parity][:, k, :])]
                             ).then_inc(h_full, 1)

            def outputs(u, e):
                i = e % 2
                pe.wait_ge(h_done, KH * (E * u + e) + KH)
                for j in range(2):
                    after(pe, y_done, 2 * E * u + 2 * e + j - 1)
                    for n in range(2):
                        tok = slice((2 * j + n) * P, (2 * j + n + 1) * P)
                        ins = products(y_ps[:, j, n * D:(n + 1) * D],
                                       [pair for k in range(KH) for pair in
                                        three(h_hi[i][:, k, tok], h_lo[i][:, k, tok], wout_hi[:, e, k, :], wout_lo[:, e, k, :])])
                    ins.then_inc(y_full, 1)

            def biases(u, u_parity):
                pe.wait_ge(gatesT_done, u + 1)
                for a in range(UT):
                    ins = nc.tensor.matmul(aux_ps[:, a // 2, (a % 2) * D:(a % 2 + 1) * D],
                                           gatesT[u_parity][:, a * P:(a + 1) * P], b_out_rows[:, :], start=True, stop=True)
                ins.then_inc(biases_full, 1)

            turn_logits(0)
            pe.wait_ge(weights["lo_done"], 2 * E)
            hidden(0, 0, 0)
            hidden(0, 0, 1)
            turn_gates(0)

            def unit(u, i, last):
                outputs(u, 0)
                hidden(u, i, 2)
                biases(u, i)
                outputs(u, 1)
                for e in range(3, E):
                    hidden(u, i, e)
                    if e == 5 and not last:
                        turn_xn(u + 1, 0)
                        turn_xn(u + 1, 1)
                    if e == 6 and not last:
                        turn_logits(u + 1)
                    outputs(u, e - 1)
                    if e == 5 and not last:
                        logits(u + 1, 1 - i)
                if not last:
                    hidden(u + 1, 1 - i, 0)
                    turn_gates(u + 1)
                outputs(u, E - 1)
                if not last:
                    hidden(u + 1, 1 - i, 1)

            unit(0, 0, False)
            unit(1, 1, False)
            with pe.Fori(1, NU // 2 - 1) as v:
                unit(2 * v, 0, False)
                unit(2 * v + 1, 1, False)
            unit(NU - 2, 0, False)
            unit(NU - 1, 1, True)


def perceiver_block(nc, x, ctx, xattn, attn, ffn, out):
    NT = x.shape[0] * x.shape[1] // P
    with ExitStack() as stack:
        xres = stack.enter_context(nc.sbuf_tensor("xres", [P, NT, x.shape[2]], F32))
        ident = stack.enter_context(nc.sbuf_tensor("ident", [P, P], F32))
        H, DK, F = attn[-1].shape
        D = x.shape[2]
        weights = linear_attention_weights(nc, stack, D, H, F)
        la_norm = Norm(nc, stack, "la_norm", 2, D)
        queries = QueryTokens(nc, stack, D // P, 2 * P)
        with ExitStack() as norm_stack:
            norm = Norm(nc, norm_stack, "xa_norm", 2, D)
            cross_attention(nc, x, ctx, *xattn, xres, ident, norm, la_norm, queries, weights, attn)
        moe_norm = Norm(nc, stack, "moe_norm", 4, D)
        tokens = TurnedTokens(nc, stack, D // P, BANK, ffn[1].shape[0])
        with ExitStack() as raw_stack:
            expert_weights = mixture_weights(nc, stack, raw_stack, *ffn[1].shape)
            linear_attention(nc, weights, D, H, DK, F, xres, ident, la_norm, queries, moe_norm, expert_weights, ffn, tokens)
        mixture(nc, expert_weights, xres, ident, moe_norm, tokens, out)


_XATTN = ["L0_xattn_Wq", "L0_xattn_Wk", "L0_xattn_Wv", "L0_xattn_Wo", "L0_xattn_bo"]
_ATTN = ["L0_attn_Wq", "L0_attn_bq", "L0_attn_Wk", "L0_attn_bk", "L0_attn_Wv", "L0_attn_bv", "L0_attn_Wo", "L0_attn_bo",
         "L0_attn_rw"]
_FFN = ["L0_ffn_router_w", "L0_ffn_w_in", "L0_ffn_b_in", "L0_ffn_w_out", "L0_ffn_b_out"]


def kernel(**inputs):
    import numpy as _np
    import concourse.bacc as _bacc
    from concourse.bass_utils import run_bass_kernel_spmd as _run

    nc = _bacc.Bacc("TRN2", target_bir_lowering=False, num_devices=1)
    arrays, aps = {}, {}
    for name in ["x", "ctx_768"] + _XATTN + _ATTN + _FFN:
        a = _np.ascontiguousarray(inputs[name])
        arrays[f"in_{name}"] = a
        aps[name] = nc.dram_tensor(f"in_{name}", a.shape, mybir.dt.from_np(a.dtype), kind="ExternalInput").ap()
    out = nc.dram_tensor("out", inputs["x"].shape, F32, kind="ExternalOutput").ap()
    perceiver_block(nc, aps["x"], aps["ctx_768"], [aps[n] for n in _XATTN], [aps[n] for n in _ATTN],
                    [aps[n] for n in _FFN], out)
    return _run(nc, [arrays], core_ids=[0]).results[0]["out"]
```
